# Optimizing a Trainium2 kernel written in Bass

```python
import numpy as np
import jax
import jax.numpy as jnp

def _softmax(x, axis=-1):
    return jax.nn.softmax(x, axis=axis)

def _gelu(x):
    return jax.nn.gelu(x, approximate=True)

def _silu(x):
    return jax.nn.silu(x)

def _sigmoid(x):
    return jax.nn.sigmoid(x)

def _layernorm(x, axis=-1, eps=1e-05):
    m = jnp.mean(x, axis=axis, keepdims=True)
    v = jnp.var(x, axis=axis, keepdims=True)
    return (x - m) / jnp.sqrt(v + eps)

def _scatter_add(tgt, idx, src, axis=0):
    return tgt.at[idx].add(src)

def _segment_sum(src, seg, n):
    return jax.ops.segment_sum(src, seg, n)
kernel_name = 'mk_xattn_ffn_d4_seqx_r8_503d05'

def setup_inputs(seed: int=0):
    np.random.seed(seed)
    _w = jnp.asarray

    def _rec_inputs():
        import jax
        import jax.numpy as jnp
        _rk = jax.random.key(seed)
        x = 0.0003765 + 1 * jax.random.normal(jax.random.fold_in(_rk, 1), (8, 128, 128), jnp.float32)
        _lenS = 128 - jax.random.randint(jax.random.fold_in(_rk, 7), (8,), 0, max(1, 128 // 4) + 1, jnp.int32)
        _lenS2 = 128 - jax.random.randint(jax.random.fold_in(_rk, 8), (8,), 0, max(1, 128 // 4) + 1, jnp.int32)
        _ctx_1024P = jax.random.normal(jax.random.fold_in(_rk, 11), (8, 16, 128), jnp.float32)
        _ctx_1024c = jax.random.dirichlet(jax.random.fold_in(_rk, 511), 0.3 * jnp.ones((16,), jnp.float32), (8, 128))
        _ctx_1024t = jnp.einsum('bsk,bkd->bsd', _ctx_1024c, _ctx_1024P)
        _ctx_1024t = _ctx_1024t * jax.lax.rsqrt(jnp.mean(jnp.square(_ctx_1024t)) + 1e-12) * 0.953939
        ctx_1024 = -0.000292821 + 1.00034 * (_ctx_1024t + 0.3 * jax.random.normal(jax.random.fold_in(_rk, 611), (8, 128, 128), jnp.float32))
        _validS = jnp.arange(128)[None, :] < _lenS[:, None]
        _validS2 = jnp.arange(128)[None, :] < _lenS2[:, None]
        _causal = jnp.tril(jnp.ones((128, 128), dtype=bool))
        mask_Bx1x1xS2_if1 = jnp.where(jnp.ones((8, 1, 1, 128), dtype=bool), 1, 0).astype(jnp.int32)
        mask_1x1xSxS2_if1 = jnp.where(jnp.ones((1, 1, 128, 128), dtype=bool), 1, 0).astype(jnp.int32)
        mask_1x1xSxS2_fk0 = jnp.where(jnp.broadcast_to(_validS2[0:1, None, None, :], (1, 1, 128, 128)), 0.0, 1.0).astype(jnp.float32)
        return (x, ctx_1024, mask_Bx1x1xS2_if1, mask_1x1xSxS2_if1, mask_1x1xSxS2_fk0)
    x, ctx_1024, mask_Bx1x1xS2_if1, mask_1x1xSxS2_if1, mask_1x1xSxS2_fk0 = _rec_inputs()

    def _L0_xattn_setup():
        import jax, jax.numpy as jnp
        import numpy as np
        EMBED = 128
        HEADS = 16
        HEAD_DIM = EMBED // HEADS
        NEG = -1e+20
        key = jax.random.key(seed)
        ks = jax.random.split(key, 8)
        N, S = (2, 256)
        values = jax.random.normal(ks[0], (N, S, EMBED), dtype=jnp.float32)
        keys = jax.random.normal(ks[1], (N, S, EMBED), dtype=jnp.float32)
        queries = jax.random.normal(ks[2], (N, S, EMBED), dtype=jnp.float32)
        mask = jnp.ones((N, 1, 1, S), dtype=jnp.int32)
        s = 1.0 / np.sqrt(HEAD_DIM)
        Wv = jax.random.normal(ks[3], (HEAD_DIM, HEAD_DIM), dtype=jnp.float32) * s
        Wk = jax.random.normal(ks[4], (HEAD_DIM, HEAD_DIM), dtype=jnp.float32) * s
        Wq = jax.random.normal(ks[5], (HEAD_DIM, HEAD_DIM), dtype=jnp.float32) * s
        Wo = jax.random.normal(ks[6], (EMBED, EMBED), dtype=jnp.float32) * (1.0 / np.sqrt(EMBED))
        bo = jnp.zeros((EMBED,), dtype=jnp.float32)
        return {'values': values, 'keys': keys, 'queries': queries, 'mask': mask, 'Wv': Wv, 'Wk': Wk, 'Wq': Wq, 'Wo': Wo, 'bo': bo}
    _L0_xattn_all = _L0_xattn_setup()
    _L0_xattn_in = {k: v for k, v in _L0_xattn_all.items() if k in ('Wv', 'Wk', 'Wq', 'Wo', 'bo')}
    del _L0_xattn_all

    def _L0_ffn_setup():
        import jax, jax.numpy as jnp
        import numpy as np
        DIM = 128
        DEPTH = 2
        HEADS = 8
        DIM_HEAD = 64
        WINDOW = 64
        INNER = HEADS * DIM_HEAD
        HID = int(DIM * 4 * 2 / 3)
        B, N = (2, 1024)
        QK_SCALE = 8.0

        def shift_token(t):
            t1, t2 = jnp.split(t, 2, axis=-1)
            t2 = jnp.pad(t2, ((0, 0), (1, 0), (0, 0)))[:, :-1]
            return jnp.concatenate([t1, t2], axis=-1)

        def l2norm(t):
            return t / jnp.clip(jnp.linalg.norm(t, axis=-1, keepdims=True), 1e-12)

        def rotate_half(x):
            x1, x2 = jnp.split(x, 2, axis=-1)
            return jnp.concatenate([-x2, x1], axis=-1)

        def rotary_xpos(q, k):
            n = q.shape[-2]
            half_idx = jnp.arange(0, DIM_HEAD, 2, dtype=jnp.float32)
            inv_freq = 1.0 / 10000.0 ** (half_idx / DIM_HEAD)
            t = jnp.arange(n, dtype=jnp.float32)
            freqs = t[:, None] * inv_freq[None, :]
            freqs = jnp.concatenate([freqs, freqs], axis=-1)
            base = (half_idx + 0.4 * DIM_HEAD) / (1.4 * DIM_HEAD)
            power = (t - n // 2) / float(WINDOW // 2)
            scale = base[None, :] ** power[:, None]
            scale = jnp.concatenate([scale, scale], axis=-1)
            cos, sin = (jnp.cos(freqs), jnp.sin(freqs))
            q = q * cos * scale + rotate_half(q) * sin * scale
            k = k * cos / scale + rotate_half(k) * sin / scale
            return (q, k)

        def local_attention(q, k, v):
            b, h, n, d = q.shape
            w = n // WINDOW
            bq = q.reshape(b, h, w, WINDOW, d) * QK_SCALE
            bk = k.reshape(b, h, w, WINDOW, d)
            bv = v.reshape(b, h, w, WINDOW, d)

            def look_around(t):
                p = jnp.pad(t, ((0, 0), (0, 0), (1, 0), (0, 0), (0, 0)))
                return jnp.concatenate([p[:, :, :w], p[:, :, 1:]], axis=3)
            bk, bv = (look_around(bk), look_around(bv))
            bt = jnp.arange(n).reshape(w, WINDOW)
            btp = jnp.pad(bt, ((1, 0), (0, 0)), constant_values=-1)
            btk = jnp.concatenate([btp[:w], btp[1:]], axis=1)
            sim = jnp.einsum('bhwid,bhwjd->bhwij', bq, bk)
            i = bt[:, :, None]
            j = btk[:, None, :]
            mask = (i < j) | (i > j + WINDOW) | (j == -1)
            sim = jnp.where(mask, -jnp.finfo(sim.dtype).max, sim)
            attn = jax.nn.softmax(sim, axis=-1)
            out = jnp.einsum('bhwij,bhwjd->bhwid', attn, bv)
            return out.reshape(b, h, n, d)

        def _layer(x, wqkv, qs, ksc, wo, lg, lb, w1, b1, w2, b2):
            b, n, _ = x.shape
            h = shift_token(x)
            qkv = h @ wqkv
            q, k, v = jnp.split(qkv, 3, axis=-1)
            to_heads = lambda t: t.reshape(b, n, HEADS, DIM_HEAD).transpose(0, 2, 1, 3)
            q, k, v = (to_heads(q), to_heads(k), to_heads(v))
            q = l2norm(q) * qs
            k = l2norm(k) * ksc
            q, k = rotary_xpos(q, k)
            o = local_attention(q, k, v)
            o = o.transpose(0, 2, 1, 3).reshape(b, n, INNER)
            x = x + o @ wo
            h = shift_token(x)
            mu = h.mean(-1, keepdims=True)
            var = h.var(-1, keepdims=True)
            h = (h - mu) / jnp.sqrt(var + 1e-05) * lg + lb
            h = h @ w1 + b1
            a, g = jnp.split(h, 2, axis=-1)
            h = a * jax.nn.gelu(g, approximate=False)
            x = x + h @ w2 + b2
            return x
        key = jax.random.key(seed)
        ks = jax.random.split(key, 6)
        return {'x': jax.random.normal(ks[0], (B, N, DIM), jnp.float32), 'wqkv': jax.random.normal(ks[1], (DEPTH, DIM, 3 * INNER), jnp.float32) * 0.02, 'q_scale': jnp.ones((DEPTH, DIM_HEAD), jnp.float32), 'k_scale': jnp.ones((DEPTH, DIM_HEAD), jnp.float32), 'wo': jax.random.normal(ks[2], (DEPTH, INNER, DIM), jnp.float32) * 0.02, 'ln_g': jnp.ones((DEPTH, DIM), jnp.float32), 'ln_b': jnp.zeros((DEPTH, DIM), jnp.float32), 'w1': jax.random.normal(ks[3], (DEPTH, DIM, 2 * HID), jnp.float32) * 0.02, 'b1': jnp.zeros((DEPTH, 2 * HID), jnp.float32), 'w2': jax.random.normal(ks[4], (DEPTH, HID, DIM), jnp.float32) * 0.02, 'b2': jnp.zeros((DEPTH, DIM), jnp.float32)}
    _L0_ffn_all = _L0_ffn_setup()
    _L0_ffn_in = {k: v for k, v in _L0_ffn_all.items() if k in ('wqkv', 'q_scale', 'k_scale', 'wo', 'ln_g', 'ln_b', 'w1', 'b1', 'w2', 'b2')}
    del _L0_ffn_all

    def _L1_xattn_setup():
        import jax, jax.numpy as jnp
        import numpy as np
        D_MODEL = 128
        NUM_HEADS = 16
        D_K = D_MODEL // NUM_HEADS
        NEG = -1000000000.0

        def _split_heads(x):
            b, s, _ = x.shape
            return x.reshape(b, s, NUM_HEADS, D_K).transpose(0, 2, 1, 3)
        key = jax.random.key(seed)
        ks = jax.random.split(key, 12)
        B, S = (4, 256)
        s = 0.02
        return {'q': jax.random.normal(ks[0], (B, S, D_MODEL), jnp.float32), 'k': jax.random.normal(ks[1], (B, S, D_MODEL), jnp.float32), 'v': jax.random.normal(ks[2], (B, S, D_MODEL), jnp.float32), 'mask': jnp.ones((1, 1, S, S), jnp.int32), 'Wq': jax.random.normal(ks[3], (D_MODEL, D_MODEL), jnp.float32) * s, 'bq': jax.random.normal(ks[4], (D_MODEL,), jnp.float32) * s, 'Wk': jax.random.normal(ks[5], (D_MODEL, D_MODEL), jnp.float32) * s, 'bk': jax.random.normal(ks[6], (D_MODEL,), jnp.float32) * s, 'Wv': jax.random.normal(ks[7], (D_MODEL, D_MODEL), jnp.float32) * s, 'bv': jax.random.normal(ks[8], (D_MODEL,), jnp.float32) * s, 'Wo': jax.random.normal(ks[9], (D_MODEL, D_MODEL), jnp.float32) * s, 'bo': jax.random.normal(ks[10], (D_MODEL,), jnp.float32) * s}
    _L1_xattn_all = _L1_xattn_setup()
    _L1_xattn_in = {k: v for k, v in _L1_xattn_all.items() if k in ('Wq', 'bq', 'Wk', 'bk', 'Wv', 'bv', 'Wo', 'bo')}
    del _L1_xattn_all

    def _L1_ffn_setup():
        import jax, jax.numpy as jnp
        import numpy as np
        B, S, D, F, E = (1, 128, 128, 512, 8)
        EPS = 1e-05

        def _sublayer(xs, g, b, W1e, b1e, W2e, b2e):
            mu = jnp.mean(xs, axis=-1, keepdims=True)
            var = jnp.mean(jnp.square(xs - mu), axis=-1, keepdims=True)
            h = (xs - mu) * jax.lax.rsqrt(var + EPS) * g + b
            return xs + jax.nn.relu(h @ W1e.T + b1e) @ W2e.T + b2e
        key = jax.random.key(seed)
        ks = jax.random.split(key, 4)
        x = jax.random.normal(ks[0], (B, S, D), jnp.float32)
        centroids = jax.random.normal(ks[1], (E, D), jnp.float32) * 0.1
        gamma = jnp.ones((E, D), jnp.float32)
        beta = jnp.zeros((E, D), jnp.float32)
        W1 = jax.random.normal(ks[2], (E, F, D), jnp.float32) * 0.02
        b1 = jnp.zeros((E, F), jnp.float32)
        W2 = jax.random.normal(ks[3], (E, D, F), jnp.float32) * 0.02
        b2 = jnp.zeros((E, D), jnp.float32)
        return {'x': x, 'centroids': centroids, 'gamma': gamma, 'beta': beta, 'W1': W1, 'b1': b1, 'W2': W2, 'b2': b2}
    _L1_ffn_all = _L1_ffn_setup()
    _L1_ffn_in = {k: v for k, v in _L1_ffn_all.items() if k in ('centroids', 'gamma', 'beta', 'W1', 'b1', 'W2', 'b2')}
    del _L1_ffn_all

    def _L2_xattn_setup():
        import jax, jax.numpy as jnp
        import numpy as np
        D_MODEL = 128
        NHEAD = 16
        D_HEAD = D_MODEL // NHEAD
        key = jax.random.key(seed)
        ks = jax.random.split(key, 11)
        B, Nq, Nk = (2, 256, 256)
        s = 1.0 / np.sqrt(D_MODEL)
        inp = {'q': jax.random.normal(ks[0], (B, Nq, D_MODEL), jnp.float32), 'k': jax.random.normal(ks[1], (B, Nk, D_MODEL), jnp.float32), 'v': jax.random.normal(ks[2], (B, Nk, D_MODEL), jnp.float32), 'Wq': jax.random.normal(ks[3], (D_MODEL, D_MODEL), jnp.float32) * s, 'bq': jnp.zeros((D_MODEL,), jnp.float32), 'Wk': jax.random.normal(ks[4], (D_MODEL, D_MODEL), jnp.float32) * s, 'bk': jnp.zeros((D_MODEL,), jnp.float32), 'Wv': jax.random.normal(ks[5], (D_MODEL, D_MODEL), jnp.float32) * s, 'bv': jnp.zeros((D_MODEL,), jnp.float32), 'Wo': jax.random.normal(ks[6], (D_MODEL, D_MODEL), jnp.float32) * s, 'bo': jnp.zeros((D_MODEL,), jnp.float32)}
        return inp
    _L2_xattn_all = _L2_xattn_setup()
    _L2_xattn_in = {k: v for k, v in _L2_xattn_all.items() if k in ('Wq', 'bq', 'Wk', 'bk', 'Wv', 'bv', 'Wo', 'bo')}
    del _L2_xattn_all

    def _L2_ffn_setup():
        import math
        import jax, jax.numpy as jnp
        import numpy as np
        CAPACITY_FACTOR = 1.25
        key = jax.random.key(seed)
        ks = jax.random.split(key, 5)
        B, S, H, F, E = (4, 512, 128, 128, 32)
        scale_in = 1.0 / math.sqrt(H)
        scale_mid = 1.0 / math.sqrt(F)
        return {'x': jax.random.normal(ks[0], (B, S, H), dtype=jnp.float32), 'w_router': jax.random.normal(ks[1], (H, E), dtype=jnp.float32) * scale_in, 'w_gate': jax.random.normal(ks[2], (E, H, F), dtype=jnp.float32) * scale_in, 'w_up': jax.random.normal(ks[3], (E, H, F), dtype=jnp.float32) * scale_in, 'w_down': jax.random.normal(ks[4], (E, F, H), dtype=jnp.float32) * scale_mid}
    _L2_ffn_all = _L2_ffn_setup()
    _L2_ffn_in = {k: v for k, v in _L2_ffn_all.items() if k in ('w_router', 'w_gate', 'w_up', 'w_down')}
    del _L2_ffn_all

    def _L3_xattn_setup():
        import jax, jax.numpy as jnp
        import numpy as np
        HEAD = 16
        NEG_FILL = -1e+20
        key = jax.random.key(seed)
        ks = jax.random.split(key, 6)
        N, S, E = (4, 256, 128)
        D = E // HEAD
        value = jax.random.normal(ks[0], (N, S, E), dtype=jnp.float32)
        key_t = jax.random.normal(ks[1], (N, S, E), dtype=jnp.float32)
        query = jax.random.normal(ks[2], (N, S, E), dtype=jnp.float32)
        mask = jnp.tril(jnp.ones((S, S), dtype=jnp.float32))[None, None, :, :]
        sc = 1.0 / np.sqrt(D)
        Wq = jax.random.normal(ks[3], (D, D), dtype=jnp.float32) * sc
        Wk = jax.random.normal(ks[4], (D, D), dtype=jnp.float32) * sc
        Wv = jax.random.normal(ks[5], (D, D), dtype=jnp.float32) * sc
        return {'value': value, 'key': key_t, 'query': query, 'mask': mask, 'Wq': Wq, 'Wk': Wk, 'Wv': Wv}
    _L3_xattn_all = _L3_xattn_setup()
    _L3_xattn_in = {k: v for k, v in _L3_xattn_all.items() if k in ('Wq', 'Wk', 'Wv')}
    del _L3_xattn_all

    def _L3_ffn_setup():
        import jax, jax.numpy as jnp
        import numpy as np
        H = 128
        I = 64
        E = 8
        TOP_K = 2
        N_SHARED = 2
        SHARED_I = I * N_SHARED
        SCALE = 2.5
        NORM_TOPK = True
        B, S = (2, 128)

        def _swiglu(x, wg, wu, wd):
            g = x @ wg.T
            u = x @ wu.T
            return jax.nn.silu(g) * u @ wd.T
        key = jax.random.key(seed)
        ks = jax.random.split(key, 8)
        std = 0.02
        return {'hidden_states': jax.random.normal(ks[0], (B, S, H), jnp.float32), 'gate_weight': jax.random.normal(ks[1], (E, H), jnp.float32) * std, 'w_gate': jax.random.normal(ks[2], (E, I, H), jnp.float32) * std, 'w_up': jax.random.normal(ks[3], (E, I, H), jnp.float32) * std, 'w_down': jax.random.normal(ks[4], (E, H, I), jnp.float32) * std, 'ws_gate': jax.random.normal(ks[5], (SHARED_I, H), jnp.float32) * std, 'ws_up': jax.random.normal(ks[6], (SHARED_I, H), jnp.float32) * std, 'ws_down': jax.random.normal(ks[7], (H, SHARED_I), jnp.float32) * std}
    _L3_ffn_all = _L3_ffn_setup()
    _L3_ffn_in = {k: v for k, v in _L3_ffn_all.items() if k in ('gate_weight', 'w_gate', 'w_up', 'w_down', 'ws_gate', 'ws_up', 'ws_down')}
    del _L3_ffn_all
    return {'x': x, 'ctx_1024': ctx_1024, 'mask_Bx1x1xS2_if1': mask_Bx1x1xS2_if1, 'mask_1x1xSxS2_if1': mask_1x1xSxS2_if1, 'mask_1x1xSxS2_fk0': mask_1x1xSxS2_fk0, 'L0_xattn_Wv': _L0_xattn_in['Wv'], 'L0_xattn_Wk': _L0_xattn_in['Wk'], 'L0_xattn_Wq': _L0_xattn_in['Wq'], 'L0_xattn_Wo': _L0_xattn_in['Wo'], 'L0_xattn_bo': _L0_xattn_in['bo'], 'L0_ffn_wqkv': _L0_ffn_in['wqkv'], 'L0_ffn_q_scale': _L0_ffn_in['q_scale'], 'L0_ffn_k_scale': _L0_ffn_in['k_scale'], 'L0_ffn_wo': _L0_ffn_in['wo'], 'L0_ffn_ln_g': _L0_ffn_in['ln_g'], 'L0_ffn_ln_b': _L0_ffn_in['ln_b'], 'L0_ffn_w1': _L0_ffn_in['w1'], 'L0_ffn_b1': _L0_ffn_in['b1'], 'L0_ffn_w2': _L0_ffn_in['w2'], 'L0_ffn_b2': _L0_ffn_in['b2'], 'L1_xattn_Wq': _L1_xattn_in['Wq'], 'L1_xattn_bq': _L1_xattn_in['bq'], 'L1_xattn_Wk': _L1_xattn_in['Wk'], 'L1_xattn_bk': _L1_xattn_in['bk'], 'L1_xattn_Wv': _L1_xattn_in['Wv'], 'L1_xattn_bv': _L1_xattn_in['bv'], 'L1_xattn_Wo': _L1_xattn_in['Wo'], 'L1_xattn_bo': _L1_xattn_in['bo'], 'L1_ffn_centroids': _L1_ffn_in['centroids'], 'L1_ffn_gamma': _L1_ffn_in['gamma'], 'L1_ffn_beta': _L1_ffn_in['beta'], 'L1_ffn_W1': _L1_ffn_in['W1'], 'L1_ffn_b1': _L1_ffn_in['b1'], 'L1_ffn_W2': _L1_ffn_in['W2'], 'L1_ffn_b2': _L1_ffn_in['b2'], 'L2_xattn_Wq': _L2_xattn_in['Wq'], 'L2_xattn_bq': _L2_xattn_in['bq'], 'L2_xattn_Wk': _L2_xattn_in['Wk'], 'L2_xattn_bk': _L2_xattn_in['bk'], 'L2_xattn_Wv': _L2_xattn_in['Wv'], 'L2_xattn_bv': _L2_xattn_in['bv'], 'L2_xattn_Wo': _L2_xattn_in['Wo'], 'L2_xattn_bo': _L2_xattn_in['bo'], 'L2_ffn_w_router': _L2_ffn_in['w_router'], 'L2_ffn_w_gate': _L2_ffn_in['w_gate'], 'L2_ffn_w_up': _L2_ffn_in['w_up'], 'L2_ffn_w_down': _L2_ffn_in['w_down'], 'L3_xattn_Wq': _L3_xattn_in['Wq'], 'L3_xattn_Wk': _L3_xattn_in['Wk'], 'L3_xattn_Wv': _L3_xattn_in['Wv'], 'L3_ffn_gate_weight': _L3_ffn_in['gate_weight'], 'L3_ffn_w_gate': _L3_ffn_in['w_gate'], 'L3_ffn_w_up': _L3_ffn_in['w_up'], 'L3_ffn_w_down': _L3_ffn_in['w_down'], 'L3_ffn_ws_gate': _L3_ffn_in['ws_gate'], 'L3_ffn_ws_up': _L3_ffn_in['ws_up'], 'L3_ffn_ws_down': _L3_ffn_in['ws_down']}

def reference(x, ctx_1024, mask_Bx1x1xS2_if1, mask_1x1xSxS2_if1, mask_1x1xSxS2_fk0, L0_xattn_Wv, L0_xattn_Wk, L0_xattn_Wq, L0_xattn_Wo, L0_xattn_bo, L0_ffn_wqkv, L0_ffn_q_scale, L0_ffn_k_scale, L0_ffn_wo, L0_ffn_ln_g, L0_ffn_ln_b, L0_ffn_w1, L0_ffn_b1, L0_ffn_w2, L0_ffn_b2, L1_xattn_Wq, L1_xattn_bq, L1_xattn_Wk, L1_xattn_bk, L1_xattn_Wv, L1_xattn_bv, L1_xattn_Wo, L1_xattn_bo, L1_ffn_centroids, L1_ffn_gamma, L1_ffn_beta, L1_ffn_W1, L1_ffn_b1, L1_ffn_W2, L1_ffn_b2, L2_xattn_Wq, L2_xattn_bq, L2_xattn_Wk, L2_xattn_bk, L2_xattn_Wv, L2_xattn_bv, L2_xattn_Wo, L2_xattn_bo, L2_ffn_w_router, L2_ffn_w_gate, L2_ffn_w_up, L2_ffn_w_down, L3_xattn_Wq, L3_xattn_Wk, L3_xattn_Wv, L3_ffn_gate_weight, L3_ffn_w_gate, L3_ffn_w_up, L3_ffn_w_down, L3_ffn_ws_gate, L3_ffn_ws_up, L3_ffn_ws_down):
    import jax
    import jax.numpy as jnp

    def _L0_xattn_ref(values, keys, queries, mask, Wv, Wk, Wq, Wo, bo):
        import jax, jax.numpy as jnp
        import numpy as np
        EMBED = 128
        HEADS = 16
        HEAD_DIM = EMBED // HEADS
        NEG = -1e+20
        N, q_len, E = queries.shape
        v_len, k_len = (values.shape[1], keys.shape[1])
        H, D = (HEADS, HEAD_DIM)
        v = values.reshape(N, v_len, H, D)
        k = keys.reshape(N, k_len, H, D)
        q = queries.reshape(N, q_len, H, D)
        v = jnp.einsum('nlhd,ed->nlhe', v, Wv)
        k = jnp.einsum('nlhd,ed->nlhe', k, Wk)
        q = jnp.einsum('nlhd,ed->nlhe', q, Wq)
        scores = jnp.einsum('nqhd,nkhd->nhqk', q, k)
        scores = jnp.where(mask == 0, NEG, scores)
        attn = jax.nn.softmax(scores / E ** 0.5, axis=3)
        out = jnp.einsum('nhqk,nkhd->nqhd', attn, v).reshape(N, q_len, E)
        return out @ Wo.T + bo

    def _L0_ffn_ref(x, wqkv, q_scale, k_scale, wo, ln_g, ln_b, w1, b1, w2, b2):
        import jax, jax.numpy as jnp
        import numpy as np
        DIM = 128
        DEPTH = 2
        HEADS = 8
        DIM_HEAD = 64
        WINDOW = 64
        INNER = HEADS * DIM_HEAD
        HID = int(DIM * 4 * 2 / 3)
        B, N = (2, 1024)
        QK_SCALE = 8.0

        def shift_token(t):
            t1, t2 = jnp.split(t, 2, axis=-1)
            t2 = jnp.pad(t2, ((0, 0), (1, 0), (0, 0)))[:, :-1]
            return jnp.concatenate([t1, t2], axis=-1)

        def l2norm(t):
            return t / jnp.clip(jnp.linalg.norm(t, axis=-1, keepdims=True), 1e-12)

        def rotate_half(x):
            x1, x2 = jnp.split(x, 2, axis=-1)
            return jnp.concatenate([-x2, x1], axis=-1)

        def rotary_xpos(q, k):
            n = q.shape[-2]
            half_idx = jnp.arange(0, DIM_HEAD, 2, dtype=jnp.float32)
            inv_freq = 1.0 / 10000.0 ** (half_idx / DIM_HEAD)
            t = jnp.arange(n, dtype=jnp.float32)
            freqs = t[:, None] * inv_freq[None, :]
            freqs = jnp.concatenate([freqs, freqs], axis=-1)
            base = (half_idx + 0.4 * DIM_HEAD) / (1.4 * DIM_HEAD)
            power = (t - n // 2) / float(WINDOW // 2)
            scale = base[None, :] ** power[:, None]
            scale = jnp.concatenate([scale, scale], axis=-1)
            cos, sin = (jnp.cos(freqs), jnp.sin(freqs))
            q = q * cos * scale + rotate_half(q) * sin * scale
            k = k * cos / scale + rotate_half(k) * sin / scale
            return (q, k)

        def local_attention(q, k, v):
            b, h, n, d = q.shape
            w = n // WINDOW
            bq = q.reshape(b, h, w, WINDOW, d) * QK_SCALE
            bk = k.reshape(b, h, w, WINDOW, d)
            bv = v.reshape(b, h, w, WINDOW, d)

            def look_around(t):
                p = jnp.pad(t, ((0, 0), (0, 0), (1, 0), (0, 0), (0, 0)))
                return jnp.concatenate([p[:, :, :w], p[:, :, 1:]], axis=3)
            bk, bv = (look_around(bk), look_around(bv))
            bt = jnp.arange(n).reshape(w, WINDOW)
            btp = jnp.pad(bt, ((1, 0), (0, 0)), constant_values=-1)
            btk = jnp.concatenate([btp[:w], btp[1:]], axis=1)
            sim = jnp.einsum('bhwid,bhwjd->bhwij', bq, bk)
            i = bt[:, :, None]
            j = btk[:, None, :]
            mask = (i < j) | (i > j + WINDOW) | (j == -1)
            sim = jnp.where(mask, -jnp.finfo(sim.dtype).max, sim)
            attn = jax.nn.softmax(sim, axis=-1)
            out = jnp.einsum('bhwij,bhwjd->bhwid', attn, bv)
            return out.reshape(b, h, n, d)

        def _layer(x, wqkv, qs, ksc, wo, lg, lb, w1, b1, w2, b2):
            b, n, _ = x.shape
            h = shift_token(x)
            qkv = h @ wqkv
            q, k, v = jnp.split(qkv, 3, axis=-1)
            to_heads = lambda t: t.reshape(b, n, HEADS, DIM_HEAD).transpose(0, 2, 1, 3)
            q, k, v = (to_heads(q), to_heads(k), to_heads(v))
            q = l2norm(q) * qs
            k = l2norm(k) * ksc
            q, k = rotary_xpos(q, k)
            o = local_attention(q, k, v)
            o = o.transpose(0, 2, 1, 3).reshape(b, n, INNER)
            x = x + o @ wo
            h = shift_token(x)
            mu = h.mean(-1, keepdims=True)
            var = h.var(-1, keepdims=True)
            h = (h - mu) / jnp.sqrt(var + 1e-05) * lg + lb
            h = h @ w1 + b1
            a, g = jnp.split(h, 2, axis=-1)
            h = a * jax.nn.gelu(g, approximate=False)
            x = x + h @ w2 + b2
            return x
        for l in range(DEPTH):
            x = _layer(x, wqkv[l], q_scale[l], k_scale[l], wo[l], ln_g[l], ln_b[l], w1[l], b1[l], w2[l], b2[l])
        return x

    def _L1_xattn_ref(q, k, v, mask, Wq, bq, Wk, bk, Wv, bv, Wo, bo):
        import jax, jax.numpy as jnp
        import numpy as np
        D_MODEL = 128
        NUM_HEADS = 16
        D_K = D_MODEL // NUM_HEADS
        NEG = -1000000000.0

        def _split_heads(x):
            b, s, _ = x.shape
            return x.reshape(b, s, NUM_HEADS, D_K).transpose(0, 2, 1, 3)
        qh = _split_heads(q @ Wq.T + bq)
        kh = _split_heads(k @ Wk.T + bk)
        vh = _split_heads(v @ Wv.T + bv)
        scores = jnp.einsum('bhqd,bhkd->bhqk', qh, kh) / jnp.sqrt(jnp.float32(D_K))
        scores = jnp.where(mask == 0, jnp.float32(NEG), scores)
        attn = jax.nn.softmax(scores, axis=-1)
        out = jnp.einsum('bhqk,bhkd->bhqd', attn, vh)
        b, h, s, dk = out.shape
        out = out.transpose(0, 2, 1, 3).reshape(b, s, D_MODEL)
        return out @ Wo.T + bo

    def _L1_ffn_ref(x, centroids, gamma, beta, W1, b1, W2, b2):
        import jax, jax.numpy as jnp
        import numpy as np
        B, S, D, F, E = (1, 128, 128, 512, 8)
        EPS = 1e-05

        def _sublayer(xs, g, b, W1e, b1e, W2e, b2e):
            mu = jnp.mean(xs, axis=-1, keepdims=True)
            var = jnp.mean(jnp.square(xs - mu), axis=-1, keepdims=True)
            h = (xs - mu) * jax.lax.rsqrt(var + EPS) * g + b
            return xs + jax.nn.relu(h @ W1e.T + b1e) @ W2e.T + b2e
        feats = x.reshape(-1, x.shape[-1])
        scores = jax.lax.stop_gradient(feats @ centroids.T)
        expert = jnp.argmax(scores, axis=1)
        onehot = jax.nn.one_hot(expert, E, dtype=feats.dtype)
        alpha = jax.nn.sigmoid(jnp.sum(feats * centroids[expert], axis=-1, keepdims=True))
        ys = jax.vmap(_sublayer, in_axes=(None, 0, 0, 0, 0, 0, 0))(feats, gamma, beta, W1, b1, W2, b2)
        y = jnp.einsum('te,etd->td', onehot, ys)
        out = alpha * y + (1.0 - alpha) * feats
        return out.reshape(x.shape)

    def _L2_xattn_ref(q, k, v, Wq, bq, Wk, bk, Wv, bv, Wo, bo):
        import jax, jax.numpy as jnp
        import numpy as np
        D_MODEL = 128
        NHEAD = 16
        D_HEAD = D_MODEL // NHEAD
        B, Nq, _ = q.shape
        Nk = k.shape[1]
        Q = q @ Wq + bq
        K = k @ Wk + bk
        V = v @ Wv + bv
        Q = Q.reshape(B, Nq, NHEAD, D_HEAD).transpose(0, 2, 1, 3)
        K = K.reshape(B, Nk, NHEAD, D_HEAD).transpose(0, 2, 1, 3)
        V = V.reshape(B, Nk, NHEAD, D_HEAD).transpose(0, 2, 1, 3)
        scores = jnp.einsum('bhqd,bhkd->bhqk', Q, K) / jnp.sqrt(jnp.float32(D_HEAD))
        attn = jax.nn.softmax(scores, axis=-1)
        context = jnp.einsum('bhqk,bhkd->bhqd', attn, V)
        context = context.transpose(0, 2, 1, 3).reshape(B, Nq, D_MODEL)
        out = context @ Wo + bo
        return out

    def _L2_ffn_ref(x, w_router, w_gate, w_up, w_down):
        import math
        import jax, jax.numpy as jnp
        import numpy as np
        CAPACITY_FACTOR = 1.25
        B, S, H = x.shape
        E = w_gate.shape[0]
        T = B * S
        C = int(math.ceil(CAPACITY_FACTOR * T / E))
        xt = x.reshape(T, H)
        logits = xt @ w_router
        probs = jax.nn.softmax(logits, axis=-1)
        top1 = jnp.argmax(probs, axis=-1)
        gate = jnp.take_along_axis(probs, top1[:, None], axis=1)[:, 0]
        onehot = jax.nn.one_hot(top1, E, dtype=jnp.int32)
        pos = jnp.cumsum(onehot, axis=0)[jnp.arange(T), top1] - 1
        accepted = pos < C
        slot = jnp.where(accepted, top1 * C + pos, E * C)
        buf = jnp.zeros((E * C + 1, H), dtype=x.dtype).at[slot].set(xt)
        buf = buf[:E * C].reshape(E, C, H)
        g = jnp.einsum('ech,ehf->ecf', buf, w_gate)
        u = jnp.einsum('ech,ehf->ecf', buf, w_up)
        y = jnp.einsum('ecf,efh->ech', jax.nn.silu(g) * u, w_down)
        out_tok = y.reshape(E * C, H)[jnp.clip(slot, 0, E * C - 1)]
        out_tok = jnp.where(accepted[:, None], out_tok * gate[:, None], 0.0)
        return (xt + out_tok).reshape(B, S, H)

    def _L3_xattn_ref(value, key, query, mask, Wq, Wk, Wv):
        import jax, jax.numpy as jnp
        import numpy as np
        HEAD = 16
        NEG_FILL = -1e+20
        N, Lq, E = query.shape
        H = HEAD
        D = E // H
        q = jnp.einsum('nqhd,de->nqhe', query.reshape(N, Lq, H, D), Wq)
        k = jnp.einsum('nkhd,de->nkhe', key.reshape(N, key.shape[1], H, D), Wk)
        v = jnp.einsum('nvhd,de->nvhe', value.reshape(N, value.shape[1], H, D), Wv)
        energy = jnp.einsum('nqhd,nkhd->nhqk', q, k)
        energy = energy * mask
        energy = jnp.where(energy == 0, NEG_FILL, energy)
        attention = jax.nn.softmax(energy, axis=-1)
        out = jnp.einsum('nhql,nlhd->nqhd', attention, v).reshape(N, Lq, H * D)
        return out

    def _L3_ffn_ref(hidden_states, gate_weight, w_gate, w_up, w_down, ws_gate, ws_up, ws_down):
        import jax, jax.numpy as jnp
        import numpy as np
        H = 128
        I = 64
        E = 8
        TOP_K = 2
        N_SHARED = 2
        SHARED_I = I * N_SHARED
        SCALE = 2.5
        NORM_TOPK = True
        B, S = (2, 128)

        def _swiglu(x, wg, wu, wd):
            g = x @ wg.T
            u = x @ wu.T
            return jax.nn.silu(g) * u @ wd.T
        b, s, h = hidden_states.shape
        x = hidden_states.reshape(-1, h)
        shared_out = _swiglu(x, ws_gate, ws_up, ws_down)
        logits = x.astype(jnp.float32) @ gate_weight.astype(jnp.float32).T
        scores = jax.nn.sigmoid(logits)
        topk_w, topk_idx = jax.lax.top_k(scores, TOP_K)
        if TOP_K > 1 and NORM_TOPK:
            topk_w = topk_w / (topk_w.sum(-1, keepdims=True) + 1e-20)
        topk_w = topk_w * SCALE
        onehot = jax.nn.one_hot(topk_idx, E, dtype=topk_w.dtype)
        combine = jnp.einsum('tk,tke->te', topk_w, onehot)
        g = jnp.einsum('th,eih->tei', x, w_gate)
        u = jnp.einsum('th,eih->tei', x, w_up)
        hmid = jax.nn.silu(g) * u
        y = jnp.einsum('tei,ehi->teh', hmid, w_down)
        routed_out = jnp.einsum('te,teh->th', combine, y)
        out = (routed_out + shared_out).reshape(b, s, h)
        return out
    x = x + _L0_xattn_ref(ctx_1024, ctx_1024, _layernorm(x, axis=-1), mask_Bx1x1xS2_if1, L0_xattn_Wv, L0_xattn_Wk, L0_xattn_Wq, L0_xattn_Wo, L0_xattn_bo)
    x = x + _L0_ffn_ref(_layernorm(x, axis=-1), L0_ffn_wqkv, L0_ffn_q_scale, L0_ffn_k_scale, L0_ffn_wo, L0_ffn_ln_g, L0_ffn_ln_b, L0_ffn_w1, L0_ffn_b1, L0_ffn_w2, L0_ffn_b2)
    x = x + _L1_xattn_ref(_layernorm(x, axis=-1), ctx_1024, ctx_1024, mask_1x1xSxS2_if1, L1_xattn_Wq, L1_xattn_bq, L1_xattn_Wk, L1_xattn_bk, L1_xattn_Wv, L1_xattn_bv, L1_xattn_Wo, L1_xattn_bo)
    x = x + _L1_ffn_ref(_layernorm(x, axis=-1), L1_ffn_centroids, L1_ffn_gamma, L1_ffn_beta, L1_ffn_W1, L1_ffn_b1, L1_ffn_W2, L1_ffn_b2)
    x = x + _L2_xattn_ref(_layernorm(x, axis=-1), ctx_1024, ctx_1024, L2_xattn_Wq, L2_xattn_bq, L2_xattn_Wk, L2_xattn_bk, L2_xattn_Wv, L2_xattn_bv, L2_xattn_Wo, L2_xattn_bo)
    x = x + _L2_ffn_ref(_layernorm(x, axis=-1), L2_ffn_w_router, L2_ffn_w_gate, L2_ffn_w_up, L2_ffn_w_down)
    x = x + _L3_xattn_ref(ctx_1024, ctx_1024, _layernorm(x, axis=-1), mask_1x1xSxS2_fk0, L3_xattn_Wq, L3_xattn_Wk, L3_xattn_Wv)
    x = x + _L3_ffn_ref(_layernorm(x, axis=-1), L3_ffn_gate_weight, L3_ffn_w_gate, L3_ffn_w_up, L3_ffn_w_down, L3_ffn_ws_gate, L3_ffn_ws_up, L3_ffn_ws_down)
    return x

_drawn_inputs = setup_inputs


def setup_inputs(seed=0):
    import zlib

    import numpy as np

    out = dict(_drawn_inputs(seed))
    spreads = {'L0_xattn_bo': (0.0, 0.1),
     'L0_ffn_q_scale': (1.0, 0.6),
     'L0_ffn_k_scale': (1.0, 0.6),
     'L0_ffn_ln_g': (1.0, 0.6),
     'L0_ffn_ln_b': (0.0, 0.8),
     'L0_ffn_b1': (0.0, 0.8),
     'L0_ffn_b2': (0.0, 0.1),
     'L1_ffn_gamma': (1.0, 0.6),
     'L1_ffn_beta': (0.0, 0.8),
     'L1_ffn_b1': (0.0, 0.8),
     'L1_ffn_b2': (0.0, 0.289),
     'L2_xattn_bq': (0.0, 0.8),
     'L2_xattn_bk': (0.0, 2.0),
     'L2_xattn_bv': (0.0, 0.288),
     'L2_xattn_bo': (0.0, 0.268)}
    factors = {'L0_ffn_w1': 6.038,
     'L0_ffn_w2': 5.905,
     'L1_xattn_Wq': 8.0,
     'L1_xattn_bq': 8.0,
     'L1_xattn_Wk': 8.0,
     'L1_xattn_bk': 200.0,
     'L1_xattn_Wv': 4.521,
     'L1_xattn_bv': 8.0,
     'L1_xattn_Wo': 4.438,
     'L1_xattn_bo': 4.972,
     'L1_ffn_W1': 3.305,
     'L3_ffn_gate_weight': 8.0,
     'L3_ffn_w_gate': 8.0,
     'L3_ffn_w_up': 8.0,
     'L3_ffn_w_down': 8.0,
     'L3_ffn_ws_gate': 8.0,
     'L3_ffn_ws_up': 8.0,
     'L3_ffn_ws_down': 8.0,
     'L2_ffn_w_router': 2.792,
     'L2_ffn_w_gate': 2.863,
     'L2_ffn_w_down': 3.543}
    for name, (base, spread) in spreads.items():
        noise = np.random.default_rng([zlib.crc32(name.encode()), seed]).standard_normal(out[name].shape)
        drawn = base * np.exp(spread * noise) if base else spread * noise
        out[name] = jnp.asarray(drawn.astype(out[name].dtype))
    for name, factor in factors.items():
        out[name] = (out[name] * factor).astype(out[name].dtype)
    return out
```

```python
from contextlib import ExitStack

import concourse.bass as bass
from concourse import mybir

ALU = mybir.AluOpType
ACT = mybir.ActivationFunctionType
AX = mybir.AxisListType
F32 = mybir.dt.float32
I32 = mybir.dt.int32

B = 8
P = 128
T = B * P
HB = B // 2
HALF = T // 2
NX = 4
XH, XD = 16, 8
LH, LD = 8, 64
LAYERS = 2
WINDOW = 64
HID = 341
HCH = [(0, 128), (128, 128), (256, HID - 256)]
E1, F1 = 8, 512
FC1 = F1 // P
E2, C2 = 32, 40
SLOTS = E2 * C2
SCH = SLOTS // P
SPAN2 = 4
E3, I3 = 8, 64
CH3 = E3 * I3 // P + 1
ROUTED_SCALE = 2.5
EPS = 1e-5
NEG = -float(2 ** 100)
LOWEST = -3.0e38


class Count:

    def __init__(self, sem):
        self.sem = sem
        self.base = 0


class Core:

    def __init__(self, nc, ctx):
        self.nc = nc
        self.ctx = ctx
        self.counts = {}
        self.made = {}

    def sb(self, name, shape, dt=F32):
        return self.ctx.enter_context(self.nc.sbuf_tensor(name, shape, dt))

    def fresh(self, ctx, name, shape, dt=F32):
        self.made[name] = self.made.get(name, 0) + 1
        return ctx.enter_context(self.nc.sbuf_tensor(f"{name}_{self.made[name]}", shape, dt))

    def count(self, name):
        if name not in self.counts:
            self.counts[name] = Count(self.ctx.enter_context(self.nc.semaphore(name)))
        return self.counts[name]


def spread(ap, n):
    return ap.unsqueeze(len(ap.shape)).to_broadcast(list(ap.shape) + [n])


def setup(k, d):
    nc = k.nc
    load, made, masks, tabs = (k.count(n) for n in ("su_load", "su_made", "su_masks", "su_tabs"))
    k.x, k.xn = k.sb("x", [P, B, P]), k.sb("xn", [P, B, P])
    k.xnT, k.ctxT = k.sb("xnT", [P, T]), k.sb("ctxT", [P, T])
    k.st, k.mv = k.sb("st", [P, B, 6]), k.sb("mv", [P, B, 2])
    k.ve, k.rs, k.mhalf = k.sb("ve", [P, B]), k.sb("rs", [P, B]), k.sb("mhalf", [P, 2 * LH])
    k.ident, k.ones, k.zeros = k.sb("ident", [P, P]), k.sb("ones", [P, HALF]), k.sb("zeros", [P, P])
    k.band, k.mask1, k.mask3 = k.sb("band", [P, P]), k.sb("mask1", [P, P]), k.sb("mask3", [P, P])
    k.negkeys, k.strip = k.sb("negkeys", [1, T]), k.sb("strip", [1, P])
    k.wq, k.wk = k.sb("wq", [P, NX, 4 * P]), k.sb("wk", [P, NX, 4 * P])
    k.bqk, k.wo, k.bo = k.sb("bqk", [P, NX, 2, 4]), k.sb("wo", [P, 3, P]), k.sb("bo", [1, 3, P])
    k.v1 = k.sb("v1", [P, B, NX, XH, XD + 1])
    k.qkT = k.sb("qkT", [P, B, 2, 4, P])
    k.prime, k.prime2 = k.sb("prime", [P, 1]), k.sb("prime2", [P, 1])
    with ExitStack() as own:
        def sb(name, shape, dt=F32):
            return k.fresh(own, name, shape, dt)
        wv, bv = sb("wv", [P, NX * P]), sb("bv", [1, NX * P])
        keys_i, mask1_i = sb("keys_i", [1, T], I32), sb("mask1_i", [P, P], I32)
        vready, vout = k.count("su_v"), k.count("su_vout")
        with nc.Block() as block:
            @block.sync
            def _(sp):
                sp.dma_start(k.ctxT[:, :], d["ctxT"]).then_inc(load.sem, 16)
                sp.dma_start(wv[:, :], d["wv"]).then_inc(load.sem, 16)
                sp.dma_start(bv[:, :], d["bv"]).then_inc(load.sem, 16)
                sp.dma_start(keys_i[:, :], d["keys"]).then_inc(load.sem, 16)
                sp.dma_start(mask1_i[:, :], d["mask1"]).then_inc(load.sem, 16)
                sp.dma_start(k.mask3[:, :], d["mask3"]).then_inc(load.sem, 16)
                sp.dma_start(k.strip[:, :], d["strip"]).then_inc(load.sem, 16)
                sp.dma_start(k.bqk[:, :, :, :], d["bqk"]).then_inc(load.sem, 16)
                sp.dma_start(k.bo[:, :, :], d["bo"]).then_inc(load.sem, 16)
                sp.wait_ge(load.sem, 16 * 13)

            @block.scalar
            def _(a):
                a.dma_start(k.x[:, :, :], d["x"]).then_inc(load.sem, 16)
                a.dma_start(k.wq[:, :, :], d["wq"]).then_inc(load.sem, 16)
                a.dma_start(k.wk[:, :, :], d["wk"]).then_inc(load.sem, 16)
                a.dma_start(k.wo[:, :, :], d["wo"]).then_inc(load.sem, 16)
                for b in range(0, B, 2):
                    a.wait_ge(vready.sem, b + 1)
                    a.activation(k.v1[:, b, :, :, 0:XD],
                                 k.ps[:, b, :].rearrange("p (a h e) -> p a h e", a=NX, e=XD),
                                 ACT.Copy).then_inc(vout.sem, 1)

            @block.gpsimd
            def _(g):
                g.memset(k.ident[:, :], 0.0).then_inc(made.sem, 1)
                g.memset(k.band[:, :], 0.0).then_inc(made.sem, 1)
                g.memset(k.ones[:, :], 1.0).then_inc(made.sem, 1)
                g.memset(k.zeros[:, :], 0.0).then_inc(made.sem, 1)
                g.memset(k.mhalf[:, :], -0.5).then_inc(made.sem, 1)
                g.memset(k.v1[:, :, :, :, XD:XD + 1], 1.0).then_inc(made.sem, 1)
                g.wait_ge(made.sem, 6)
                g.affine_select(out=k.ident[:, :], in_=k.ident[:, :], compare_op=ALU.not_equal, fill=1.0,
                                base=0, pattern=[[-1, P]], channel_multiplier=1).then_inc(made.sem, 1)
                g.affine_select(out=k.band[:, :], in_=k.band[:, :], compare_op=ALU.is_ge, fill=NEG,
                                base=0, pattern=[[-1, P]], channel_multiplier=1).then_inc(made.sem, 1)
                g.wait_ge(made.sem, 8)
                g.affine_select(out=k.band[:, :], in_=k.band[:, :], compare_op=ALU.is_ge, fill=NEG,
                                base=WINDOW, pattern=[[1, P]], channel_multiplier=-1).then_inc(made.sem, 1)

            @block.vector
            def _(v):
                v.wait_ge(load.sem, 16 * 13)
                v.tensor_scalar(k.negkeys[:, :], keys_i[:, :], 0.0, NEG, ALU.is_equal, ALU.mult)
                v.tensor_scalar(k.mask1[:, :], mask1_i[:, :], 0.0, NEG, ALU.is_equal, ALU.mult)
                for b in range(1, B, 2):
                    v.wait_ge(vready.sem, b + 1)
                    v.tensor_copy(k.v1[:, b, :, :, 0:XD],
                                  k.ps[:, b, :].rearrange("p (a h e) -> p a h e", a=NX, e=XD))\
                     .then_inc(vout.sem, 1)

            @block.tensor
            def _(t):
                t.wait_ge(load.sem, 16 * 13)
                t.wait_ge(made.sem, 3)
                for b in range(B):
                    t.matmul(k.ps[:, b, :], k.ctxT[:, b * P:(b + 1) * P], wv[:, :], start=True, stop=False)
                    t.matmul(k.ps[:, b, :], k.ones[0:1, 0:P], bv[0:1, :], start=False, stop=True)\
                     .then_inc(vready.sem, 1)


def layer_norm(k, src, dst, dst_t, gain=None, shift=None):
    nc, ps = k.nc, k.ps
    stats, var, rstd, norm, turned, out = (k.count("ln_" + n) for n in (
        "stats", "var", "rstd", "norm", "turned", "out"))
    with nc.Block() as block:
        @block.vector
        def _(v):
            for b in range(B):
                v.bn_stats(k.st[:, b, :], src(b)).then_inc(stats.sem, 1)
            for b in range(B):
                v.wait_ge(stats.sem, stats.base + b + 1)
                v.bn_aggr(k.mv[:, b, :], k.st[:, b, :]).then_inc(var.sem, 1)
            v.wait_ge(var.sem, var.base + B)
            v.tensor_scalar(k.ve[:, :], k.mv[:, :, 1], EPS, None, ALU.add).then_inc(var.sem, 1)
            v.wait_ge(rstd.sem, rstd.base + 1)
            for b in range(B):
                v.tensor_scalar(dst[:, b, :], src(b), k.mv[:, b, 0:1], k.rs[:, b:b + 1],
                                ALU.subtract, ALU.mult).then_inc(norm.sem, 1)

        @block.gpsimd
        def _(g):
            g.wait_ge(var.sem, var.base + B + 1)
            g.tensor_tensor(k.rs[:, :], k.ve[:, :], k.mhalf[:, 0:B], ALU.pow).then_inc(rstd.sem, 1)

        @block.tensor
        def _(t):
            for b in range(B):
                t.wait_ge(norm.sem, norm.base + b + 1)
                t.transpose(ps[:, b // HB, P * (b % HB):P * (b % HB) + P], dst[:, b, :],
                            k.ident[:, :]).then_inc(turned.sem, 1)

        @block.scalar
        def _(a):
            for h in range(2):
                a.wait_ge(turned.sem, turned.base + HB * (h + 1))
                cols = slice(h * HALF, (h + 1) * HALF)
                if gain is None:
                    a.activation(dst_t[:, cols], ps[:, h, :], ACT.Copy).then_inc(out.sem, 1)
                else:
                    a.activation(dst_t[:, cols], ps[:, h, :], ACT.Identity, scale=gain, bias=shift)\
                     .then_inc(out.sem, 1)
    stats.base += B
    var.base += B + 1
    rstd.base += 1
    norm.base += B
    turned.base += B
    out.base += 2


def cross_projections(k, a):
    nc, ps = k.nc, k.ps
    qready, kready, qout, kout = (k.count("pj_" + n) for n in ("qready", "kready", "qout", "kout"))
    units = [(g, h) for g in range(4) for h in range(2)]
    with nc.Block() as block:
        @block.tensor
        def _(t):
            for n, (g, h) in enumerate(units):
                cols = slice(h * HALF, (h + 1) * HALF)
                if n >= 4:
                    t.wait_ge(qout.sem, qout.base + n - 3)
                t.matmul(ps[:, n % 4, :], k.wq[:, a, g * P:(g + 1) * P], k.xnT[:, cols],
                         start=True, stop=True).then_inc(qready.sem, 1)
                if n >= 4:
                    t.wait_ge(kout.sem, kout.base + n - 3)
                m = t.matmul(ps[:, 4 + n % 4, :], k.wk[:, a, g * P:(g + 1) * P], k.ctxT[:, cols],
                             start=True, stop=(a != 0))
                if a == 0:
                    m = t.matmul(ps[:, 4 + n % 4, :], k.strip[0:1, :], k.negkeys[0:1, cols],
                                 start=False, stop=True)
                m.then_inc(kready.sem, 1)

        @block.scalar
        def _(s):
            for n, (g, h) in enumerate(units):
                s.wait_ge(qready.sem, qready.base + n + 1)
                s.activation(k.qkT[:, HB * h:HB * h + HB, 0, g, :],
                             ps[:, n % 4, :].rearrange("p (b t) -> p b t", b=HB), ACT.Identity,
                             bias=k.bqk[:, a, 0, g:g + 1]).then_inc(qout.sem, 1)

        @block.vector
        def _(v):
            for n, (g, h) in enumerate(units):
                v.wait_ge(kready.sem, kready.base + n + 1)
                v.tensor_scalar(k.qkT[:, HB * h:HB * h + HB, 1, g, :],
                                ps[:, 4 + n % 4, :].rearrange("p (b t) -> p b t", b=HB),
                                k.bqk[:, a, 1, g:g + 1], None, ALU.add).then_inc(kout.sem, 1)
    for s in (qready, kready, qout, kout):
        s.base += len(units)


def over_batches(eng, step):
    step(0, 0, 0)
    step(1, 1, 1)
    with eng.Fori(0, (B - 4) // 2) as i:
        step(2 * i + 2, 0, 2)
        step(2 * i + 3, 1, 2)
    step(B - 2, 0, B - 2)
    step(B - 1, 1, B - 1)


def attention(k, kind, x, values, weights, bias=None):
    nc, ps = k.nc, k.ps
    local, select = kind == "local", kind == 3
    project = not select
    G = 2 if local else 4
    W = LD if local else XD
    NH = 4 * G
    CH = NH * W // P
    scale = {"local": 8.0, 0: P ** -0.5, 1: XD ** -0.5, 2: XD ** -0.5, 3: 1.0}[kind]
    mask = {"local": k.band, 0: k.zeros, 1: k.mask1, 2: k.zeros, 3: k.mask3}[kind]
    slot_in = [k.count("at_slot0_in"), k.count("at_slot1_in")]
    (scored, times, zeroed, top, minus, expd, turned, evac_even, evac_odd, pv, recip, normed,
     oturned, oT_out, projected, res) = (k.count("at_" + n) for n in (
        "scored", "times", "zeroed", "top", "minus", "expd", "turned", "evac_even",
        "evac_odd", "pv", "recip", "normed", "oturned", "oT_out", "projected", "res"))
    with ExitStack() as own:
        def sb(name, shape):
            return k.fresh(own, name, shape)
        slot, sm = sb("slot", [P, 2, 2, 4, P]), sb("sm", [P, 2, G, 4, P])
        pace = sb("pace", [P, 2, G])
        mx, pt, zt = sb("mx", [P, 2, G, 4]), sb("pt", [P, 2, 4, P]), sb("zt", [P, 2, 4, P])
        ro, on, oT = sb("ro", [P, NH]), sb("on", [P, NH, W]), sb("oT", [P, CH * P])
        on_flat = on[:, :, :].rearrange("p h w -> p (h w)")

        def qk(p, which, g, j):
            if local:
                return slot[LD * g:LD * (g + 1), p, which, j, :]
            rows = XD + 1 if kind == 0 else XD
            return slot[32 * g:32 * g + rows, p, which, j, :]

        def scores(g, j):
            return ps[:, g, j * P:(j + 1) * P]

        def out(g, j):
            if local:
                return ps[:, 2 + g, j * (W + 1):(j + 1) * (W + 1)]
            return ps[:, 6, (4 * g + j) * (W + 1):(4 * g + j + 1) * (W + 1)]

        if local:
            o_all = ps[:, 2:4, 0:4 * (W + 1)].rearrange("p g (h w) -> p g h w", w=W + 1)
            on_all = on[:, :, :].rearrange("p (g h) w -> p g h w", g=2)
            ro_all = ro[:, :].rearrange("p (g h) -> p g h", g=2)
            o_sum, o_val = o_all[:, :, :, W], o_all[:, :, :, 0:W]
        else:
            o_all = ps[:, 6, 0:NH * (W + 1)].rearrange("p (h w) -> p h w", w=W + 1)
            on_all, ro_all = on[:, :, :], ro[:, :]
            o_sum, o_val = o_all[:, :, W], o_all[:, :, 0:W]
        oT_ps = ps[:, 6, :] if local else ps[:, 7, 0:P]
        proj_ps = ps[:, 7, 3 * P:4 * P]

        with nc.Block() as block:
            @block.sync
            def _(sp):
                sp.dma_start(slot[:, 0], k.qkT[:, 0]).then_inc(slot_in[0].sem, 16)
                sp.dma_start(slot[:, 1], k.qkT[:, 1]).then_inc(slot_in[1].sem, 16)
                with sp.Fori(0, (B - 2) // 2) as i:
                    for p in range(2):
                        sp.wait_ge(scored.sem, scored.base + NH * (2 * i + p + 1))
                        sp.dma_start(slot[:, p], k.qkT[:, 2 * i + 2 + p]).then_inc(slot_in[p].sem, 16)

            @block.tensor
            def _(t):
                def score(b, p, first=False):
                    t.wait_ge(slot_in[p].sem, slot_in[p].base + 8 * (b - p) + 16)
                    for g in range(0, G, 2):
                        if not first and select:
                            t.wait_ge(times.sem, times.base + G * (b - 1) + g + 2)
                        elif not first:
                            t.wait_ge(top.sem, top.base + NH * (b - 1) + 4 * g + 8)
                        for j in range(4):
                            for gg in (g, g + 1):
                                t.matmul(scores(gg, j), qk(p, 0, gg, j), qk(p, 1, gg, j),
                                         start=True, stop=True).then_inc(scored.sem, 1)

                def turn(b, p, g, first):
                    t.wait_ge(expd.sem, expd.base + G * b + g + 1)
                    if not (first and g < 2):
                        e = evac_odd if g % 2 else evac_even
                        t.wait_ge(e.sem, e.base + G // 2 * b + g // 2)
                    for j in range(4):
                        m = t.transpose(ps[:, 4 + g % 2, j * P:(j + 1) * P], sm[:, p, g, j, :],
                                        k.ident[:, :])
                    m.then_inc(turned.sem, 1)

                def weigh(b, g, first):
                    e = evac_odd if g % 2 else evac_even
                    t.wait_ge(e.sem, e.base + G // 2 * b + g // 2 + 1)
                    if g == 0 and not first:
                        t.wait_ge(normed.sem, normed.base + b)
                    for j in range(4):
                        m = t.matmul(out(g, j), pt[:, g % 2, j, :], values(b, 4 * g + j),
                                     start=True, stop=True)
                    m.then_inc(pv.sem, 1)

                def project_out(b, first):
                    t.wait_ge(normed.sem, normed.base + b + 1)
                    if not first:
                        t.wait_ge(res.sem, res.base + b)
                    for n in range(CH):
                        m = t.transpose(oT_ps[:, n * P:(n + 1) * P], on_flat[:, n * P:(n + 1) * P],
                                        k.ident[:, :])
                    m.then_inc(oturned.sem, 1)
                    t.wait_ge(oT_out.sem, oT_out.base + b + 1)
                    for n in range(CH):
                        m = t.matmul(proj_ps, oT[:, n * P:(n + 1) * P], weights(n), start=(n == 0),
                                     stop=(bias is None and n == CH - 1))
                    if bias is not None:
                        m = t.matmul(proj_ps, k.ones[0:1, 0:P], bias, start=False, stop=True)
                    m.then_inc(projected.sem, 1)

                def step(b, p, place):
                    if place < B - 1:
                        score(b + 1, 1 - p)
                    if place > 0 and project:
                        project_out(b - 1, place == 1)
                    turn(b, p, 0, place == 0)
                    turn(b, p, 1, place == 0)
                    for g in range(2, G):
                        weigh(b, g - 2, place == 0)
                        turn(b, p, g, place == 0)
                    weigh(b, G - 2, place == 0)
                    weigh(b, G - 1, place == 0)

                score(0, 0, True)
                over_batches(t, step)
                if project:
                    project_out(B - 1, False)

            @block.vector
            def _(v):
                def masked_max(b, p, g, early):
                    if select:
                        v.wait_ge(zeroed.sem, zeroed.base + G * b + g + 1)
                    else:
                        v.wait_ge(scored.sem, scored.base + NH * b + 8 * (g // 2) + 8)
                        if not early:
                            v.wait_ge(turned.sem, turned.base + G * (b - 2) + g + 1)
                    v.memset(pace[:, p, g:g + 1], 0.0)
                    for j in range(4):
                        v.tensor_tensor_reduce(
                            sm[:, p, g, j, :], sm[:, p, g, j, :] if select else scores(g, j),
                            zt[:, g % 2, j, :] if select else mask[:, :], 1.0, LOWEST, ALU.add, ALU.max,
                            mx[:, p, g, j:j + 1]).then_inc(top.sem, 1)

                def multiply(b, p, g, early):
                    v.wait_ge(scored.sem, scored.base + NH * b + 8 * (g // 2) + 8)
                    if not early:
                        v.wait_ge(turned.sem, turned.base + G * (b - 2) + g + 1)
                    v.tensor_tensor(sm[:, p, g], ps[:, g, :].rearrange("p (j t) -> p j t", j=4),
                                    mask[:, :].unsqueeze(1).to_broadcast([P, 4, P]), ALU.mult)\
                     .then_inc(times.sem, 1)

                def zero_term(b, p, g, first):
                    v.wait_ge(times.sem, times.base + G * b + g + 1)
                    if not (first and g < 2):
                        v.wait_ge(top.sem, top.base + 4 * (G * b + g - 1))
                    v.tensor_scalar(zt[:, g % 2], sm[:, p, g], 0.0, NEG, ALU.is_equal, ALU.mult)\
                     .then_inc(zeroed.sem, 1)

                def evacuate(b, g, first):
                    v.wait_ge(turned.sem, turned.base + G * b + g + 1)
                    if not (first and g < 2):
                        v.wait_ge(pv.sem, pv.base + G * b + g - 1)
                    v.tensor_copy(pt[:, g % 2], ps[:, 4 + g % 2, :].rearrange("p (j t) -> p j t", j=4))\
                     .then_inc(evac_even.sem, 1)

                def normalise(b, first):
                    v.wait_ge(pv.sem, pv.base + G * b + G)
                    v.reciprocal(ro_all, o_sum).then_inc(recip.sem, 1)
                    v.wait_ge(recip.sem, recip.base + b + 1)
                    if project and not first:
                        v.wait_ge(oturned.sem, oturned.base + b)
                    v.tensor_tensor(on_all, o_val, spread(ro_all, W), ALU.mult).then_inc(normed.sem, 1)
                    if not project:
                        v.wait_ge(normed.sem, normed.base + b + 1)
                        v.tensor_tensor(x[:, b, :], x[:, b, :], on_flat, ALU.add).then_inc(res.sem, 1)
                        v.wait_ge(res.sem, res.base + b + 1)

                def residual(b):
                    v.wait_ge(projected.sem, projected.base + b + 1)
                    v.tensor_tensor(x[:, b, :], x[:, b, :], proj_ps, ALU.add).then_inc(res.sem, 1)

                def scores_of(b, p, early, between, first=False):
                    ahead = 2 if select else 0
                    for g in range(G + ahead):
                        if select and g < G:
                            multiply(b, p, g, early)
                        if select and 1 <= g <= G:
                            zero_term(b, p, g - 1, first)
                        if g >= ahead:
                            masked_max(b, p, g - ahead, early)
                        for work in between.get(g, ()):
                            work()

                def step(b, p, place):
                    first = place == 0
                    work = [lambda: evacuate(b, 0, first)]
                    if place > 0 and project:
                        work.insert(0 if local else 1, lambda: residual(b - 1))
                    if G > 2:
                        work.append(lambda: evacuate(b, 2, first))
                    if place < B - 1:
                        n = len(work)
                        slots = {1: work[:1], G - 2: work[1:n - 1], G - 1: work[n - 1:]} if G > 2 else \
                            {G - 1: work}
                        scores_of(b + 1, 1 - p, place == 0, slots)
                    else:
                        for w in work:
                            w()
                    normalise(b, first)

                scores_of(0, 0, True, {}, True)
                over_batches(v, step)
                if project:
                    residual(B - 1)

            @block.gpsimd
            def _(g_):
                def subtract(b, p, g):
                    g_.wait_ge(top.sem, top.base + NH * b + 4 * g + 4)
                    g_.tensor_tensor(sm[:, p, g], sm[:, p, g], spread(mx[:, p, g, :], P), ALU.subtract)\
                      .then_inc(minus.sem, 1)

                def shift(b, p):
                    for g in range(G):
                        subtract(b, p, g)

                def step(b, p, place):
                    if place < B - 1:
                        shift(b + 1, 1 - p)

                shift(0, 0)
                over_batches(g_, step)

            @block.scalar
            def _(a):
                def exponent(b, p, g):
                    a.wait_ge(minus.sem, minus.base + G * b + g + 1)
                    a.activation(sm[:, p, g], sm[:, p, g], ACT.Exp, scale=scale).then_inc(expd.sem, 1)

                def evacuate(b, g, first):
                    a.wait_ge(turned.sem, turned.base + G * b + g + 1)
                    if not (first and g < 2):
                        a.wait_ge(pv.sem, pv.base + G * b + g - 1)
                    a.activation(pt[:, g % 2], ps[:, 4 + g % 2, :].rearrange("p (j t) -> p j t", j=4),
                                 ACT.Copy).then_inc(evac_odd.sem, 1)

                def take_oT(b, first):
                    a.wait_ge(oturned.sem, oturned.base + b + 1)
                    if not first:
                        a.wait_ge(projected.sem, projected.base + b)
                    a.activation(oT[:, :], oT_ps, ACT.Copy).then_inc(oT_out.sem, 1)

                def step(b, p, place):
                    if place > 0 and project:
                        take_oT(b - 1, place == 1)
                    for g in range(0, G, 2):
                        if place < B - 1:
                            exponent(b + 1, 1 - p, g)
                        evacuate(b, g + 1, place == 0)
                        if place < B - 1:
                            exponent(b + 1, 1 - p, g + 1)

                a.activation(k.prime[:, :], k.ones[:, 0:1], ACT.Exp)
                for g in range(G):
                    exponent(0, 0, g)
                over_batches(a, step)
                if project:
                    take_oT(B - 1, False)
    for s in slot_in:
        s.base += 16 * B // 2
    scored.base += NH * B
    top.base += NH * B
    for s in (minus, expd, turned, pv):
        s.base += G * B
    for s in (evac_even, evac_odd):
        s.base += G // 2 * B
    for s in (recip, normed, res):
        s.base += B
    if select:
        times.base += G * B
        zeroed.base += G * B
    if project:
        for s in (oturned, oT_out, projected):
            s.base += B


def cross_attention(k, a):
    layer_norm(k, lambda b: k.x[:, b, :], k.xn, k.xnT)
    cross_projections(k, a)
    attention(k, a, k.x, lambda b, h: k.v1[:, b, a, h, :], lambda n: k.wo[:, a, :],
              k.bo[0:1, a, :] if a < 3 else None)



def shift_tokens(k, y, hT):
    nc, ps = k.nc, k.ps
    turned, out = k.count("sh_turned"), k.count("sh_out")
    with nc.Block() as block:
        @block.tensor
        def _(t):
            for b in range(B):
                t.transpose(ps[:, b // HB, P * (b % HB):P * (b % HB) + P], y[:, b, :],
                            k.ident[:, :]).then_inc(turned.sem, 1)

        @block.scalar
        def _(a):
            for h in range(2):
                a.wait_ge(turned.sem, turned.base + HB * (h + 1))
                dst = hT[:, h * HALF:(h + 1) * HALF].rearrange("p (b t) -> p b t", b=HB)
                src = ps[:, h, :].rearrange("p (b t) -> p b t", b=HB)
                a.activation(dst[0:P // 2], src[0:P // 2], ACT.Copy).then_inc(out.sem, 1)
                a.activation(dst[P // 2:P, :, 1:P], src[P // 2:P, :, 0:P - 1], ACT.Copy).then_inc(out.sem, 1)
    turned.base += B
    out.base += 4


def local_qkv(k, hT, wqkv, v2, tab_a, tab_b):
    nc, ps = k.nc, k.ps
    slot_in = [k.count("lq_slot0_in"), k.count("lq_slot1_in")]
    made, raw_out, v_out, squared, rotated, summed, rstd, added, scaled, turned, out = (
        k.count("lq_" + n) for n in ("made", "raw_out", "v_out", "squared", "rotated", "summed", "rstd",
                                     "added", "scaled", "turned", "out"))
    with ExitStack() as own:
        def sb(name, shape):
            return k.fresh(own, name, shape)
        hs, raw, sq = sb("hs", [P, 2, P]), sb("raw", [P, 2, 2, LH, LD]), sb("sq", [P, 2, 2, LH, LD])
        t1, t2 = sb("t1", [P, 2, 2, LH, LD]), sb("t2", [P, 2, 2, LH, LD])
        ss, ssm, rn = sb("ss", [P, 2, 2 * LH]), sb("ssm", [P, 2, 2 * LH]), sb("rn", [P, 2, 2 * LH])
        half = LD // 2
        with nc.Block() as block:
            @block.sync
            def _(sp):
                hb = hT[:, :].rearrange("p (b t) -> p b t", b=B)
                sp.dma_start(hs[:, 0], hb[:, 0]).then_inc(slot_in[0].sem, 16)
                sp.dma_start(hs[:, 1], hb[:, 1]).then_inc(slot_in[1].sem, 16)
                with sp.Fori(0, (B - 2) // 2) as i:
                    for p in range(2):
                        sp.wait_ge(made.sem, made.base + 3 * (2 * i + p + 1))
                        sp.dma_start(hs[:, p], hb[:, 2 * i + 2 + p]).then_inc(slot_in[p].sem, 16)

            @block.tensor
            def _(t):
                def qkv(b, p, early):
                    t.wait_ge(slot_in[p].sem, slot_in[p].base + 8 * (b - p) + 16)
                    if not early:
                        t.wait_ge(v_out.sem, v_out.base + b - 1)
                    for n in range(3):
                        t.matmul(ps[:, 3 * p + n, :], hs[:, p, :], wqkv[:, n, :],
                                 start=True, stop=True).then_inc(made.sem, 1)

                def turn(b, p, first):
                    t.wait_ge(scaled.sem, scaled.base + b + 1)
                    if not first:
                        t.wait_ge(out.sem, out.base + 2 * b)
                    for w in range(2):
                        for c in range(4):
                            m = t.transpose(ps[:, 6 + w, c * P:(c + 1) * P], t1[:, p, w, 2 * c:2 * c + 2, :]
                                            .rearrange("p h e -> p (h e)"), k.ident[:, :])
                        m.then_inc(turned.sem, 1)

                def step(b, p, place):
                    if place < B - 1:
                        qkv(b + 1, 1 - p, place == 0)
                    turn(b, p, place == 0)

                qkv(0, 0, True)
                over_batches(t, step)

            @block.scalar
            def _(a):
                def take(b, p, early):
                    if not early:
                        a.wait_ge(rotated.sem, rotated.base + 3 * (b - 1))
                    for w in range(2):
                        a.wait_ge(made.sem, made.base + 3 * b + w + 1)
                        a.activation(raw[:, p, w], ps[:, 3 * p + w, :].rearrange("p (h e) -> p h e", e=LD),
                                     ACT.Copy).then_inc(raw_out.sem, 1)
                    a.wait_ge(made.sem, made.base + 3 * b + 3)
                    a.activation(v2[:, b, :, 0:LD], ps[:, 3 * p + 2, :].rearrange("p (h e) -> p h e", e=LD),
                                 ACT.Copy).then_inc(v_out.sem, 1)
                    a.wait_ge(raw_out.sem, raw_out.base + 2 * b + 2)
                    if not early:
                        a.wait_ge(summed.sem, summed.base + 2 * (b - 1))
                    a.activation(sq[:, p], raw[:, p], ACT.Square).then_inc(squared.sem, 1)

                def give(b):
                    for w in range(2):
                        a.wait_ge(turned.sem, turned.base + 2 * b + w + 1)
                        a.activation(k.qkT[:, b, w], ps[:, 6 + w, :].rearrange("p (c t) -> p c t", c=4),
                                     ACT.Copy).then_inc(out.sem, 1)

                def step(b, p, place):
                    if place < B - 1:
                        take(b + 1, 1 - p, place == 0)
                    give(b)

                a.activation(k.prime[:, :], k.ones[:, 0:1], ACT.Exp)
                take(0, 0, True)
                over_batches(a, step)

            @block.vector
            def _(v):
                def rotate(b, p, early):
                    v.wait_ge(raw_out.sem, raw_out.base + 2 * b + 2)
                    if not early:
                        v.wait_ge(turned.sem, turned.base + 2 * (b - 1))
                    def each(tab, lo):
                        return tab[:, :, lo:lo + half].unsqueeze(2).to_broadcast([P, 2, LH, half])
                    v.tensor_tensor(t1[:, p], raw[:, p], tab_a[:, :, :].unsqueeze(2)
                                    .to_broadcast([P, 2, LH, LD]), ALU.mult).then_inc(rotated.sem, 1)
                    v.tensor_tensor(t2[:, p, :, :, 0:half], raw[:, p, :, :, half:LD], each(tab_b, 0),
                                    ALU.mult).then_inc(rotated.sem, 1)
                    v.tensor_tensor(t2[:, p, :, :, half:LD], raw[:, p, :, :, 0:half], each(tab_b, half),
                                    ALU.mult).then_inc(rotated.sem, 1)
                    v.wait_ge(squared.sem, squared.base + b + 1)
                    v.tensor_reduce(ss[:, p, :], sq[:, p].rearrange("p w h e -> p (w h) e"), AX.X, ALU.add)\
                     .then_inc(summed.sem, 1)
                    v.wait_ge(summed.sem, summed.base + 2 * b + 1)
                    v.tensor_scalar(ssm[:, p, :], ss[:, p, :], 1e-24, None, ALU.max).then_inc(summed.sem, 1)

                def step(b, p, place):
                    if place < B - 1:
                        rotate(b + 1, 1 - p, place == 0)

                rotate(0, 0, True)
                over_batches(v, step)

            @block.gpsimd
            def _(g):
                def scale(b, p):
                    g.wait_ge(rotated.sem, rotated.base + 3 * b + 3)
                    g.tensor_tensor(t1[:, p], t1[:, p], t2[:, p], ALU.add).then_inc(added.sem, 1)
                    g.wait_ge(summed.sem, summed.base + 2 * b + 2)
                    g.tensor_tensor(rn[:, p, :], ssm[:, p, :], k.mhalf[:, :], ALU.pow).then_inc(rstd.sem, 1)
                    g.wait_ge(added.sem, added.base + b + 1)
                    g.wait_ge(rstd.sem, rstd.base + b + 1)
                    g.tensor_tensor(t1[:, p].rearrange("p w h e -> p (w h) e"),
                                    t1[:, p].rearrange("p w h e -> p (w h) e"), spread(rn[:, p, :], LD),
                                    ALU.mult).then_inc(scaled.sem, 1)

                def step(b, p, place):
                    if place < B - 1:
                        scale(b + 1, 1 - p)

                scale(0, 0)
                over_batches(g, step)
    for s in slot_in:
        s.base += 16 * B // 2
    for s, n in ((made, 3), (raw_out, 2), (v_out, 1), (squared, 1), (rotated, 3), (summed, 2), (rstd, 1),
                 (added, 1), (scaled, 1), (turned, 2), (out, 2)):
        s.base += n * B


def gated_ffn(k, y, hT, w1, b1, w2, b2):
    nc, ps = k.nc, k.ps
    made, gelud, gated, out, res = (k.count("gf_" + n) for n in ("made", "gelud", "gated", "out", "res"))
    NC = len(HCH)
    units = [(h, c) for h in range(2) for c in range(NC)]
    with ExitStack() as own:
        gl = k.fresh(own, "gl", [P, 2, HALF])
        uT = k.fresh(own, "uT", [P, 2, NC, HALF])
        with nc.Block() as block:
            @block.tensor
            def _(t):
                def up(n):
                    h, c = units[n]
                    o, m = HCH[c]
                    if n >= 2:
                        t.wait_ge(gated.sem, gated.base + n - 1)
                    for w in range(2):
                        t.matmul(ps[0:m, 2 * (n % 2) + w, :], w1[:, w * HID + o:w * HID + o + m],
                                 hT[:, h * HALF:(h + 1) * HALF], start=True, stop=True)\
                         .then_inc(made.sem, 1)

                def down(h):
                    t.wait_ge(gated.sem, gated.base + NC * (h + 1))
                    for b in range(HB):
                        o = ps[:, 4 + h, b * P:(b + 1) * P]
                        for c, (_, m) in enumerate(HCH):
                            t.matmul(o, uT[0:m, h, c, b * P:(b + 1) * P], w2[0:m, c, :],
                                     start=(c == 0), stop=False)
                        x = t.matmul(o, k.ones[0:1, 0:P], b2, start=False, stop=True)
                    x.then_inc(out.sem, 1)

                for n in range(NC + 1):
                    up(n)
                down(0)
                for n in range(NC + 1, 2 * NC):
                    up(n)
                down(1)

            @block.scalar
            def _(a):
                for n, (h, c) in enumerate(units):
                    m = HCH[c][1]
                    a.wait_ge(made.sem, made.base + 2 * n + 2)
                    if n >= 2:
                        a.wait_ge(gated.sem, gated.base + n - 1)
                    a.activation(gl[0:m, n % 2, :], ps[0:m, 2 * (n % 2) + 1, :], ACT.Gelu,
                                 bias=b1[0:m, 1, c:c + 1]).then_inc(gelud.sem, 1)

            @block.vector
            def _(v):
                def residual(h):
                    v.wait_ge(out.sem, out.base + h + 1)
                    v.tensor_tensor(y[:, HB * h:HB * h + HB, :], y[:, HB * h:HB * h + HB, :],
                                    ps[:, 4 + h, :].rearrange("p (b c) -> p b c", b=HB), ALU.add)\
                     .then_inc(res.sem, 1)
                for n, (h, c) in enumerate(units):
                    m = HCH[c][1]
                    v.wait_ge(gelud.sem, gelud.base + n + 1)
                    v.scalar_tensor_tensor(out=uT[0:m, h, c, :], in0=ps[0:m, 2 * (n % 2), :],
                                           scalar=b1[0:m, 0, c:c + 1], in1=gl[0:m, n % 2, :],
                                           op0=ALU.add, op1=ALU.mult).then_inc(gated.sem, 1)
                residual(0)
                residual(1)
    made.base += 4 * NC
    gelud.base += 2 * NC
    gated.base += 2 * NC
    out.base += 2
    res.base += 2


def local_transformer(k, d):
    nc, ps = k.nc, k.ps
    load, made, tabs = k.count("lt_load"), k.count("lt_made"), k.count("lt_tabs")
    with ExitStack() as own:
        def sb(name, shape):
            return k.fresh(own, name, shape)
        y = k.xn
        hT, v2, htok, hnT = sb("hT", [P, T]), sb("v2", [P, B, LH, LD + 1]), sb("htok", [P, B, P]), k.xnT
        wqkv, wo = sb("wqkv", [P, LAYERS, 3, LH * LD]), sb("lwo", [P, LAYERS, 4, P])
        w1, w2 = sb("w1", [P, LAYERS, 2 * HID]), sb("w2", [P, LAYERS, len(HCH), P])
        b1, b2 = sb("b1", [P, LAYERS, 2, len(HCH)]), sb("b2", [1, LAYERS, P])
        gb, qks = sb("gb", [P, LAYERS, 2]), sb("qks", [P, LAYERS, 2, LD])
        rotc, rots = sb("rotc", [P, 2, LD]), sb("rots", [P, 2, LD])
        tab_a, tab_b = sb("tab_a", [P, LAYERS, 2, LD]), sb("tab_b", [P, LAYERS, 2, LD])
        half = LD // 2
        with nc.Block() as block:
            @block.sync
            def _(sp):
                for dst, src in ((wqkv, "wqkv"), (wo, "lwo"), (w1, "w1"), (w2, "w2"), (b1, "b1"), (b2, "b2"),
                                 (gb, "gb"), (rotc, "rotc"), (rots, "rots")):
                    sp.dma_start(dst[:], d[src]).then_inc(load.sem, 16)
                sp.dma_start(qks[:, :, :, :], d["qks"].to_broadcast([P, LAYERS, 2, LD])).then_inc(load.sem, 16)
                sp.wait_ge(load.sem, load.base + 160)

            @block.gpsimd
            def _(g):
                g.memset(v2[:, :, :, LD:LD + 1], 1.0).then_inc(made.sem, 1)

            @block.vector
            def _(v):
                v.memset(hT[P // 2:P, :].rearrange("p (b t) -> p b t", b=B)[:, :, 0:1], 0.0)
                v.wait_ge(load.sem, load.base + 160)
                for l in range(LAYERS):
                    v.tensor_tensor(tab_a[:, l], rotc[:, :, :], qks[:, l], ALU.mult)
                    v.tensor_tensor(tab_b[:, l, :, 0:half], rots[:, :, 0:half], qks[:, l, :, half:LD], ALU.mult)
                    v.tensor_tensor(tab_b[:, l, :, half:LD], rots[:, :, half:LD], qks[:, l, :, 0:half], ALU.mult)
        layer_norm(k, lambda b: k.x[:, b, :], k.xn, k.xnT)
        for l in range(LAYERS):
            shift_tokens(k, y, hT)
            local_qkv(k, hT, wqkv[:, l], v2, tab_a[:, l], tab_b[:, l])
            attention(k, "local", y, lambda b, h: v2[:, b, h, :], lambda n: wo[:, l, n, :])
            shift_tokens(k, y, hT)
            turn_back(k, hT)
            layer_norm(k, lambda b: ps[:, 2 + b // HB, P * (b % HB):P * (b % HB) + P], htok, hnT,
                       gb[:, l, 0:1], gb[:, l, 1:2])
            gated_ffn(k, y, hnT, w1[:, l], b1[:, l], w2[:, l], b2[:, l])
        add_stream(k, y)


def turn_back(k, hT):
    with k.nc.Block() as block:
        @block.tensor
        def _(t):
            for b in range(B):
                t.transpose(k.ps[:, 2 + b // HB, P * (b % HB):P * (b % HB) + P], hT[:, b * P:(b + 1) * P],
                            k.ident[:, :])


def add_stream(k, y):
    with k.nc.Block() as block:
        @block.vector
        def _(v):
            v.tensor_tensor(k.x[:, :, :], k.x[:, :, :], y[:, :, :], ALU.add)


def route(v, done, vals, iota, top, at, first, hot):
    n, e = vals.shape[1], vals.shape[2]
    places = iota.unsqueeze(1).to_broadcast([P, n, e])

    def then(m):
        m.then_inc(done.sem, 1)
        done.base += 1
        v.wait_ge(done.sem, done.base)

    then(v.tensor_reduce(top, vals, AX.X, ALU.max))
    then(v.tensor_tensor(at, vals, spread(top, e), ALU.is_equal))
    then(v.scalar_tensor_tensor(out=at, in0=at, scalar=-64.0, in1=places, op0=ALU.mult, op1=ALU.add))
    then(v.tensor_reduce(first, at, AX.X, ALU.min))
    then(v.tensor_tensor(hot, at, spread(first, e), ALU.is_equal))


def top1_experts(k, d):
    nc, ps = k.nc, k.ps
    load, own_step, scored, routed, turned, hot_out, b2_made, alpha_out = (k.count("t1_" + n) for n in (
        "load", "own_step", "scored", "routed", "turned", "hot_out", "b2_made", "alpha"))
    w_in = [k.count("t1_w0_in"), k.count("t1_w1_in")]
    hx, up, relu_a, relu_v, down, summed = (k.count("t1_" + n) for n in (
        "hx", "up", "relu_a", "relu_v", "down", "summed"))
    layer_norm(k, lambda b: k.x[:, b, :], k.xn, k.xnT)
    with ExitStack() as own:
        def sb(name, shape):
            return k.fresh(own, name, shape)
        zn, zT, acc = sb("zn", [P, B, P]), sb("zT", [P, T]), sb("acc", [P, B, P])
        cent, iota, b2 = sb("cent", [P, E1]), sb("iota1", [P, E1]), sb("t1b2", [E1, P])
        sc, at, hot = sb("sc", [P, B, E1]), sb("at", [P, B, E1]), sb("hot", [P, B, E1])
        top, first, alpha = sb("top", [P, B]), sb("first", [P, B]), sb("alpha", [P, B])
        hotT = sb("hotT", [E1, T])
        w1, w2, eb = sb("w1s", [P, 2, F1]), sb("w2s", [P, 2, FC1, P]), sb("ebs", [P, 2, 2 + FC1])
        hT, r1 = sb("h1T", [P, 2, T]), sb("r1", [P, 2, FC1, HALF])
        layer_norm(k, lambda b: k.xn[:, b, :], zn, zT)
        with nc.Block() as block:
            @block.sync
            def _(sp):
                sp.dma_start(cent[:, :], d["cent"]).then_inc(load.sem, 16)
                sp.dma_start(iota[:, :], d["iota"][:, 0:E1].to_broadcast([P, E1])).then_inc(load.sem, 16)
                sp.dma_start(b2[:, :], d["t1b2"]).then_inc(load.sem, 16)

            @block.tensor
            def _(t):
                t.wait_ge(load.sem, 48)
                for b in range(B):
                    m = t.matmul(ps[:, 0, b * E1:(b + 1) * E1], k.xnT[:, b * P:(b + 1) * P], cent[:, :],
                                 start=True, stop=True)
                m.then_inc(scored.sem, 1)
                t.wait_ge(routed.sem, 1)
                for b in range(B):
                    t.transpose(ps[0:E1, 1 + b // HB, P * (b % HB):P * (b % HB) + P], hot[:, b, :],
                                k.ident[:, :]).then_inc(turned.sem, 1)
                t.wait_ge(hot_out.sem, 2)
                for b in range(B):
                    t.matmul(ps[:, 4 + b // HB, P * (b % HB):P * (b % HB) + P], hotT[:, b * P:(b + 1) * P],
                             b2[:, :], start=True, stop=True).then_inc(b2_made.sem, 1)

            @block.vector
            def _(v):
                v.wait_ge(scored.sem, 1)
                v.tensor_copy(sc[:, :, :], ps[:, 0, 0:B * E1].rearrange("p (b e) -> p b e", b=B))\
                 .then_inc(own_step.sem, 1)
                own_step.base += 1
                v.wait_ge(own_step.sem, own_step.base)
                v.wait_ge(load.sem, 48)
                route(v, own_step, sc[:, :, :], iota[:, :], top[:, :], at[:, :, :], first[:, :], hot[:, :, :])
                v.memset(k.prime2[:, :], 0.0).then_inc(routed.sem, 1)
                for h in range(2):
                    v.wait_ge(b2_made.sem, HB * (h + 1))
                    v.tensor_copy(acc[:, HB * h:HB * h + HB, :],
                                  ps[:, 4 + h, :].rearrange("p (b c) -> p b c", b=HB))

            @block.scalar
            def _(a):
                a.wait_ge(routed.sem, 1)
                a.activation(alpha[:, :], top[:, :], ACT.Sigmoid).then_inc(alpha_out.sem, 1)
                for h in range(2):
                    a.wait_ge(turned.sem, HB * (h + 1))
                    a.activation(hotT[:, h * HALF:(h + 1) * HALF], ps[0:E1, 1 + h, :], ACT.Copy)\
                     .then_inc(hot_out.sem, 1)

        with nc.Block() as block:
            @block.sync
            def _(sp):
                def fetch(e, p, early):
                    if not early:
                        sp.wait_ge(down.sem, 2 * (e - 1))
                    sp.dma_start(w1[:, p, :], d["t1w1"][e]).then_inc(w_in[p].sem, 16)
                    sp.dma_start(w2[:, p], d["t1w2"][e]).then_inc(w_in[p].sem, 16)
                    sp.dma_start(eb[:, p, :], d["t1eb"][e]).then_inc(w_in[p].sem, 16)
                fetch(0, 0, True)
                fetch(1, 1, True)
                with sp.Fori(0, (E1 - 2) // 2) as i:
                    fetch(2 * i + 2, 0, False)
                    fetch(2 * i + 3, 1, False)

            @block.tensor
            def _(t):
                def step(e, p, place):
                    t.wait_ge(w_in[p].sem, 24 * (e - p) + 48)
                    t.wait_ge(hx.sem, e + 1)
                    for h in range(2):
                        for c in range(FC1):
                            if place > 0 or h > 0:
                                r = relu_v if c % 2 else relu_a
                                t.wait_ge(r.sem, 4 * e + 2 * h + c // 2 - 1)
                            t.matmul(ps[:, c, :], w1[:, p, c * P:(c + 1) * P],
                                     hT[:, p, h * HALF:(h + 1) * HALF], start=True, stop=True)\
                             .then_inc(up.sem, 1)
                    for h in range(2):
                        t.wait_ge(relu_a.sem, 4 * e + 2 * h + 2)
                        t.wait_ge(relu_v.sem, 4 * e + 2 * h + 2)
                        if place > 1:
                            t.wait_ge(summed.sem, 8 * (e - 2) + 4 * h + 4)
                        for b in range(HB):
                            for c in range(FC1):
                                m = t.matmul(ps[:, 4 + 2 * p + h, b * P:(b + 1) * P],
                                             r1[:, h, c, b * P:(b + 1) * P], w2[:, p, c, :],
                                             start=(c == 0), stop=(c == FC1 - 1))
                        m.then_inc(down.sem, 1)
                over_batches(t, step)

            @block.scalar
            def _(a):
                def step(e, p, place):
                    for h in range(2):
                        for c in range(0, FC1, 2):
                            a.wait_ge(up.sem, 8 * e + 4 * h + c + 1)
                            if place > 0 and c == 0:
                                a.wait_ge(down.sem, 2 * (e - 1) + h + 1)
                            a.activation(r1[:, h, c, :], ps[:, c, :], ACT.Relu,
                                         bias=eb[:, p, 2 + c:3 + c]).then_inc(relu_a.sem, 1)
                a.activation(k.prime[:, :], k.ones[:, 0:1], ACT.Exp)
                over_batches(a, step)

            @block.vector
            def _(v):
                def inputs(e, p, early):
                    v.wait_ge(w_in[p].sem, 24 * (e - p) + 48)
                    if not early:
                        v.wait_ge(down.sem, 2 * (e - 1))
                    v.tensor_scalar(hT[:, p, :], zT[:, :], eb[:, p, 0:1], eb[:, p, 1:2], ALU.mult, ALU.add)\
                     .then_inc(hx.sem, 1)

                def step(e, p, place):
                    for h in range(2):
                        for c in range(1, FC1, 2):
                            v.wait_ge(up.sem, 8 * e + 4 * h + c + 1)
                            if place > 0 and c == 1:
                                v.wait_ge(down.sem, 2 * (e - 1) + h + 1)
                            v.tensor_scalar(r1[:, h, c, :], ps[:, c, :], eb[:, p, 2 + c:3 + c], 0.0,
                                            ALU.add, ALU.max).then_inc(relu_v.sem, 1)
                    if place < E1 - 1:
                        inputs(e + 1, 1 - p, place == 0)
                    for h in range(2):
                        v.wait_ge(down.sem, 2 * e + h + 1)
                        for b in range(HB * h, HB * h + HB):
                            if place > 0 and b == 0:
                                v.wait_ge(summed.sem, 8 * e)
                            v.scalar_tensor_tensor(
                                out=acc[:, b, :], in0=ps[:, 4 + 2 * p + h, P * (b % HB):P * (b % HB) + P],
                                scalar=hot[:, b, bass.ds(e, 1)], in1=acc[:, b, :], op0=ALU.mult,
                                op1=ALU.add).then_inc(summed.sem, 1)
                inputs(0, 0, True)
                over_batches(v, step)
        finish_gated(k, acc, alpha)


def finish_gated(k, acc, gate):
    nc = k.nc
    gated = k.count("fg_gated")
    with nc.Block() as block:
        @block.vector
        def _(v):
            for b in range(B):
                v.scalar_tensor_tensor(out=k.xn[:, b, :], in0=acc[:, b, :], scalar=gate[:, b:b + 1],
                                       in1=k.xn[:, b, :], op0=ALU.mult, op1=ALU.add).then_inc(gated.sem, 1)
            v.wait_ge(gated.sem, gated.base + B)
            v.tensor_tensor(k.x[:, :, :], k.x[:, :, :], k.xn[:, :, :], ALU.add)
    gated.base += B


def capacity_experts(k, d):
    nc, ps = k.nc, k.ps
    load, own_step, scored, lessed, expd, routed, counted, diag, rows, rows_out = (k.count("ce_" + n) for n in (
        "load", "own_step", "scored", "lessed", "expd", "routed", "counted", "diag", "rows", "rows_out"))
    iota_made, hot_made, sent = k.count("ce_iota"), k.count("ce_hot"), k.count("ce_sent")
    w_in = [k.count("ce_w0_in"), k.count("ce_w1_in")]
    up, silud, hid_made, down, y_out = (k.count("ce_" + n) for n in ("up", "silud", "hid", "down", "y_out"))
    yturned, y_sb_out, back_made, combined = (k.count("ce_" + n) for n in ("yturned", "y_sb", "back", "combined"))
    layer_norm(k, lambda b: k.x[:, b, :], k.xn, k.xnT)
    GB = (SPAN2 * C2)
    with ExitStack() as own:
        def sb(name, shape, dt=F32, ctx=own):
            return k.fresh(ctx, name, shape, dt)
        gate, slot, slot_row = sb("gate", [P, B]), sb("slot_of", [P, B]), sb("slot_row", [P, T])
        bufT, yT = sb("bufT", [P, SLOTS]), sb("yT", [P, SLOTS])
        mine = sb("mine", [P, SCH])
        with ExitStack() as early:
            rw, iota, tri = sb("rw", [P, E2], ctx=early), sb("iota2", [P, E2], ctx=early), sb("tri", [P, P], ctx=early)
            slots_i, slots_f = sb("slots_i", [P, SLOTS], I32, early), sb("slots_f", [P, SLOTS], ctx=early)
            mine_i = sb("mine_i", [P, SCH], I32, early)
            pr, at, hot = (sb(n, [P, B, E2], ctx=early) for n in ("pr", "at2", "hot2"))
            base, dg = sb("base", [P, B, E2], ctx=early), sb("dg", [P, B, P], ctx=early)
            top, rsum, first, pos, eid, over = (sb(n, [P, B], ctx=early) for n in (
                "top2", "rsum", "first2", "pos", "eid", "over"))
            send = sb("send", [P, B, SLOTS], ctx=early)
            with nc.Block() as block:
                @block.sync
                def _(sp):
                    sp.dma_start(rw[:, :], d["rw"]).then_inc(load.sem, 16)
                    sp.dma_start(iota[:, :], d["iota"].to_broadcast([P, E2])).then_inc(load.sem, 16)

                @block.gpsimd
                def _(g):
                    g.memset(tri[:, :], 1.0).then_inc(iota_made.sem, 1)
                    g.iota(slots_i[:, :], pattern=[[1, SLOTS]], base=0, channel_multiplier=0)\
                     .then_inc(iota_made.sem, 1)
                    g.iota(mine_i[:, :], pattern=[[P, SCH]], base=0, channel_multiplier=1)\
                     .then_inc(iota_made.sem, 1)
                    g.memset(base[:, 0, :], 0.0).then_inc(iota_made.sem, 1)
                    g.wait_ge(iota_made.sem, 4)
                    g.affine_select(out=tri[:, :], in_=tri[:, :], compare_op=ALU.is_gt, fill=0.0, base=0,
                                    pattern=[[1, P]], channel_multiplier=-1).then_inc(iota_made.sem, 1)

                @block.tensor
                def _(t):
                    t.wait_ge(load.sem, 32)
                    for b in range(B):
                        m = t.matmul(ps[:, 0, b * E2:(b + 1) * E2], k.xnT[:, b * P:(b + 1) * P], rw[:, :],
                                     start=True, stop=True)
                    m.then_inc(scored.sem, 1)
                    t.wait_ge(iota_made.sem, 5)
                    t.wait_ge(routed.sem, 1)
                    flat = hot[:, :, :].rearrange("p b e -> p (b e)")
                    t.matmul(ps[:, 1, 0:B * E2], tri[:, :], flat, start=True, stop=True).then_inc(counted.sem, 1)
                    t.matmul(ps[:, 2, 0:B * E2], k.ones[:, 0:P], flat, start=True, stop=True)\
                     .then_inc(counted.sem, 1)
                    for b in range(B):
                        t.wait_ge(diag.sem, b + 1)
                        t.matmul(ps[:, 3 + b // HB, P * (b % HB):P * (b % HB) + P], k.ones[:, 0:P],
                                 dg[:, b, :], start=True, stop=True).then_inc(rows.sem, 1)
                    for n, (lo, hi) in enumerate(((0, 512), (512, 1024), (1024, SLOTS))):
                        for b in range(B):
                            t.wait_ge(hot_made.sem, b + 1)
                            m = t.matmul(ps[:, 5 + n, 0:hi - lo], k.xn[:, b, :], send[:, b, lo:hi],
                                         start=(b == 0), stop=(b == B - 1))
                        m.then_inc(sent.sem, 1)

                @block.scalar
                def _(a):
                    a.wait_ge(lessed.sem, 1)
                    a.activation(pr[:, :, :], pr[:, :, :], ACT.Exp).then_inc(expd.sem, 1)
                    for h in range(2):
                        a.wait_ge(rows.sem, HB * (h + 1))
                        a.activation(slot_row[:, h * HALF:(h + 1) * HALF], ps[:, 3 + h, :], ACT.Copy)\
                         .then_inc(rows_out.sem, 1)
                    for n, (lo, hi) in enumerate(((0, 512), (512, 1024), (1024, SLOTS))):
                        a.wait_ge(sent.sem, n + 1)
                        a.activation(bufT[:, lo:hi], ps[:, 5 + n, 0:hi - lo], ACT.Copy)

                @block.vector
                def _(v):
                    def then(m):
                        m.then_inc(own_step.sem, 1)
                        own_step.base += 1
                        v.wait_ge(own_step.sem, own_step.base)
                    v.wait_ge(iota_made.sem, 4)
                    v.tensor_copy(slots_f[:, :], slots_i[:, :])
                    v.tensor_copy(mine[:, :], mine_i[:, :])
                    v.wait_ge(scored.sem, 1)
                    then(v.tensor_reduce(top[:, :], ps[:, 0, 0:B * E2].rearrange("p (b e) -> p b e", b=B),
                                         AX.X, ALU.max))
                    v.tensor_tensor(pr[:, :, :], ps[:, 0, 0:B * E2].rearrange("p (b e) -> p b e", b=B),
                                    spread(top[:, :], E2), ALU.subtract).then_inc(lessed.sem, 1)
                    v.wait_ge(expd.sem, 1)
                    then(v.tensor_reduce(rsum[:, :], pr[:, :, :], AX.X, ALU.add))
                    then(v.reciprocal(rsum[:, :], rsum[:, :]))
                    then(v.tensor_tensor(pr[:, :, :], pr[:, :, :], spread(rsum[:, :], E2), ALU.mult))
                    v.wait_ge(load.sem, 32)
                    route(v, own_step, pr[:, :, :], iota[:, :], gate[:, :], at[:, :, :], first[:, :],
                          hot[:, :, :])
                    v.memset(k.prime2[:, :], 0.0).then_inc(routed.sem, 1)
                    v.wait_ge(counted.sem, 2)
                    for b in range(1, B):
                        then(v.tensor_tensor(base[:, b, :], base[:, b - 1, :],
                                             ps[:, 2, (b - 1) * E2:b * E2], ALU.add))
                    then(v.tensor_tensor(base[:, :, :], base[:, :, :],
                                         ps[:, 1, 0:B * E2].rearrange("p (b e) -> p b e", b=B), ALU.add))
                    then(v.tensor_tensor(base[:, :, :], base[:, :, :], hot[:, :, :], ALU.mult))
                    then(v.tensor_reduce(pos[:, :], base[:, :, :], AX.X, ALU.add))
                    then(v.tensor_scalar(eid[:, :], first[:, :], 64.0, float(C2), ALU.add, ALU.mult))
                    then(v.tensor_scalar(over[:, :], pos[:, :], float(C2), 4.0 * SLOTS, ALU.is_ge, ALU.mult))
                    then(v.tensor_tensor(slot[:, :], pos[:, :], eid[:, :], ALU.add))
                    then(v.tensor_tensor(slot[:, :], slot[:, :], over[:, :], ALU.add))
                    for b in range(B):
                        v.tensor_scalar(dg[:, b, :], k.ident[:, :], slot[:, b:b + 1], None, ALU.mult)\
                         .then_inc(diag.sem, 1)
                    for b in range(B):
                        v.tensor_scalar(send[:, b, :], slots_f[:, :], slot[:, b:b + 1], None, ALU.is_equal)\
                         .then_inc(hot_made.sem, 1)

        back = sb("back", [P, SCH, T])
        w = sb("w2x", [P, 2, 3, SPAN2, P])
        sg, hid = sb("sg", [P, 2, GB]), sb("hid", [P, 2, GB])
        ysl = sb("ysl", [P, SCH, P])
        with nc.Block() as block:
            @block.sync
            def _(sp):
                def fetch(s, p, early):
                    if not early:
                        sp.wait_ge(down.sem, s - 1)
                    sp.dma_start(w[:, p], d["w2x"][s]).then_inc(w_in[p].sem, 16)
                fetch(0, 0, True)
                fetch(1, 1, True)
                with sp.Fori(0, (B - 2) // 2) as i:
                    fetch(2 * i + 2, 0, False)
                    fetch(2 * i + 3, 1, False)

            @block.tensor
            def _(t):
                def ups(s, p, early):
                    t.wait_ge(w_in[p].sem, 8 * (s - p) + 16)
                    if not early:
                        t.wait_ge(hid_made.sem, s - 1)
                    for q in range(SPAN2):
                        for n in range(2):
                            t.matmul(ps[:, 2 * p + n, q * C2:(q + 1) * C2], w[:, p, n, q, :],
                                     bufT[:, bass.ds(s * GB + q * C2, C2)], start=True, stop=True)\
                             .then_inc(up.sem, 1)

                def downs(s, p, place):
                    t.wait_ge(hid_made.sem, s + 1)
                    if place > 1:
                        t.wait_ge(y_out.sem, s - 1)
                    for q in range(SPAN2):
                        m = t.matmul(ps[:, 4 + p, q * C2:(q + 1) * C2], w[:, p, 2, q, :],
                                     hid[:, p, q * C2:(q + 1) * C2], start=True, stop=True)
                    m.then_inc(down.sem, 1)

                def step(s, p, place):
                    if place < B - 1:
                        ups(s + 1, 1 - p, place == 0)
                    downs(s, p, place)
                ups(0, 0, True)
                over_batches(t, step)

            @block.scalar
            def _(a):
                def silu(s, p):
                    a.wait_ge(up.sem, 2 * SPAN2 * (s + 1))
                    a.activation(sg[:, p, :], ps[:, 2 * p, 0:GB], ACT.Silu).then_inc(silud.sem, 1)

                def step(s, p, place):
                    if place < B - 1:
                        silu(s + 1, 1 - p)
                    a.wait_ge(down.sem, s + 1)
                    a.activation(yT[:, bass.ds(s * GB, GB)], ps[:, 4 + p, 0:GB], ACT.Copy).then_inc(y_out.sem, 1)
                a.activation(k.prime[:, :], k.ones[:, 0:1], ACT.Silu)
                silu(0, 0)
                over_batches(a, step)

            @block.vector
            def _(v):
                def step(s, p, place):
                    v.wait_ge(silud.sem, s + 1)
                    if place > 1:
                        v.wait_ge(down.sem, s - 1)
                    v.tensor_tensor(hid[:, p, :], sg[:, p, :], ps[:, 2 * p + 1, 0:GB], ALU.mult)\
                     .then_inc(hid_made.sem, 1)
                over_batches(v, step)
                for c in range(SCH):
                    v.tensor_scalar(back[:, c, :], slot_row[:, :], mine[:, c:c + 1], None, ALU.is_equal)

        with nc.Block() as block:
            @block.tensor
            def _(t):
                for c in range(SCH):
                    t.transpose(ps[:, c // 4, P * (c % 4):P * (c % 4) + P], yT[:, c * P:(c + 1) * P],
                                k.ident[:, :]).then_inc(yturned.sem, 1)
                t.wait_ge(y_sb_out.sem, 3)
                for b in range(B):
                    for c in range(SCH):
                        m = t.matmul(ps[:, 4 + b // 2, P * (b % 2):P * (b % 2) + P],
                                     back[:, c, b * P:(b + 1) * P], ysl[:, c, :],
                                     start=(c == 0), stop=(c == SCH - 1))
                    m.then_inc(back_made.sem, 1)

            @block.scalar
            def _(a):
                for n, (lo, hi) in enumerate(((0, 4), (4, 8), (8, SCH))):
                    a.wait_ge(yturned.sem, hi)
                    a.activation(ysl[:, lo:hi, :], ps[:, n, 0:(hi - lo) * P].rearrange("p (c h) -> p c h", h=P),
                                 ACT.Copy).then_inc(y_sb_out.sem, 1)

            @block.vector
            def _(v):
                for b in range(B):
                    v.wait_ge(back_made.sem, 2 * (b // 2) + 2)
                    v.scalar_tensor_tensor(out=k.xn[:, b, :], in0=ps[:, 4 + b // 2, P * (b % 2):P * (b % 2) + P],
                                           scalar=gate[:, b:b + 1], in1=k.xn[:, b, :], op0=ALU.mult,
                                           op1=ALU.add).then_inc(combined.sem, 1)
                    v.wait_ge(combined.sem, b + 1)
                    v.tensor_tensor(k.x[:, b, :], k.x[:, b, :], k.xn[:, b, :], ALU.add)


def top2_experts(k, d):
    nc, ps = k.nc, k.ps
    load, own_step, scored, sig, routed, cturned, cT_out, mixed, up, silud, hid_made, out = (
        k.count("t2_" + n) for n in ("load", "own_step", "scored", "sig", "routed", "cturned", "cT_out",
                                     "mixed", "up", "silud", "hid", "out"))
    layer_norm(k, lambda b: k.x[:, b, :], k.xn, k.xnT)
    units = [(h, c) for h in range(2) for c in range(CH3)]
    with ExitStack() as own:
        def sb(name, shape):
            return k.fresh(own, name, shape)
        gw, iota, sel = sb("gw", [P, E3]), sb("iota3", [P, E3]), sb("sel", [E3, CH3 - 1, P])
        wg, wu, wd = (sb(n, [P, CH3, P]) for n in ("wg3", "wu3", "wd3"))
        sc, at, hot1, hot2, mix = (sb(n, [P, B, E3]) for n in ("sc3", "at3", "hot31", "hot32", "mix"))
        top1, top2, first, tot = (sb(n, [P, B]) for n in ("top31", "top32", "first3", "tot"))
        cT, sg, uu, hid = sb("cT", [E3, T]), sb("sg3", [P, 2, HALF]), sb("uu", [P, 2, HALF]), \
            sb("hid3", [P, 2, CH3, HALF])
        with nc.Block() as block:
            @block.sync
            def _(sp):
                for dst, src in ((gw, "gw"), (sel, "sel"), (wg, "wg3"), (wu, "wu3"), (wd, "wd3")):
                    sp.dma_start(dst[:], d[src]).then_inc(load.sem, 16)
                sp.dma_start(iota[:, :], d["iota"][:, 0:E3].to_broadcast([P, E3])).then_inc(load.sem, 16)

            @block.tensor
            def _(t):
                t.wait_ge(load.sem, 96)
                for b in range(B):
                    m = t.matmul(ps[:, 0, b * E3:(b + 1) * E3], k.xnT[:, b * P:(b + 1) * P], gw[:, :],
                                 start=True, stop=True)
                m.then_inc(scored.sem, 1)
                t.wait_ge(routed.sem, 1)
                for b in range(B):
                    t.transpose(ps[0:E3, 1 + b // HB, P * (b % HB):P * (b % HB) + P], mix[:, b, :],
                                k.ident[:, :]).then_inc(cturned.sem, 1)

            @block.scalar
            def _(a):
                a.wait_ge(scored.sem, 1)
                a.activation(sc[:, :, :], ps[:, 0, 0:B * E3].rearrange("p (b e) -> p b e", b=B), ACT.Sigmoid)\
                 .then_inc(sig.sem, 1)
                for h in range(2):
                    a.wait_ge(cturned.sem, HB * (h + 1))
                    a.activation(cT[:, h * HALF:(h + 1) * HALF], ps[0:E3, 1 + h, :], ACT.Copy)\
                     .then_inc(cT_out.sem, 1)

            @block.vector
            def _(v):
                def then(m):
                    m.then_inc(own_step.sem, 1)
                    own_step.base += 1
                    v.wait_ge(own_step.sem, own_step.base)
                v.wait_ge(load.sem, 96)
                v.wait_ge(sig.sem, 1)
                route(v, own_step, sc[:, :, :], iota[:, :], top1[:, :], at[:, :, :], first[:, :], hot1[:, :, :])
                then(v.scalar_tensor_tensor(out=sc[:, :, :], in0=hot1[:, :, :], scalar=-4.0, in1=sc[:, :, :],
                                            op0=ALU.mult, op1=ALU.add))
                route(v, own_step, sc[:, :, :], iota[:, :], top2[:, :], at[:, :, :], first[:, :], hot2[:, :, :])
                then(v.tensor_tensor(tot[:, :], top1[:, :], top2[:, :], ALU.add))
                then(v.tensor_scalar(tot[:, :], tot[:, :], 1e-20, None, ALU.add))
                then(v.reciprocal(tot[:, :], tot[:, :]))
                then(v.tensor_tensor(hot1[:, :, :], hot1[:, :, :], spread(top1[:, :], E3), ALU.mult))
                then(v.tensor_tensor(hot2[:, :, :], hot2[:, :, :], spread(top2[:, :], E3), ALU.mult))
                then(v.tensor_tensor(mix[:, :, :], hot1[:, :, :], hot2[:, :, :], ALU.add))
                then(v.tensor_scalar(tot[:, :], tot[:, :], ROUTED_SCALE, None, ALU.mult))
                v.tensor_tensor(mix[:, :, :], mix[:, :, :], spread(tot[:, :], E3), ALU.mult)\
                 .then_inc(routed.sem, 1)

        with nc.Block() as block:
            @block.tensor
            def _(t):
                def ups(n):
                    h, c = units[n]
                    if n >= 2:
                        t.wait_ge(hid_made.sem, n - 1)
                    cols = slice(h * HALF, (h + 1) * HALF)
                    bank = 3 * (n % 2)
                    t.matmul(ps[:, bank, :], wg[:, c, :], k.xnT[:, cols], start=True, stop=True)\
                     .then_inc(up.sem, 1)
                    m = t.matmul(ps[:, bank + 1, :], wu[:, c, :], k.xnT[:, cols], start=True, stop=True)
                    if c < CH3 - 1:
                        m = t.matmul(ps[:, bank + 2, :], sel[:, c, :], cT[:, cols], start=True, stop=True)
                    m.then_inc(up.sem, 1)

                def downs(h):
                    t.wait_ge(hid_made.sem, CH3 * (h + 1))
                    for b in range(HB):
                        for c in range(CH3):
                            m = t.matmul(ps[:, 6 + h, b * P:(b + 1) * P], hid[:, h, c, b * P:(b + 1) * P],
                                         wd[:, c, :], start=(c == 0), stop=(c == CH3 - 1))
                    m.then_inc(out.sem, 1)
                for n in range(CH3 + 1):
                    ups(n)
                downs(0)
                for n in range(CH3 + 1, 2 * CH3):
                    ups(n)
                downs(1)

            @block.scalar
            def _(a):
                for n in range(2 * CH3):
                    a.wait_ge(up.sem, 2 * n + 1)
                    if n >= 2:
                        a.wait_ge(mixed.sem, n - 1)
                    a.activation(sg[:, n % 2, :], ps[:, 3 * (n % 2), :], ACT.Silu).then_inc(silud.sem, 1)

            @block.vector
            def _(v):
                for n, (h, c) in enumerate(units):
                    v.wait_ge(silud.sem, n + 1)
                    v.wait_ge(up.sem, 2 * n + 2)
                    bank = 3 * (n % 2)
                    if c < CH3 - 1:
                        v.tensor_tensor(uu[:, n % 2, :], sg[:, n % 2, :], ps[:, bank + 1, :], ALU.mult)\
                         .then_inc(mixed.sem, 1)
                        v.wait_ge(mixed.sem, n + 1)
                        v.tensor_tensor(hid[:, h, c, :], uu[:, n % 2, :], ps[:, bank + 2, :], ALU.mult)\
                         .then_inc(hid_made.sem, 1)
                    else:
                        v.tensor_tensor(hid[:, h, c, :], sg[:, n % 2, :], ps[:, bank + 1, :], ALU.mult)\
                         .then_inc(hid_made.sem, 1)
                        v.memset(k.prime2[:, :], 0.0).then_inc(mixed.sem, 1)
                for h in range(2):
                    v.wait_ge(out.sem, h + 1)
                    v.tensor_tensor(k.x[:, HB * h:HB * h + HB, :], k.x[:, HB * h:HB * h + HB, :],
                                    ps[:, 6 + h, :].rearrange("p (b c) -> p b c", b=HB), ALU.add)


def store(k, out):
    done = k.count("stored")
    with k.nc.Block() as block:
        @block.sync
        def _(sp):
            sp.dma_start(out.rearrange("b t d -> t b d"), k.x[:, :, :]).then_inc(done.sem, 16)
            sp.wait_ge(done.sem, 16)


def build(nc, d, out, stages=8):
    with ExitStack() as ctx:
        k = Core(nc, ctx)
        k.ps = ctx.enter_context(nc.psum_tensor("ps", [P, 8, 512], F32))
        setup(k, d)
        cross_attention(k, 0)
        if stages > 1:
            local_transformer(k, d)
        if stages > 2:
            cross_attention(k, 1)
        if stages > 3:
            top1_experts(k, d)
        if stages > 4:
            cross_attention(k, 2)
        if stages > 5:
            capacity_experts(k, d)
        if stages > 6:
            cross_attention(k, 3)
        if stages > 7:
            top2_experts(k, d)
        store(k, out)




def heads_apart(np, m):
    out = np.zeros(m.shape[:-1] + (4, 4, 32), m.dtype)
    out[..., 0:XD] = m.reshape(m.shape[:-1] + (4, 4, XD)).swapaxes(-3, -2)
    return out.reshape(m.shape[:-1] + (4 * P,))


def per_head(np, w):
    out = np.zeros((P, P), w.dtype)
    for h in range(XH):
        out[h * XD:(h + 1) * XD, h * XD:(h + 1) * XD] = w
    return out


def layouts(np, i):
    f = np.float32
    c = np.ascontiguousarray
    zero = np.zeros(P, f)
    d = {}
    d["x"] = c(i["x"].transpose(1, 0, 2))
    d["ctxT"] = c(i["ctx_1024"].transpose(2, 0, 1).reshape(P, T))
    wq = [per_head(np, i["L0_xattn_Wq"].T), i["L1_xattn_Wq"].T, i["L2_xattn_Wq"], per_head(np, i["L3_xattn_Wq"])]
    wk = [per_head(np, i["L0_xattn_Wk"].T), i["L1_xattn_Wk"].T, i["L2_xattn_Wk"], per_head(np, i["L3_xattn_Wk"])]
    wv = [per_head(np, i["L0_xattn_Wv"].T), i["L1_xattn_Wv"].T, i["L2_xattn_Wv"], per_head(np, i["L3_xattn_Wv"])]
    d["wq"] = c(np.stack([heads_apart(np, w) for w in wq], 1))
    d["wk"] = c(np.stack([heads_apart(np, w) for w in wk], 1))
    d["wv"] = c(np.concatenate(wv, 1))
    d["bv"] = np.concatenate([zero, i["L1_xattn_bv"], i["L2_xattn_bv"], zero])[None]
    bq = [heads_apart(np, v) for v in (zero, i["L1_xattn_bq"], i["L2_xattn_bq"], zero)]
    bk = [heads_apart(np, v) for v in (zero, i["L1_xattn_bk"], i["L2_xattn_bk"], zero)]
    one = np.zeros((4, 4, 32), f)
    one[:, :, XD] = 1.0
    bq[0] = one.reshape(4 * P)
    d["bqk"] = c(np.stack([np.stack(bq), np.stack(bk)], 1).reshape(NX, 2, 4, P).transpose(3, 0, 1, 2))
    d["strip"] = c(one.reshape(4, P)[0:1])
    d["wo"] = c(np.stack([i["L0_xattn_Wo"].T, i["L1_xattn_Wo"].T, i["L2_xattn_Wo"]], 1))
    d["bo"] = np.stack([i["L0_xattn_bo"], i["L1_xattn_bo"], i["L2_xattn_bo"]])[None]
    d["keys"] = i["mask_Bx1x1xS2_if1"].reshape(1, T)
    d["mask1"] = i["mask_1x1xSxS2_if1"].reshape(P, P)
    d["mask3"] = i["mask_1x1xSxS2_fk0"].reshape(P, P)
    order = np.arange(LH).reshape(2, 4).T.reshape(-1)
    w = i["L0_ffn_wqkv"].reshape(LAYERS, P, 3, LH, LD).copy()
    w[:, :, 0:2] = w[:, :, 0:2][:, :, :, order]
    d["wqkv"] = c(w.reshape(LAYERS, P, 3, LH * LD).transpose(1, 0, 2, 3))
    d["lwo"] = c(i["L0_ffn_wo"].reshape(LAYERS, 4, P, P).transpose(2, 0, 1, 3))
    d["w1"] = c(i["L0_ffn_w1"].transpose(1, 0, 2))
    nch = len(HCH)
    w2 = np.zeros((LAYERS, nch * P, P), f)
    w2[:, 0:HID] = i["L0_ffn_w2"]
    d["w2"] = c(w2.reshape(LAYERS, nch, P, P).transpose(2, 0, 1, 3))
    b1 = np.zeros((LAYERS, 2, nch * P), f)
    b1[:, :, 0:HID] = i["L0_ffn_b1"].reshape(LAYERS, 2, HID)
    d["b1"] = c(b1.reshape(LAYERS, 2, nch, P).transpose(3, 0, 1, 2))
    d["b2"] = i["L0_ffn_b2"][None]
    d["gb"] = c(np.stack([i["L0_ffn_ln_g"], i["L0_ffn_ln_b"]], 1).transpose(2, 0, 1))
    d["qks"] = c(np.stack([i["L0_ffn_q_scale"], i["L0_ffn_k_scale"]], 1)[None])
    half = np.arange(0, LD, 2, dtype=f)
    t = np.arange(P, dtype=f)
    ang = t[:, None] * (f(1.0) / f(10000.0) ** (half / f(LD)))[None]
    ang = np.concatenate([ang, ang], 1)
    base = (half + f(0.4 * LD)) / f(1.4 * LD)
    sc = base[None] ** ((t - P // 2) / f(WINDOW // 2))[:, None]
    sc = np.concatenate([sc, sc], 1)
    cos, sin = np.cos(ang), np.sin(ang)
    sign = np.where(np.arange(LD) < LD // 2, f(-1), f(1))
    d["rotc"] = c(np.stack([cos * sc, cos / sc], 1).astype(f))
    d["rots"] = c(np.stack([sin * sc * sign, sin / sc * sign], 1).astype(f))
    d["cent"] = c(i["L1_ffn_centroids"].T)
    d["t1w1"] = c(i["L1_ffn_W1"].transpose(0, 2, 1))
    d["t1w2"] = c(i["L1_ffn_W2"].transpose(0, 2, 1).reshape(E1, FC1, P, P).transpose(0, 2, 1, 3))
    d["t1eb"] = c(np.concatenate([i["L1_ffn_gamma"][:, :, None], i["L1_ffn_beta"][:, :, None],
                                  i["L1_ffn_b1"].reshape(E1, FC1, P).transpose(0, 2, 1)], 2))
    d["t1b2"] = i["L1_ffn_b2"]
    d["iota"] = np.arange(E2, dtype=f)[None]
    d["rw"] = i["L2_ffn_w_router"]
    w = np.stack([i["L2_ffn_w_gate"], i["L2_ffn_w_up"], i["L2_ffn_w_down"]])
    d["w2x"] = c(w.reshape(3, E2 // SPAN2, SPAN2, P, P).transpose(1, 3, 0, 2, 4))
    d["gw"] = c(i["L3_ffn_gate_weight"].T)

    def chunks(routed, shared):
        return c(np.concatenate([routed.reshape(E3 * I3, P), shared]).reshape(CH3, P, P).transpose(2, 0, 1))
    d["wg3"] = chunks(i["L3_ffn_w_gate"], i["L3_ffn_ws_gate"])
    d["wu3"] = chunks(i["L3_ffn_w_up"], i["L3_ffn_ws_up"])
    down = np.concatenate([i["L3_ffn_w_down"].transpose(0, 2, 1).reshape(E3 * I3, P), i["L3_ffn_ws_down"].T])
    d["wd3"] = c(down.reshape(CH3, P, P).transpose(1, 0, 2))
    d["sel"] = c(np.repeat(np.eye(E3, dtype=f), I3, 1).reshape(E3, CH3 - 1, P))
    return d


STAGES = 8


def kernel(**inputs):
    import numpy as np
    import concourse.bacc as _bacc
    from concourse.bass_utils import run_bass_kernel_spmd as _run

    nc = _bacc.Bacc("TRN2", target_bir_lowering=False, num_devices=1)
    arrays = {"in_" + n: np.ascontiguousarray(a) for n, a in
              layouts(np, {n: np.asarray(a) for n, a in inputs.items()}).items()}
    d = {n[3:]: nc.dram_tensor(n, a.shape, mybir.dt.from_np(a.dtype), kind="ExternalInput").ap()
         for n, a in arrays.items()}
    out = nc.dram_tensor("out_0", (B, P, P), F32, kind="ExternalOutput").ap()
    build(nc, d, out, STAGES)
    return _run(nc, [arrays], core_ids=[0]).results[0]["out_0"]
```

```python
from contextlib import ExitStack

import concourse.bass as bass
from concourse import mybir

ALU = mybir.AluOpType
ACT = mybir.ActivationFunctionType
AX = mybir.AxisListType
F32 = mybir.dt.float32
I32 = mybir.dt.int32

B = 8
P = 128
T = B * P
HB = B // 2
HALF = T // 2
NX = 4
XH, XD = 16, 8
LH, LD = 8, 64
LAYERS = 2
WINDOW = 64
HID = 341
HCH = [(0, 128), (128, 128), (256, HID - 256)]
E1, F1 = 8, 512
FC1 = F1 // P
E2, C2 = 32, 40
SLOTS = E2 * C2
SCH = SLOTS // P
SPAN2 = 4
E3, I3 = 8, 64
CH3 = E3 * I3 // P + 1
ROUTED_SCALE = 2.5
EPS = 1e-5
NEG = -float(2 ** 100)
LOWEST = -3.0e38


class Count:

    def __init__(self, sem):
        self.sem = sem
        self.base = 0


class Core:

    def __init__(self, nc, ctx):
        self.nc = nc
        self.ctx = ctx
        self.counts = {}
        self.made = {}

    def sb(self, name, shape, dt=F32):
        return self.ctx.enter_context(self.nc.sbuf_tensor(name, shape, dt))

    def fresh(self, ctx, name, shape, dt=F32):
        self.made[name] = self.made.get(name, 0) + 1
        return ctx.enter_context(self.nc.sbuf_tensor(f"{name}_{self.made[name]}", shape, dt))

    def count(self, name):
        if name not in self.counts:
            self.counts[name] = Count(self.ctx.enter_context(self.nc.semaphore(name)))
        return self.counts[name]


def spread(ap, n):
    return ap.unsqueeze(len(ap.shape)).to_broadcast(list(ap.shape) + [n])


def setup(k, d):
    nc = k.nc
    load_v, load, made = (k.count(n) for n in ("su_load_v", "su_load", "su_made"))
    k.x, k.xn = k.sb("x", [P, B, P]), k.sb("xn", [P, B, P])
    k.xnT, k.ctxT = k.sb("xnT", [P, T]), k.sb("ctxT", [P, T])
    k.st, k.mv = k.sb("st", [P, B, 6]), k.sb("mv", [P, B, 2])
    k.std, k.rs = k.sb("std", [P, B]), k.sb("rs", [P, B])
    k.ident, k.ones, k.zeros = k.sb("ident", [P, P]), k.sb("ones", [P, HALF]), k.sb("zeros", [P, P])
    k.band, k.mask1, k.mask3 = k.sb("band", [P, P]), k.sb("mask1", [P, P]), k.sb("mask3", [P, P])
    k.negkeys = k.sb("negkeys", [P, B, P])
    k.wq, k.wk = k.sb("wq", [P, NX, 4 * P]), k.sb("wk", [P, NX, 4 * P])
    k.bqk, k.wo, k.bo = k.sb("bqk", [P, NX, 2, 4]), k.sb("wo", [P, 3, P]), k.sb("bo", [P, 3, P])
    k.v1 = k.sb("v1", [P, B, NX, XH, XD + 1])
    k.qkT = k.sb("qkT", [P, B, 2, 4, P])
    k.kslot = k.sb("kslot", [P, 2, 4, 4, P])
    k.eps = k.sb("eps", [P, 1])
    k.prime, k.prime2 = k.sb("prime", [P, 1]), k.sb("prime2", [P, 1])
    with ExitStack() as own:
        def sb(name, shape, dt=F32):
            return k.fresh(own, name, shape, dt)
        wv, bv = sb("wv", [P, NX * P]), sb("bv", [P, NX * P])
        keys_i, mask1_i = sb("keys_i", [P, B, P], I32), sb("mask1_i", [P, P], I32)
        vready = k.count("su_v")
        with nc.Block() as block:
            @block.sync
            def _(sp):
                sp.dma_start(k.ctxT[:, 0:HALF], d["ctxT"][:, 0:HALF]).then_inc(load_v.sem, 16)
                sp.dma_start(bv[:, :], d["bv"].to_broadcast([P, NX * P])).then_inc(load_v.sem, 16)
                sp.dma_start(k.x[:, :, :], d["x"]).then_inc(load.sem, 16)
                sp.dma_start(keys_i[:, :, :], d["keys"].to_broadcast([P, B, P])).then_inc(load.sem, 16)
                sp.dma_start(mask1_i[:, :], d["mask1"]).then_inc(load.sem, 16)
                sp.dma_start(k.mask3[:, :], d["mask3"]).then_inc(load.sem, 16)
                sp.dma_start(k.bqk[:, :, :, :], d["bqk"]).then_inc(load.sem, 16)
                sp.dma_start(k.bo[:, :, :], d["bo"].to_broadcast([P, 3, P])).then_inc(load.sem, 16)
                sp.wait_ge(load.sem, 16 * 9)

            @block.scalar
            def _(a):
                a.dma_start(wv[:, :], d["wv"]).then_inc(load_v.sem, 16)
                a.dma_start(k.ctxT[:, HALF:T], d["ctxT"][:, HALF:T]).then_inc(load_v.sem, 16)
                a.dma_start(k.wk[:, :, :], d["wk"]).then_inc(load.sem, 16)
                a.dma_start(k.wq[:, :, :], d["wq"]).then_inc(load.sem, 16)
                a.dma_start(k.wo[:, :, :], d["wo"]).then_inc(load.sem, 16)

            @block.gpsimd
            def _(g):
                g.memset(k.ident[:, :], 0.0).then_inc(made.sem, 1)
                g.memset(k.band[:, :], 0.0).then_inc(made.sem, 1)
                g.memset(k.ones[:, :], 1.0).then_inc(made.sem, 1)
                g.memset(k.zeros[:, :], 0.0).then_inc(made.sem, 1)
                g.memset(k.v1[:, :, :, :, XD:XD + 1], 1.0).then_inc(made.sem, 1)
                g.wait_ge(made.sem, 5)
                g.affine_select(out=k.ident[:, :], in_=k.ident[:, :], compare_op=ALU.not_equal, fill=1.0,
                                base=0, pattern=[[-1, P]], channel_multiplier=1).then_inc(made.sem, 1)
                g.affine_select(out=k.band[:, :], in_=k.band[:, :], compare_op=ALU.is_ge, fill=NEG,
                                base=0, pattern=[[-1, P]], channel_multiplier=1).then_inc(made.sem, 1)
                g.wait_ge(made.sem, 7)
                g.affine_select(out=k.band[:, :], in_=k.band[:, :], compare_op=ALU.is_ge, fill=NEG,
                                base=WINDOW, pattern=[[1, P]], channel_multiplier=-1).then_inc(made.sem, 1)

            @block.vector
            def _(v):
                v.memset(k.eps[:, :], EPS)
                v.memset(k.kslot[:, :], 0.0)
                v.wait_ge(load_v.sem, 64)
                for b in range(B):
                    v.wait_ge(vready.sem, b + 1)
                    v.tensor_tensor(k.v1[:, b, :, :, 0:XD],
                                    k.ps[:, b, :].rearrange("p (a h e) -> p a h e", a=NX, e=XD),
                                    bv[:, :].rearrange("p (a h e) -> p a h e", a=NX, e=XD), ALU.add)
                v.wait_ge(load.sem, 16 * 9)
                v.tensor_scalar(k.negkeys[:, :, :], keys_i[:, :, :], 0.0, NEG, ALU.is_equal, ALU.mult)
                v.tensor_scalar(k.mask1[:, :], mask1_i[:, :], 0.0, NEG, ALU.is_equal, ALU.mult)

            @block.tensor
            def _(t):
                t.wait_ge(load_v.sem, 64)
                for b in range(B):
                    t.matmul(k.ps[:, b, :], k.ctxT[:, b * P:(b + 1) * P], wv[:, :], start=True, stop=True)\
                     .then_inc(vready.sem, 1)


def layer_norm(k, src, dst, dst_t, gain=None, shift=None, keys_of=None):
    nc, ps = k.nc, k.ps
    stats, var, std, rstd, norm, turned, out, kready, kout = (k.count("ln_" + n) for n in (
        "stats", "var", "std", "rstd", "norm", "turned", "out", "kready", "kout"))
    units = [(g, h) for g in range(4) for h in range(2)] if keys_of is not None else []
    with nc.Block() as block:
        @block.vector
        def _(v):
            for b in range(B):
                v.bn_stats(k.st[:, b, :], src(b)).then_inc(stats.sem, 1)
            for b in range(B):
                v.wait_ge(stats.sem, stats.base + b + 1)
                v.bn_aggr(k.mv[:, b, :], k.st[:, b, :]).then_inc(var.sem, 1)
            v.wait_ge(std.sem, std.base + 1)
            v.reciprocal(k.rs[:, :], k.std[:, :]).then_inc(rstd.sem, 1)
            v.wait_ge(rstd.sem, rstd.base + 1)
            for b in range(B):
                v.tensor_scalar(dst[:, b, :], src(b), k.mv[:, b, 0:1], k.rs[:, b:b + 1],
                                ALU.subtract, ALU.mult).then_inc(norm.sem, 1)

        @block.tensor
        def _(t):
            for n, (g, h) in enumerate(units):
                if n >= 6:
                    t.wait_ge(kout.sem, kout.base + n - 5)
                t.matmul(ps[:, 2 + n % 6, :], k.wk[:, keys_of, g * P:(g + 1) * P],
                         k.ctxT[:, h * HALF:(h + 1) * HALF], start=True, stop=True).then_inc(kready.sem, 1)
            for b in range(B):
                t.wait_ge(norm.sem, norm.base + b + 1)
                t.transpose(ps[:, b // HB, P * (b % HB):P * (b % HB) + P], dst[:, b, :],
                            k.ident[:, :]).then_inc(turned.sem, 1)

        @block.scalar
        def _(a):
            def keys(n):
                g, h = units[n]
                a.wait_ge(kready.sem, kready.base + n + 1)
                a.activation(k.qkT[:, HB * h:HB * h + HB, 1, g, :],
                             ps[:, 2 + n % 6, :].rearrange("p (b t) -> p b t", b=HB), ACT.Identity,
                             bias=k.bqk[:, keys_of, 1, g:g + 1]).then_inc(kout.sem, 1)
            a.activation(k.prime[:, :], k.ones[:, 0:1], ACT.Sqrt)
            for n in range(len(units) // 4):
                keys(n)
            a.wait_ge(var.sem, var.base + B)
            a.activation(k.std[:, :], k.mv[:, :, 1], ACT.Sqrt, bias=k.eps[:, :]).then_inc(std.sem, 1)
            for n in range(len(units) // 4, len(units)):
                keys(n)
            for h in range(2):
                a.wait_ge(turned.sem, turned.base + HB * (h + 1))
                cols = slice(h * HALF, (h + 1) * HALF)
                if gain is None:
                    a.activation(dst_t[:, cols], ps[:, h, :], ACT.Copy).then_inc(out.sem, 1)
                else:
                    a.activation(dst_t[:, cols], ps[:, h, :], ACT.Identity, scale=gain, bias=shift)\
                     .then_inc(out.sem, 1)
    for s, n in ((stats, B), (var, B), (std, 1), (rstd, 1), (norm, B), (turned, B), (out, 2),
                 (kready, len(units)), (kout, len(units))):
        s.base += n


def query_projections(k, a):
    nc, ps = k.nc, k.ps
    qready, qout = k.count("pj_qready"), k.count("pj_qout")
    units = [(g, h) for g in range(4) for h in range(2)]
    with nc.Block() as block:
        @block.tensor
        def _(t):
            for n, (g, h) in enumerate(units):
                t.matmul(ps[:, n, :], k.wq[:, a, g * P:(g + 1) * P], k.xnT[:, h * HALF:(h + 1) * HALF],
                         start=True, stop=True).then_inc(qready.sem, 1)

        def take(n):
            g, h = units[n]
            return (k.qkT[:, HB * h:HB * h + HB, 0, g, :], ps[:, n, :].rearrange("p (b t) -> p b t", b=HB),
                    k.bqk[:, a, 0, g:g + 1])

        @block.scalar
        def _(s):
            for n in range(0, len(units), 2):
                dst, src, bias = take(n)
                s.wait_ge(qready.sem, qready.base + n + 1)
                s.activation(dst, src, ACT.Identity, bias=bias).then_inc(qout.sem, 1)

        @block.vector
        def _(v):
            for n in range(1, len(units), 2):
                dst, src, bias = take(n)
                v.wait_ge(qready.sem, qready.base + n + 1)
                v.tensor_scalar(dst, src, bias, None, ALU.add).then_inc(qout.sem, 1)

        if a < 3:
            @block.gpsimd
            def _(g):
                g.tensor_tensor(k.x[:, :, :], k.x[:, :, :],
                                k.bo[:, a, :].unsqueeze(1).to_broadcast([P, B, P]), ALU.add)
    for s in (qready, qout):
        s.base += len(units)


def over_batches(eng, step):
    step(0, 0, 0)
    step(1, 1, 1)
    with eng.Fori(0, (B - 4) // 2) as i:
        step(2 * i + 2, 0, 2)
        step(2 * i + 3, 1, 2)
    step(B - 2, 0, B - 2)
    step(B - 1, 1, B - 1)


def attention(k, kind, x, kslot, values, weights):
    nc, ps = k.nc, k.ps
    local, select = kind == "local", kind == 3
    project = not select
    G = 2 if local else 4
    W = LD if local else XD
    NH = 4 * G
    R = 2 if local else 4
    copies = R + 2 if kind == 0 else R + 1
    CH = NH * W // P
    scale = {"local": 8.0, 0: P ** -0.5, 1: XD ** -0.5, 2: XD ** -0.5, 3: 1.0}[kind]
    mask = {"local": k.band, 0: None, 1: k.mask1, 2: k.zeros, 3: k.mask3}[kind]
    slot_in = [k.count("at_slot0_in"), k.count("at_slot1_in")]
    (scored, times, zeroed, top, minus, expd, turned, evac_even, evac_odd, pv, recip, normed,
     oturned, oT_out, projected, res) = (k.count("at_" + n) for n in (
        "scored", "times", "zeroed", "top", "minus", "expd", "turned", "evac_even",
        "evac_odd", "pv", "recip", "normed", "oturned", "oT_out", "projected", "res"))
    with ExitStack() as own:
        def sb(name, shape):
            return k.fresh(own, name, shape)
        qslot, sm = sb("qslot", [P, 2, 4, P]), sb("sm", [P, 2, G, 4, P])
        pace = sb("pace", [P, 2, G])
        mx, pt, zt = sb("mx", [P, 2, G, 4]), sb("pt", [P, 2, 4, P]), sb("zt", [P, 2, 4, P])
        ro, on, oT = sb("ro", [P, NH]), sb("on", [P, NH, W]), sb("oT", [P, CH * P])
        mslot = k.fresh(own, "mslot", [P, 2, P]) if kind == 0 else None
        on_flat = on[:, :, :].rearrange("p h w -> p (h w)")

        def out(g, j):
            if local:
                return ps[:, 2 + g, j * (W + 1):(j + 1) * (W + 1)]
            return ps[:, 6, (4 * g + j) * (W + 1):(4 * g + j + 1) * (W + 1)]

        if local:
            o_all = ps[:, 2:4, 0:4 * (W + 1)].rearrange("p g (h w) -> p g h w", w=W + 1)
            on_all = on[:, :, :].rearrange("p (g h) w -> p g h w", g=2)
            ro_all = ro[:, :].rearrange("p (g h) -> p g h", g=2)
            o_sum, o_val = o_all[:, :, :, W], o_all[:, :, :, 0:W]
        else:
            o_all = ps[:, 6, 0:NH * (W + 1)].rearrange("p (h w) -> p h w", w=W + 1)
            on_all, ro_all = on[:, :, :], ro[:, :]
            o_sum, o_val = o_all[:, :, W], o_all[:, :, 0:W]
        oT_ps = ps[:, 6, :] if local else ps[:, 7, 0:P]
        proj_ps = ps[:, 7, 3 * P:4 * P]

        with nc.Block() as block:
            @block.sync
            def _(sp):
                def copy(b, p):
                    sp.dma_start(qslot[:, p], k.qkT[:, b, 0]).then_inc(slot_in[p].sem, 16)
                    if kind == 0:
                        sp.dma_start(mslot[:, p], k.negkeys[:, b]).then_inc(slot_in[p].sem, 16)
                    for r in range(R):
                        rows = slice(r * P // R, (r + 1) * P // R)
                        sp.dma_start(kslot[rows, p, :, r, :], k.qkT[rows, b, 1]).then_inc(slot_in[p].sem, 16)
                copy(0, 0)
                copy(1, 1)
                with sp.Fori(0, (B - 2) // 2) as i:
                    for p in range(2):
                        if kind == 0:
                            sp.wait_ge(top.sem, top.base + NH * (2 * i + p + 1))
                        else:
                            sp.wait_ge(scored.sem, scored.base + G * (2 * i + p + 1))
                        copy(2 * i + 2 + p, p)

            @block.tensor
            def _(t):
                def score(b, p, g, first=False):
                    t.wait_ge(slot_in[p].sem, slot_in[p].base + copies * (8 * (b - p) + 16))
                    if not first and select:
                        t.wait_ge(times.sem, times.base + G * (b - 1) + g + 1)
                    elif not first:
                        t.wait_ge(top.sem, top.base + NH * (b - 1) + 4 * g + 4)
                    for c in range(g * 4 // R, (g + 1) * 4 // R):
                        at = c * R * P - g * 4 * P
                        m = t.matmul(ps[:, g, at:at + R * P], qslot[:, p, c, :], kslot[:, p, c],
                                     start=True, stop=True)
                    m.then_inc(scored.sem, 1)

                def turn(b, p, g, first):
                    t.wait_ge(expd.sem, expd.base + G * b + g + 1)
                    if not (first and g < 2):
                        e = evac_odd if g % 2 else evac_even
                        t.wait_ge(e.sem, e.base + G // 2 * b + g // 2)
                    for j in range(4):
                        m = t.transpose(ps[:, 4 + g % 2, j * P:(j + 1) * P], sm[:, p, g, j, :],
                                        k.ident[:, :])
                    m.then_inc(turned.sem, 1)

                def weigh(b, g, first):
                    e = evac_odd if g % 2 else evac_even
                    t.wait_ge(e.sem, e.base + G // 2 * b + g // 2 + 1)
                    if g == 0 and not first:
                        t.wait_ge(normed.sem, normed.base + b)
                    for j in range(4):
                        m = t.matmul(out(g, j), pt[:, g % 2, j, :], values(b, 4 * g + j),
                                     start=True, stop=True)
                    m.then_inc(pv.sem, 1)

                def turn_out(b, first):
                    t.wait_ge(normed.sem, normed.base + b + 1)
                    if not first:
                        t.wait_ge(res.sem, res.base + b)
                    for n in range(CH):
                        m = t.transpose(oT_ps[:, n * P:(n + 1) * P], on_flat[:, n * P:(n + 1) * P],
                                        k.ident[:, :])
                    m.then_inc(oturned.sem, 1)

                def project_out(b):
                    t.wait_ge(oT_out.sem, oT_out.base + b + 1)
                    for n in range(CH):
                        m = t.matmul(proj_ps, oT[:, n * P:(n + 1) * P], weights(n), start=(n == 0),
                                     stop=(n == CH - 1))
                    m.then_inc(projected.sem, 1)

                def step(b, p, place):
                    if place < B - 1:
                        score(b + 1, 1 - p, 0)
                    if place > 0 and project:
                        turn_out(b - 1, place == 1)
                    turn(b, p, 0, place == 0)
                    turn(b, p, 1, place == 0)
                    if place > 0 and project:
                        project_out(b - 1)
                    for g in range(2, G):
                        if place < B - 1:
                            score(b + 1, 1 - p, g - 1)
                        weigh(b, g - 2, place == 0)
                        turn(b, p, g, place == 0)
                    if place < B - 1:
                        score(b + 1, 1 - p, G - 1)
                    weigh(b, G - 2, place == 0)
                    weigh(b, G - 1, place == 0)

                for g in range(G):
                    score(0, 0, g, True)
                over_batches(t, step)
                if project:
                    turn_out(B - 1, False)
                    project_out(B - 1)

            @block.vector
            def _(v):
                def masked_max(b, p, g, early):
                    if select:
                        v.wait_ge(zeroed.sem, zeroed.base + G * b + g + 1)
                    else:
                        v.wait_ge(scored.sem, scored.base + G * b + g + 1)
                        if not early:
                            v.wait_ge(turned.sem, turned.base + G * (b - 2) + g + 1)
                    v.memset(pace[:, p, g:g + 1], 0.0)
                    for j in range(4):
                        v.tensor_tensor_reduce(
                            sm[:, p, g, j, :], sm[:, p, g, j, :] if select else ps[:, g, j * P:(j + 1) * P],
                            zt[:, g % 2, j, :] if select else mslot[:, p, :] if kind == 0 else mask[:, :], 1.0, LOWEST, ALU.add, ALU.max,
                            mx[:, p, g, j:j + 1]).then_inc(top.sem, 1)

                def multiply(b, p, g, early):
                    v.wait_ge(scored.sem, scored.base + G * b + g + 1)
                    if not early:
                        v.wait_ge(turned.sem, turned.base + G * (b - 2) + g + 1)
                    v.tensor_tensor(sm[:, p, g], ps[:, g, :].rearrange("p (j t) -> p j t", j=4),
                                    mask[:, :].unsqueeze(1).to_broadcast([P, 4, P]), ALU.mult)\
                     .then_inc(times.sem, 1)

                def zero_term(b, p, g, first):
                    v.wait_ge(times.sem, times.base + G * b + g + 1)
                    if not (first and g < 2):
                        v.wait_ge(top.sem, top.base + 4 * (G * b + g - 1))
                    v.tensor_scalar(zt[:, g % 2], sm[:, p, g], 0.0, NEG, ALU.is_equal, ALU.mult)\
                     .then_inc(zeroed.sem, 1)

                def evacuate(b, g, first):
                    v.wait_ge(turned.sem, turned.base + G * b + g + 1)
                    if not (first and g < 2):
                        v.wait_ge(pv.sem, pv.base + G * b + g - 1)
                    v.tensor_copy(pt[:, g % 2], ps[:, 4 + g % 2, :].rearrange("p (j t) -> p j t", j=4))\
                     .then_inc(evac_even.sem, 1)

                def normalise(b, first):
                    v.wait_ge(pv.sem, pv.base + G * b + G)
                    v.reciprocal(ro_all, o_sum).then_inc(recip.sem, 1)
                    v.wait_ge(recip.sem, recip.base + b + 1)
                    if project and not first:
                        v.wait_ge(oturned.sem, oturned.base + b)
                    v.tensor_tensor(on_all, o_val, spread(ro_all, W), ALU.mult).then_inc(normed.sem, 1)
                    if not project:
                        v.wait_ge(normed.sem, normed.base + b + 1)
                        v.tensor_tensor(x[:, b, :], x[:, b, :], on_flat, ALU.add).then_inc(res.sem, 1)
                        v.wait_ge(res.sem, res.base + b + 1)

                def residual(b):
                    v.wait_ge(projected.sem, projected.base + b + 1)
                    v.tensor_tensor(x[:, b, :], x[:, b, :], proj_ps, ALU.add).then_inc(res.sem, 1)

                def scores_of(b, p, early, between, first=False):
                    ahead = 2 if select else 0
                    for g in range(G + ahead):
                        if select and g < G:
                            multiply(b, p, g, early)
                        if select and 1 <= g <= G:
                            zero_term(b, p, g - 1, first)
                        if g >= ahead:
                            masked_max(b, p, g - ahead, early)
                        for work in between.get(g, ()):
                            work()

                def step(b, p, place):
                    first = place == 0
                    between = {0: [lambda: evacuate(b, 0, first)]}
                    if place > 0 and project:
                        between[0].append(lambda: residual(b - 1))
                    if G > 2:
                        between[1] = [lambda: evacuate(b, 2, first)]
                    if place < B - 1:
                        scores_of(b + 1, 1 - p, place == 0, between)
                    else:
                        for g in between:
                            for work in between[g]:
                                work()
                    normalise(b, first)

                scores_of(0, 0, True, {}, True)
                over_batches(v, step)
                if project:
                    residual(B - 1)

            @block.gpsimd
            def _(g_):
                def subtract(b, p, g):
                    g_.wait_ge(top.sem, top.base + NH * b + 4 * g + 4)
                    g_.tensor_tensor(sm[:, p, g], sm[:, p, g], spread(mx[:, p, g, :], P), ALU.subtract)\
                      .then_inc(minus.sem, 1)

                def shift(b, p):
                    for g in range(G):
                        subtract(b, p, g)

                def step(b, p, place):
                    if place < B - 1:
                        shift(b + 1, 1 - p)

                shift(0, 0)
                over_batches(g_, step)

            @block.scalar
            def _(a):
                def exponent(b, p, g):
                    a.wait_ge(minus.sem, minus.base + G * b + g + 1)
                    a.activation(sm[:, p, g], sm[:, p, g], ACT.Exp, scale=scale).then_inc(expd.sem, 1)

                def evacuate(b, g, first):
                    a.wait_ge(turned.sem, turned.base + G * b + g + 1)
                    if not (first and g < 2):
                        a.wait_ge(pv.sem, pv.base + G * b + g - 1)
                    a.activation(pt[:, g % 2], ps[:, 4 + g % 2, :].rearrange("p (j t) -> p j t", j=4),
                                 ACT.Copy).then_inc(evac_odd.sem, 1)

                def take_oT(b, first):
                    a.wait_ge(oturned.sem, oturned.base + b + 1)
                    if not first:
                        a.wait_ge(projected.sem, projected.base + b)
                    a.activation(oT[:, :], oT_ps, ACT.Copy).then_inc(oT_out.sem, 1)

                def step(b, p, place):
                    if place > 0 and project:
                        take_oT(b - 1, place == 1)
                    for g in range(0, G, 2):
                        evacuate(b, g + 1, place == 0)
                        if place < B - 1:
                            exponent(b + 1, 1 - p, g)
                            exponent(b + 1, 1 - p, g + 1)

                a.activation(k.prime[:, :], k.ones[:, 0:1], ACT.Exp)
                for g in range(G):
                    exponent(0, 0, g)
                over_batches(a, step)
                if project:
                    take_oT(B - 1, False)
    for s in slot_in:
        s.base += 16 * copies * B // 2
    scored.base += G * B
    top.base += NH * B
    for s in (minus, expd, turned, pv):
        s.base += G * B
    for s in (evac_even, evac_odd):
        s.base += G // 2 * B
    for s in (recip, normed, res):
        s.base += B
    if select:
        times.base += G * B
        zeroed.base += G * B
    if project:
        for s in (oturned, oT_out, projected):
            s.base += B


def cross_attention(k, a):
    layer_norm(k, lambda b: k.x[:, b, :], k.xn, k.xnT, keys_of=a)
    query_projections(k, a)
    attention(k, a, k.x, k.kslot, lambda b, h: k.v1[:, b, a, h, :], lambda n: k.wo[:, a, :])



def shift_tokens(k, y, hT):
    nc, ps = k.nc, k.ps
    turned, out = k.count("sh_turned"), k.count("sh_out")
    with nc.Block() as block:
        @block.tensor
        def _(t):
            for b in range(B):
                t.transpose(ps[:, b // HB, P * (b % HB):P * (b % HB) + P], y[:, b, :],
                            k.ident[:, :]).then_inc(turned.sem, 1)

        @block.scalar
        def _(a):
            for h in range(2):
                a.wait_ge(turned.sem, turned.base + HB * (h + 1))
                dst = hT[:, h * HALF:(h + 1) * HALF].rearrange("p (b t) -> p b t", b=HB)
                src = ps[:, h, :].rearrange("p (b t) -> p b t", b=HB)
                a.activation(dst[0:P // 2], src[0:P // 2], ACT.Copy).then_inc(out.sem, 1)
                a.activation(dst[P // 2:P, :, 1:P], src[P // 2:P, :, 0:P - 1], ACT.Copy).then_inc(out.sem, 1)
    turned.base += B
    out.base += 4


def local_qkv(k, hT, wqkv, v2, tab_a, tab_b):
    nc, ps = k.nc, k.ps
    slot_in = [k.count("lq_slot0_in"), k.count("lq_slot1_in")]
    made, raw_out, v_out, squared, rotated, swapped, summed, norms, rstd, added, scaled, turned, out = (
        k.count("lq_" + n) for n in ("made", "raw_out", "v_out", "squared", "rotated", "swapped", "summed",
                                     "norms", "rstd", "added", "scaled", "turned", "out"))
    with ExitStack() as own:
        def sb(name, shape):
            return k.fresh(own, name, shape)
        hs, raw, sq = sb("hs", [P, 2, P]), sb("raw", [P, 2, 2, LH, LD]), sb("sq", [P, 2, 2, LH, LD])
        t1, t2 = sb("t1", [P, 2, 2, LH, LD]), sb("t2", [P, 2, 2, LH, LD])
        ss, ssm, nrm, rn = (sb(n, [P, 2, 2 * LH]) for n in ("ss", "ssm", "nrm", "rn"))
        half = LD // 2
        with nc.Block() as block:
            @block.sync
            def _(sp):
                hb = hT[:, :].rearrange("p (b t) -> p b t", b=B)
                sp.dma_start(hs[:, 0], hb[:, 0]).then_inc(slot_in[0].sem, 16)
                sp.dma_start(hs[:, 1], hb[:, 1]).then_inc(slot_in[1].sem, 16)
                with sp.Fori(0, (B - 2) // 2) as i:
                    for p in range(2):
                        sp.wait_ge(made.sem, made.base + 3 * (2 * i + p + 1))
                        sp.dma_start(hs[:, p], hb[:, 2 * i + 2 + p]).then_inc(slot_in[p].sem, 16)

            @block.tensor
            def _(t):
                def qkv(b, p, early):
                    t.wait_ge(slot_in[p].sem, slot_in[p].base + 8 * (b - p) + 16)
                    if not early:
                        t.wait_ge(v_out.sem, v_out.base + b - 1)
                    for n in range(3):
                        t.matmul(ps[:, 3 * p + n, :], hs[:, p, :], wqkv[:, n, :],
                                 start=True, stop=True).then_inc(made.sem, 1)

                def turn(b, p, first):
                    t.wait_ge(scaled.sem, scaled.base + b + 1)
                    if not first:
                        t.wait_ge(out.sem, out.base + 2 * b)
                    for w in range(2):
                        for c in range(4):
                            m = t.transpose(ps[:, 6 + w, c * P:(c + 1) * P], t1[:, p, w, 2 * c:2 * c + 2, :]
                                            .rearrange("p h e -> p (h e)"), k.ident[:, :])
                        m.then_inc(turned.sem, 1)

                def step(b, p, place):
                    if place < B - 1:
                        qkv(b + 1, 1 - p, place == 0)
                    turn(b, p, place == 0)

                qkv(0, 0, True)
                over_batches(t, step)

            @block.scalar
            def _(a):
                def take(b, p, early):
                    if not early:
                        a.wait_ge(rotated.sem, rotated.base + b - 1)
                        a.wait_ge(swapped.sem, swapped.base + 2 * (b - 1))
                    for w in range(2):
                        a.wait_ge(made.sem, made.base + 3 * b + w + 1)
                        a.activation(raw[:, p, w], ps[:, 3 * p + w, :].rearrange("p (h e) -> p h e", e=LD),
                                     ACT.Copy).then_inc(raw_out.sem, 1)
                    a.wait_ge(made.sem, made.base + 3 * b + 3)
                    a.activation(v2[:, b, :, 0:LD], ps[:, 3 * p + 2, :].rearrange("p (h e) -> p h e", e=LD),
                                 ACT.Copy).then_inc(v_out.sem, 1)
                    a.wait_ge(raw_out.sem, raw_out.base + 2 * b + 2)
                    if not early:
                        a.wait_ge(summed.sem, summed.base + 2 * (b - 1))
                    a.activation(sq[:, p], raw[:, p], ACT.Square).then_inc(squared.sem, 1)

                def norm(b, p):
                    a.wait_ge(summed.sem, summed.base + 2 * b + 2)
                    a.activation(nrm[:, p, :], ssm[:, p, :], ACT.Sqrt).then_inc(norms.sem, 1)

                def give(b):
                    for w in range(2):
                        a.wait_ge(turned.sem, turned.base + 2 * b + w + 1)
                        a.activation(k.qkT[:, b, w], ps[:, 6 + w, :].rearrange("p (c t) -> p c t", c=4),
                                     ACT.Copy).then_inc(out.sem, 1)

                def step(b, p, place):
                    if place < B - 1:
                        take(b + 1, 1 - p, place == 0)
                    give(b)
                    if place < B - 1:
                        norm(b + 1, 1 - p)

                a.activation(k.prime[:, :], k.ones[:, 0:1], ACT.Sqrt)
                take(0, 0, True)
                norm(0, 0)
                over_batches(a, step)

            @block.vector
            def _(v):
                def rotate(b, p, early):
                    v.wait_ge(raw_out.sem, raw_out.base + 2 * b + 2)
                    if not early:
                        v.wait_ge(turned.sem, turned.base + 2 * (b - 1))
                    v.tensor_tensor(t1[:, p], raw[:, p], tab_a[:, :, :].unsqueeze(2)
                                    .to_broadcast([P, 2, LH, LD]), ALU.mult).then_inc(rotated.sem, 1)
                    v.wait_ge(squared.sem, squared.base + b + 1)
                    v.tensor_reduce(ss[:, p, :], sq[:, p].rearrange("p w h e -> p (w h) e"), AX.X, ALU.add)\
                     .then_inc(summed.sem, 1)
                    v.wait_ge(summed.sem, summed.base + 2 * b + 1)
                    v.tensor_scalar(ssm[:, p, :], ss[:, p, :], 1e-24, None, ALU.max).then_inc(summed.sem, 1)
                    v.wait_ge(swapped.sem, swapped.base + 2 * b + 2)
                    v.wait_ge(rotated.sem, rotated.base + b + 1)
                    v.tensor_tensor(t1[:, p], t1[:, p], t2[:, p], ALU.add).then_inc(added.sem, 1)

                def scale(b, p):
                    v.wait_ge(norms.sem, norms.base + b + 1)
                    v.reciprocal(rn[:, p, :], nrm[:, p, :]).then_inc(rstd.sem, 1)
                    v.wait_ge(added.sem, added.base + b + 1)
                    v.wait_ge(rstd.sem, rstd.base + b + 1)
                    both = t1[:, p].rearrange("p w h e -> p (w h) e")
                    v.tensor_tensor(both, both, spread(rn[:, p, :], LD), ALU.mult).then_inc(scaled.sem, 1)

                def step(b, p, place):
                    if place < B - 1:
                        rotate(b + 1, 1 - p, place == 0)
                        scale(b + 1, 1 - p)

                rotate(0, 0, True)
                scale(0, 0)
                over_batches(v, step)

            @block.gpsimd
            def _(g):
                def swap(b, p, early):
                    g.wait_ge(raw_out.sem, raw_out.base + 2 * b + 2)
                    if not early:
                        g.wait_ge(added.sem, added.base + b - 1)
                    for lo, other in ((0, half), (half, 0)):
                        g.tensor_tensor(
                            t2[:, p, :, :, lo:lo + half], raw[:, p, :, :, other:other + half],
                            tab_b[:, :, lo:lo + half].unsqueeze(2).to_broadcast([P, 2, LH, half]),
                            ALU.mult).then_inc(swapped.sem, 1)

                def step(b, p, place):
                    if place < B - 1:
                        swap(b + 1, 1 - p, place == 0)

                swap(0, 0, True)
                over_batches(g, step)
    for s in slot_in:
        s.base += 16 * B // 2
    for s, n in ((made, 3), (raw_out, 2), (v_out, 1), (squared, 1), (rotated, 1), (swapped, 2),
                 (summed, 2), (norms, 1), (rstd, 1), (added, 1), (scaled, 1), (turned, 2), (out, 2)):
        s.base += n * B


def gated_ffn(k, y, hT, w1, b1, w2, b2):
    nc, ps = k.nc, k.ps
    made, gelud, gated, out, res = (k.count("gf_" + n) for n in ("made", "gelud", "gated", "out", "res"))
    NC = len(HCH)
    units = [(h, c) for h in range(2) for c in range(NC)]
    with ExitStack() as own:
        gl = k.fresh(own, "gl", [P, 2, HALF])
        uT = k.fresh(own, "uT", [P, 2, NC, HALF])
        with nc.Block() as block:
            @block.tensor
            def _(t):
                def up(n):
                    h, c = units[n]
                    o, m = HCH[c]
                    if n >= 2:
                        t.wait_ge(gated.sem, gated.base + n - 1)
                    for w in range(2):
                        t.matmul(ps[0:m, 2 * (n % 2) + w, :], w1[:, w * HID + o:w * HID + o + m],
                                 hT[:, h * HALF:(h + 1) * HALF], start=True, stop=True)\
                         .then_inc(made.sem, 1)

                def down(h):
                    t.wait_ge(gated.sem, gated.base + NC * (h + 1))
                    for b in range(HB):
                        o = ps[:, 4 + h, b * P:(b + 1) * P]
                        for c, (_, m) in enumerate(HCH):
                            t.matmul(o, uT[0:m, h, c, b * P:(b + 1) * P], w2[0:m, c, :],
                                     start=(c == 0), stop=False)
                        x = t.matmul(o, k.ones[0:1, 0:P], b2, start=False, stop=True)
                    x.then_inc(out.sem, 1)

                for n in range(NC + 1):
                    up(n)
                down(0)
                for n in range(NC + 1, 2 * NC):
                    up(n)
                down(1)

            @block.scalar
            def _(a):
                for n, (h, c) in enumerate(units):
                    m = HCH[c][1]
                    a.wait_ge(made.sem, made.base + 2 * n + 2)
                    if n >= 2:
                        a.wait_ge(gated.sem, gated.base + n - 1)
                    a.activation(gl[0:m, n % 2, :], ps[0:m, 2 * (n % 2) + 1, :], ACT.Gelu,
                                 bias=b1[0:m, 1, c:c + 1]).then_inc(gelud.sem, 1)

            @block.vector
            def _(v):
                def residual(h):
                    v.wait_ge(out.sem, out.base + h + 1)
                    v.tensor_tensor(y[:, HB * h:HB * h + HB, :], y[:, HB * h:HB * h + HB, :],
                                    ps[:, 4 + h, :].rearrange("p (b c) -> p b c", b=HB), ALU.add)\
                     .then_inc(res.sem, 1)
                for n, (h, c) in enumerate(units):
                    m = HCH[c][1]
                    v.wait_ge(gelud.sem, gelud.base + n + 1)
                    v.scalar_tensor_tensor(out=uT[0:m, h, c, :], in0=ps[0:m, 2 * (n % 2), :],
                                           scalar=b1[0:m, 0, c:c + 1], in1=gl[0:m, n % 2, :],
                                           op0=ALU.add, op1=ALU.mult).then_inc(gated.sem, 1)
                residual(0)
                residual(1)
    made.base += 4 * NC
    gelud.base += 2 * NC
    gated.base += 2 * NC
    out.base += 2
    res.base += 2


def local_transformer(k, d):
    nc, ps = k.nc, k.ps
    load, made, tabs = k.count("lt_load"), k.count("lt_made"), k.count("lt_tabs")
    with ExitStack() as own:
        def sb(name, shape):
            return k.fresh(own, name, shape)
        y = k.xn
        hT, v2, htok, hnT = sb("hT", [P, T]), sb("v2", [P, B, LH, LD + 1]), sb("htok", [P, B, P]), k.xnT
        wqkv, wo = sb("wqkv", [P, LAYERS, 3, LH * LD]), sb("lwo", [P, LAYERS, 4, P])
        w1, w2 = sb("w1", [P, LAYERS, 2 * HID]), sb("w2", [P, LAYERS, len(HCH), P])
        b1, b2 = sb("b1", [P, LAYERS, 2, len(HCH)]), sb("b2", [1, LAYERS, P])
        gb, qks = sb("gb", [P, LAYERS, 2]), sb("qks", [P, LAYERS, 2, LD])
        rotc, rots = sb("rotc", [P, 2, LD]), sb("rots", [P, 2, LD])
        tab_a, tab_b = sb("tab_a", [P, LAYERS, 2, LD]), sb("tab_b", [P, LAYERS, 2, LD])
        half = LD // 2
        kslot = sb("lkslot", [P, 2, 4, 2, P])
        with nc.Block() as block:
            @block.sync
            def _(sp):
                for dst, src in ((wqkv, "wqkv"), (wo, "lwo"), (w1, "w1"), (w2, "w2"), (b1, "b1"), (b2, "b2"),
                                 (gb, "gb"), (rotc, "rotc"), (rots, "rots")):
                    sp.dma_start(dst[:], d[src]).then_inc(load.sem, 16)
                sp.dma_start(qks[:, :, :, :], d["qks"].to_broadcast([P, LAYERS, 2, LD])).then_inc(load.sem, 16)
                sp.wait_ge(load.sem, load.base + 160)

            @block.gpsimd
            def _(g):
                g.memset(v2[:, :, :, LD:LD + 1], 1.0).then_inc(made.sem, 1)

            @block.vector
            def _(v):
                v.memset(kslot[:, :], 0.0)
                v.memset(hT[P // 2:P, :].rearrange("p (b t) -> p b t", b=B)[:, :, 0:1], 0.0)
                v.wait_ge(load.sem, load.base + 160)
                for l in range(LAYERS):
                    v.tensor_tensor(tab_a[:, l], rotc[:, :, :], qks[:, l], ALU.mult)
                    v.tensor_tensor(tab_b[:, l, :, 0:half], rots[:, :, 0:half], qks[:, l, :, half:LD], ALU.mult)
                    v.tensor_tensor(tab_b[:, l, :, half:LD], rots[:, :, half:LD], qks[:, l, :, 0:half], ALU.mult)
        layer_norm(k, lambda b: k.x[:, b, :], k.xn, k.xnT)
        for l in range(LAYERS):
            shift_tokens(k, y, hT)
            local_qkv(k, hT, wqkv[:, l], v2, tab_a[:, l], tab_b[:, l])
            attention(k, "local", y, kslot, lambda b, h: v2[:, b, h, :], lambda n: wo[:, l, n, :])
            shift_tokens(k, y, hT)
            turn_back(k, hT)
            layer_norm(k, lambda b: ps[:, 2 + b // HB, P * (b % HB):P * (b % HB) + P], htok, hnT,
                       gb[:, l, 0:1], gb[:, l, 1:2])
            gated_ffn(k, y, hnT, w1[:, l], b1[:, l], w2[:, l], b2[:, l])
        add_stream(k, y)


def turn_back(k, hT):
    with k.nc.Block() as block:
        @block.tensor
        def _(t):
            for b in range(B):
                t.transpose(k.ps[:, 2 + b // HB, P * (b % HB):P * (b % HB) + P], hT[:, b * P:(b + 1) * P],
                            k.ident[:, :])


def add_stream(k, y):
    with k.nc.Block() as block:
        @block.vector
        def _(v):
            v.tensor_tensor(k.x[:, :, :], k.x[:, :, :], y[:, :, :], ALU.add)


def route(v, done, vals, iota, top, at, first, hot):
    n, e = vals.shape[1], vals.shape[2]
    places = iota.unsqueeze(1).to_broadcast([P, n, e])

    def then(m):
        m.then_inc(done.sem, 1)
        done.base += 1
        v.wait_ge(done.sem, done.base)

    then(v.tensor_reduce(top, vals, AX.X, ALU.max))
    then(v.tensor_tensor(at, vals, spread(top, e), ALU.is_equal))
    then(v.scalar_tensor_tensor(out=at, in0=at, scalar=-64.0, in1=places, op0=ALU.mult, op1=ALU.add))
    then(v.tensor_reduce(first, at, AX.X, ALU.min))
    then(v.tensor_tensor(hot, at, spread(first, e), ALU.is_equal))


def top1_experts(k, d):
    nc, ps = k.nc, k.ps
    load, own_step, scored, routed, turned, hot_out, b2_made, alpha_out = (k.count("t1_" + n) for n in (
        "load", "own_step", "scored", "routed", "turned", "hot_out", "b2_made", "alpha"))
    w_in = [k.count("t1_w0_in"), k.count("t1_w1_in")]
    hx, up, relu_a, relu_v, down, summed = (k.count("t1_" + n) for n in (
        "hx", "up", "relu_a", "relu_v", "down", "summed"))
    layer_norm(k, lambda b: k.x[:, b, :], k.xn, k.xnT)
    with ExitStack() as own:
        def sb(name, shape):
            return k.fresh(own, name, shape)
        zn, zT, acc = sb("zn", [P, B, P]), sb("zT", [P, T]), sb("acc", [P, B, P])
        cent, iota, b2 = sb("cent", [P, E1]), sb("iota1", [P, E1]), sb("t1b2", [E1, P])
        sc, at, hot = sb("sc", [P, B, E1]), sb("at", [P, B, E1]), sb("hot", [P, B, E1])
        top, first, alpha = sb("top", [P, B]), sb("first", [P, B]), sb("alpha", [P, B])
        hotT = sb("hotT", [E1, T])
        w1, w2, eb = sb("w1s", [P, 2, F1]), sb("w2s", [P, 2, FC1, P]), sb("ebs", [P, 2, 2 + FC1])
        hT, r1 = sb("h1T", [P, 2, T]), sb("r1", [P, 2, FC1, HALF])
        layer_norm(k, lambda b: k.xn[:, b, :], zn, zT)
        with nc.Block() as block:
            @block.sync
            def _(sp):
                sp.dma_start(cent[:, :], d["cent"]).then_inc(load.sem, 16)
                sp.dma_start(iota[:, :], d["iota"][:, 0:E1].to_broadcast([P, E1])).then_inc(load.sem, 16)
                sp.dma_start(b2[:, :], d["t1b2"]).then_inc(load.sem, 16)

            @block.tensor
            def _(t):
                t.wait_ge(load.sem, 48)
                for b in range(B):
                    m = t.matmul(ps[:, 0, b * E1:(b + 1) * E1], k.xnT[:, b * P:(b + 1) * P], cent[:, :],
                                 start=True, stop=True)
                m.then_inc(scored.sem, 1)
                t.wait_ge(routed.sem, 1)
                for b in range(B):
                    t.transpose(ps[0:E1, 1 + b // HB, P * (b % HB):P * (b % HB) + P], hot[:, b, :],
                                k.ident[:, :]).then_inc(turned.sem, 1)
                t.wait_ge(hot_out.sem, 2)
                for b in range(B):
                    t.matmul(ps[:, 4 + b // HB, P * (b % HB):P * (b % HB) + P], hotT[:, b * P:(b + 1) * P],
                             b2[:, :], start=True, stop=True).then_inc(b2_made.sem, 1)

            @block.vector
            def _(v):
                v.wait_ge(scored.sem, 1)
                v.tensor_copy(sc[:, :, :], ps[:, 0, 0:B * E1].rearrange("p (b e) -> p b e", b=B))\
                 .then_inc(own_step.sem, 1)
                own_step.base += 1
                v.wait_ge(own_step.sem, own_step.base)
                v.wait_ge(load.sem, 48)
                route(v, own_step, sc[:, :, :], iota[:, :], top[:, :], at[:, :, :], first[:, :], hot[:, :, :])
                v.memset(k.prime2[:, :], 0.0).then_inc(routed.sem, 1)
                for h in range(2):
                    v.wait_ge(b2_made.sem, HB * (h + 1))
                    v.tensor_copy(acc[:, HB * h:HB * h + HB, :],
                                  ps[:, 4 + h, :].rearrange("p (b c) -> p b c", b=HB))

            @block.scalar
            def _(a):
                a.wait_ge(routed.sem, 1)
                a.activation(alpha[:, :], top[:, :], ACT.Sigmoid).then_inc(alpha_out.sem, 1)
                for h in range(2):
                    a.wait_ge(turned.sem, HB * (h + 1))
                    a.activation(hotT[:, h * HALF:(h + 1) * HALF], ps[0:E1, 1 + h, :], ACT.Copy)\
                     .then_inc(hot_out.sem, 1)

        with nc.Block() as block:
            @block.sync
            def _(sp):
                def fetch(e, p, early):
                    if not early:
                        sp.wait_ge(down.sem, 2 * (e - 1))
                    sp.dma_start(w1[:, p, :], d["t1w1"][e]).then_inc(w_in[p].sem, 16)
                    sp.dma_start(w2[:, p], d["t1w2"][e]).then_inc(w_in[p].sem, 16)
                    sp.dma_start(eb[:, p, :], d["t1eb"][e]).then_inc(w_in[p].sem, 16)
                fetch(0, 0, True)
                fetch(1, 1, True)
                with sp.Fori(0, (E1 - 2) // 2) as i:
                    fetch(2 * i + 2, 0, False)
                    fetch(2 * i + 3, 1, False)

            @block.tensor
            def _(t):
                def step(e, p, place):
                    t.wait_ge(w_in[p].sem, 24 * (e - p) + 48)
                    t.wait_ge(hx.sem, e + 1)
                    for h in range(2):
                        for c in range(FC1):
                            if place > 0 or h > 0:
                                r = relu_v if c % 2 else relu_a
                                t.wait_ge(r.sem, 4 * e + 2 * h + c // 2 - 1)
                            t.matmul(ps[:, c, :], w1[:, p, c * P:(c + 1) * P],
                                     hT[:, p, h * HALF:(h + 1) * HALF], start=True, stop=True)\
                             .then_inc(up.sem, 1)
                    for h in range(2):
                        t.wait_ge(relu_a.sem, 4 * e + 2 * h + 2)
                        t.wait_ge(relu_v.sem, 4 * e + 2 * h + 2)
                        if place > 1:
                            t.wait_ge(summed.sem, 8 * (e - 2) + 4 * h + 4)
                        for b in range(HB):
                            for c in range(FC1):
                                m = t.matmul(ps[:, 4 + 2 * p + h, b * P:(b + 1) * P],
                                             r1[:, h, c, b * P:(b + 1) * P], w2[:, p, c, :],
                                             start=(c == 0), stop=(c == FC1 - 1))
                        m.then_inc(down.sem, 1)
                over_batches(t, step)

            @block.scalar
            def _(a):
                def step(e, p, place):
                    for h in range(2):
                        for c in range(0, FC1, 2):
                            a.wait_ge(up.sem, 8 * e + 4 * h + c + 1)
                            if place > 0 and c == 0:
                                a.wait_ge(down.sem, 2 * (e - 1) + h + 1)
                            a.activation(r1[:, h, c, :], ps[:, c, :], ACT.Relu,
                                         bias=eb[:, p, 2 + c:3 + c]).then_inc(relu_a.sem, 1)
                a.activation(k.prime[:, :], k.ones[:, 0:1], ACT.Exp)
                over_batches(a, step)

            @block.vector
            def _(v):
                def inputs(e, p, early):
                    v.wait_ge(w_in[p].sem, 24 * (e - p) + 48)
                    if not early:
                        v.wait_ge(down.sem, 2 * (e - 1))
                    v.tensor_scalar(hT[:, p, :], zT[:, :], eb[:, p, 0:1], eb[:, p, 1:2], ALU.mult, ALU.add)\
                     .then_inc(hx.sem, 1)

                def step(e, p, place):
                    for h in range(2):
                        for c in range(1, FC1, 2):
                            v.wait_ge(up.sem, 8 * e + 4 * h + c + 1)
                            if place > 0 and c == 1:
                                v.wait_ge(down.sem, 2 * (e - 1) + h + 1)
                            v.tensor_scalar(r1[:, h, c, :], ps[:, c, :], eb[:, p, 2 + c:3 + c], 0.0,
                                            ALU.add, ALU.max).then_inc(relu_v.sem, 1)
                    if place < E1 - 1:
                        inputs(e + 1, 1 - p, place == 0)
                    for h in range(2):
                        v.wait_ge(down.sem, 2 * e + h + 1)
                        for b in range(HB * h, HB * h + HB):
                            if place > 0 and b == 0:
                                v.wait_ge(summed.sem, 8 * e)
                            v.scalar_tensor_tensor(
                                out=acc[:, b, :], in0=ps[:, 4 + 2 * p + h, P * (b % HB):P * (b % HB) + P],
                                scalar=hot[:, b, bass.ds(e, 1)], in1=acc[:, b, :], op0=ALU.mult,
                                op1=ALU.add).then_inc(summed.sem, 1)
                inputs(0, 0, True)
                over_batches(v, step)
        finish_gated(k, acc, alpha)


def finish_gated(k, acc, gate):
    nc = k.nc
    gated = k.count("fg_gated")
    with nc.Block() as block:
        @block.vector
        def _(v):
            for b in range(B):
                v.scalar_tensor_tensor(out=k.xn[:, b, :], in0=acc[:, b, :], scalar=gate[:, b:b + 1],
                                       in1=k.xn[:, b, :], op0=ALU.mult, op1=ALU.add).then_inc(gated.sem, 1)
            v.wait_ge(gated.sem, gated.base + B)
            v.tensor_tensor(k.x[:, :, :], k.x[:, :, :], k.xn[:, :, :], ALU.add)
    gated.base += B


def capacity_experts(k, d):
    nc, ps = k.nc, k.ps
    load, own_step, scored, lessed, expd, routed, counted, diag, rows, rows_out = (k.count("ce_" + n) for n in (
        "load", "own_step", "scored", "lessed", "expd", "routed", "counted", "diag", "rows", "rows_out"))
    iota_made, hot_made, sent = k.count("ce_iota"), k.count("ce_hot"), k.count("ce_sent")
    w_in = [k.count("ce_w0_in"), k.count("ce_w1_in")]
    up, silud, hid_made, down, y_out = (k.count("ce_" + n) for n in ("up", "silud", "hid", "down", "y_out"))
    yturned, y_sb_out, back_made, combined = (k.count("ce_" + n) for n in ("yturned", "y_sb", "back", "combined"))
    layer_norm(k, lambda b: k.x[:, b, :], k.xn, k.xnT)
    GB = (SPAN2 * C2)
    with ExitStack() as own:
        def sb(name, shape, dt=F32, ctx=own):
            return k.fresh(ctx, name, shape, dt)
        gate, slot, slot_row = sb("gate", [P, B]), sb("slot_of", [P, B]), sb("slot_row", [P, T])
        bufT, yT = sb("bufT", [P, SLOTS]), sb("yT", [P, SLOTS])
        mine = sb("mine", [P, SCH])
        with ExitStack() as early:
            rw, iota, tri = sb("rw", [P, E2], ctx=early), sb("iota2", [P, E2], ctx=early), sb("tri", [P, P], ctx=early)
            slots_i, slots_f = sb("slots_i", [P, SLOTS], I32, early), sb("slots_f", [P, SLOTS], ctx=early)
            mine_i = sb("mine_i", [P, SCH], I32, early)
            pr, at, hot = (sb(n, [P, B, E2], ctx=early) for n in ("pr", "at2", "hot2"))
            base, dg = sb("base", [P, B, E2], ctx=early), sb("dg", [P, B, P], ctx=early)
            top, rsum, first, pos, eid, over = (sb(n, [P, B], ctx=early) for n in (
                "top2", "rsum", "first2", "pos", "eid", "over"))
            send = sb("send", [P, B, SLOTS], ctx=early)
            with nc.Block() as block:
                @block.sync
                def _(sp):
                    sp.dma_start(rw[:, :], d["rw"]).then_inc(load.sem, 16)
                    sp.dma_start(iota[:, :], d["iota"].to_broadcast([P, E2])).then_inc(load.sem, 16)

                @block.gpsimd
                def _(g):
                    g.memset(tri[:, :], 1.0).then_inc(iota_made.sem, 1)
                    g.iota(slots_i[:, :], pattern=[[1, SLOTS]], base=0, channel_multiplier=0)\
                     .then_inc(iota_made.sem, 1)
                    g.iota(mine_i[:, :], pattern=[[P, SCH]], base=0, channel_multiplier=1)\
                     .then_inc(iota_made.sem, 1)
                    g.memset(base[:, 0, :], 0.0).then_inc(iota_made.sem, 1)
                    g.wait_ge(iota_made.sem, 4)
                    g.affine_select(out=tri[:, :], in_=tri[:, :], compare_op=ALU.is_gt, fill=0.0, base=0,
                                    pattern=[[1, P]], channel_multiplier=-1).then_inc(iota_made.sem, 1)

                @block.tensor
                def _(t):
                    t.wait_ge(load.sem, 32)
                    for b in range(B):
                        m = t.matmul(ps[:, 0, b * E2:(b + 1) * E2], k.xnT[:, b * P:(b + 1) * P], rw[:, :],
                                     start=True, stop=True)
                    m.then_inc(scored.sem, 1)
                    t.wait_ge(iota_made.sem, 5)
                    t.wait_ge(routed.sem, 1)
                    flat = hot[:, :, :].rearrange("p b e -> p (b e)")
                    t.matmul(ps[:, 1, 0:B * E2], tri[:, :], flat, start=True, stop=True).then_inc(counted.sem, 1)
                    t.matmul(ps[:, 2, 0:B * E2], k.ones[:, 0:P], flat, start=True, stop=True)\
                     .then_inc(counted.sem, 1)
                    for b in range(B):
                        t.wait_ge(diag.sem, b + 1)
                        t.matmul(ps[:, 3 + b // HB, P * (b % HB):P * (b % HB) + P], k.ones[:, 0:P],
                                 dg[:, b, :], start=True, stop=True).then_inc(rows.sem, 1)
                    for n, (lo, hi) in enumerate(((0, 512), (512, 1024), (1024, SLOTS))):
                        for b in range(B):
                            t.wait_ge(hot_made.sem, b + 1)
                            m = t.matmul(ps[:, 5 + n, 0:hi - lo], k.xn[:, b, :], send[:, b, lo:hi],
                                         start=(b == 0), stop=(b == B - 1))
                        m.then_inc(sent.sem, 1)

                @block.scalar
                def _(a):
                    a.wait_ge(lessed.sem, 1)
                    a.activation(pr[:, :, :], pr[:, :, :], ACT.Exp).then_inc(expd.sem, 1)
                    for h in range(2):
                        a.wait_ge(rows.sem, HB * (h + 1))
                        a.activation(slot_row[:, h * HALF:(h + 1) * HALF], ps[:, 3 + h, :], ACT.Copy)\
                         .then_inc(rows_out.sem, 1)
                    for n, (lo, hi) in enumerate(((0, 512), (512, 1024), (1024, SLOTS))):
                        a.wait_ge(sent.sem, n + 1)
                        a.activation(bufT[:, lo:hi], ps[:, 5 + n, 0:hi - lo], ACT.Copy)

                @block.vector
                def _(v):
                    def then(m):
                        m.then_inc(own_step.sem, 1)
                        own_step.base += 1
                        v.wait_ge(own_step.sem, own_step.base)
                    v.wait_ge(iota_made.sem, 4)
                    v.tensor_copy(slots_f[:, :], slots_i[:, :])
                    v.tensor_copy(mine[:, :], mine_i[:, :])
                    v.wait_ge(scored.sem, 1)
                    then(v.tensor_reduce(top[:, :], ps[:, 0, 0:B * E2].rearrange("p (b e) -> p b e", b=B),
                                         AX.X, ALU.max))
                    v.tensor_tensor(pr[:, :, :], ps[:, 0, 0:B * E2].rearrange("p (b e) -> p b e", b=B),
                                    spread(top[:, :], E2), ALU.subtract).then_inc(lessed.sem, 1)
                    v.wait_ge(expd.sem, 1)
                    then(v.tensor_reduce(rsum[:, :], pr[:, :, :], AX.X, ALU.add))
                    then(v.reciprocal(rsum[:, :], rsum[:, :]))
                    then(v.tensor_tensor(pr[:, :, :], pr[:, :, :], spread(rsum[:, :], E2), ALU.mult))
                    v.wait_ge(load.sem, 32)
                    route(v, own_step, pr[:, :, :], iota[:, :], gate[:, :], at[:, :, :], first[:, :],
                          hot[:, :, :])
                    v.memset(k.prime2[:, :], 0.0).then_inc(routed.sem, 1)
                    v.wait_ge(counted.sem, 2)
                    for b in range(1, B):
                        then(v.tensor_tensor(base[:, b, :], base[:, b - 1, :],
                                             ps[:, 2, (b - 1) * E2:b * E2], ALU.add))
                    then(v.tensor_tensor(base[:, :, :], base[:, :, :],
                                         ps[:, 1, 0:B * E2].rearrange("p (b e) -> p b e", b=B), ALU.add))
                    then(v.tensor_tensor(base[:, :, :], base[:, :, :], hot[:, :, :], ALU.mult))
                    then(v.tensor_reduce(pos[:, :], base[:, :, :], AX.X, ALU.add))
                    then(v.tensor_scalar(eid[:, :], first[:, :], 64.0, float(C2), ALU.add, ALU.mult))
                    then(v.tensor_scalar(over[:, :], pos[:, :], float(C2), 4.0 * SLOTS, ALU.is_ge, ALU.mult))
                    then(v.tensor_tensor(slot[:, :], pos[:, :], eid[:, :], ALU.add))
                    then(v.tensor_tensor(slot[:, :], slot[:, :], over[:, :], ALU.add))
                    for b in range(B):
                        v.tensor_scalar(dg[:, b, :], k.ident[:, :], slot[:, b:b + 1], None, ALU.mult)\
                         .then_inc(diag.sem, 1)
                    for b in range(B):
                        v.tensor_scalar(send[:, b, :], slots_f[:, :], slot[:, b:b + 1], None, ALU.is_equal)\
                         .then_inc(hot_made.sem, 1)

        back = sb("back", [P, SCH, T])
        w = sb("w2x", [P, 2, 3, SPAN2, P])
        sg, hid = sb("sg", [P, 2, GB]), sb("hid", [P, 2, GB])
        ysl = sb("ysl", [P, SCH, P])
        with nc.Block() as block:
            @block.sync
            def _(sp):
                def fetch(s, p, early):
                    if not early:
                        sp.wait_ge(down.sem, s - 1)
                    sp.dma_start(w[:, p], d["w2x"][s]).then_inc(w_in[p].sem, 16)
                fetch(0, 0, True)
                fetch(1, 1, True)
                with sp.Fori(0, (B - 2) // 2) as i:
                    fetch(2 * i + 2, 0, False)
                    fetch(2 * i + 3, 1, False)

            @block.tensor
            def _(t):
                def ups(s, p, early):
                    t.wait_ge(w_in[p].sem, 8 * (s - p) + 16)
                    if not early:
                        t.wait_ge(hid_made.sem, s - 1)
                    for q in range(SPAN2):
                        for n in range(2):
                            t.matmul(ps[:, 2 * p + n, q * C2:(q + 1) * C2], w[:, p, n, q, :],
                                     bufT[:, bass.ds(s * GB + q * C2, C2)], start=True, stop=True)\
                             .then_inc(up.sem, 1)

                def downs(s, p, place):
                    t.wait_ge(hid_made.sem, s + 1)
                    if place > 1:
                        t.wait_ge(y_out.sem, s - 1)
                    for q in range(SPAN2):
                        m = t.matmul(ps[:, 4 + p, q * C2:(q + 1) * C2], w[:, p, 2, q, :],
                                     hid[:, p, q * C2:(q + 1) * C2], start=True, stop=True)
                    m.then_inc(down.sem, 1)

                def step(s, p, place):
                    if place < B - 1:
                        ups(s + 1, 1 - p, place == 0)
                    downs(s, p, place)
                ups(0, 0, True)
                over_batches(t, step)

            @block.scalar
            def _(a):
                def silu(s, p):
                    a.wait_ge(up.sem, 2 * SPAN2 * (s + 1))
                    a.activation(sg[:, p, :], ps[:, 2 * p, 0:GB], ACT.Silu).then_inc(silud.sem, 1)

                def step(s, p, place):
                    if place < B - 1:
                        silu(s + 1, 1 - p)
                    a.wait_ge(down.sem, s + 1)
                    a.activation(yT[:, bass.ds(s * GB, GB)], ps[:, 4 + p, 0:GB], ACT.Copy).then_inc(y_out.sem, 1)
                a.activation(k.prime[:, :], k.ones[:, 0:1], ACT.Silu)
                silu(0, 0)
                over_batches(a, step)

            @block.vector
            def _(v):
                def step(s, p, place):
                    v.wait_ge(silud.sem, s + 1)
                    if place > 1:
                        v.wait_ge(down.sem, s - 1)
                    v.tensor_tensor(hid[:, p, :], sg[:, p, :], ps[:, 2 * p + 1, 0:GB], ALU.mult)\
                     .then_inc(hid_made.sem, 1)
                over_batches(v, step)
                for c in range(SCH):
                    v.tensor_scalar(back[:, c, :], slot_row[:, :], mine[:, c:c + 1], None, ALU.is_equal)

        with nc.Block() as block:
            @block.tensor
            def _(t):
                for c in range(SCH):
                    t.transpose(ps[:, c // 4, P * (c % 4):P * (c % 4) + P], yT[:, c * P:(c + 1) * P],
                                k.ident[:, :]).then_inc(yturned.sem, 1)
                t.wait_ge(y_sb_out.sem, 3)
                for b in range(B):
                    for c in range(SCH):
                        m = t.matmul(ps[:, 4 + b // 2, P * (b % 2):P * (b % 2) + P],
                                     back[:, c, b * P:(b + 1) * P], ysl[:, c, :],
                                     start=(c == 0), stop=(c == SCH - 1))
                    m.then_inc(back_made.sem, 1)

            @block.scalar
            def _(a):
                for n, (lo, hi) in enumerate(((0, 4), (4, 8), (8, SCH))):
                    a.wait_ge(yturned.sem, hi)
                    a.activation(ysl[:, lo:hi, :], ps[:, n, 0:(hi - lo) * P].rearrange("p (c h) -> p c h", h=P),
                                 ACT.Copy).then_inc(y_sb_out.sem, 1)

            @block.vector
            def _(v):
                for b in range(B):
                    v.wait_ge(back_made.sem, 2 * (b // 2) + 2)
                    v.scalar_tensor_tensor(out=k.xn[:, b, :], in0=ps[:, 4 + b // 2, P * (b % 2):P * (b % 2) + P],
                                           scalar=gate[:, b:b + 1], in1=k.xn[:, b, :], op0=ALU.mult,
                                           op1=ALU.add).then_inc(combined.sem, 1)
                    v.wait_ge(combined.sem, b + 1)
                    v.tensor_tensor(k.x[:, b, :], k.x[:, b, :], k.xn[:, b, :], ALU.add)


def top2_experts(k, d):
    nc, ps = k.nc, k.ps
    load, own_step, scored, sig, routed, cturned, cT_out, mixed, up, silud, hid_made, out = (
        k.count("t2_" + n) for n in ("load", "own_step", "scored", "sig", "routed", "cturned", "cT_out",
                                     "mixed", "up", "silud", "hid", "out"))
    layer_norm(k, lambda b: k.x[:, b, :], k.xn, k.xnT)
    units = [(h, c) for h in range(2) for c in range(CH3)]
    with ExitStack() as own:
        def sb(name, shape):
            return k.fresh(own, name, shape)
        gw, iota, sel = sb("gw", [P, E3]), sb("iota3", [P, E3]), sb("sel", [E3, CH3 - 1, P])
        wg, wu, wd = (sb(n, [P, CH3, P]) for n in ("wg3", "wu3", "wd3"))
        sc, at, hot1, hot2, mix = (sb(n, [P, B, E3]) for n in ("sc3", "at3", "hot31", "hot32", "mix"))
        top1, top2, first, tot = (sb(n, [P, B]) for n in ("top31", "top32", "first3", "tot"))
        cT, sg, uu, hid = sb("cT", [E3, T]), sb("sg3", [P, 2, HALF]), sb("uu", [P, 2, HALF]), \
            sb("hid3", [P, 2, CH3, HALF])
        with nc.Block() as block:
            @block.sync
            def _(sp):
                for dst, src in ((gw, "gw"), (sel, "sel"), (wg, "wg3"), (wu, "wu3"), (wd, "wd3")):
                    sp.dma_start(dst[:], d[src]).then_inc(load.sem, 16)
                sp.dma_start(iota[:, :], d["iota"][:, 0:E3].to_broadcast([P, E3])).then_inc(load.sem, 16)

            @block.tensor
            def _(t):
                t.wait_ge(load.sem, 96)
                for b in range(B):
                    m = t.matmul(ps[:, 0, b * E3:(b + 1) * E3], k.xnT[:, b * P:(b + 1) * P], gw[:, :],
                                 start=True, stop=True)
                m.then_inc(scored.sem, 1)
                t.wait_ge(routed.sem, 1)
                for b in range(B):
                    t.transpose(ps[0:E3, 1 + b // HB, P * (b % HB):P * (b % HB) + P], mix[:, b, :],
                                k.ident[:, :]).then_inc(cturned.sem, 1)

            @block.scalar
            def _(a):
                a.wait_ge(scored.sem, 1)
                a.activation(sc[:, :, :], ps[:, 0, 0:B * E3].rearrange("p (b e) -> p b e", b=B), ACT.Sigmoid)\
                 .then_inc(sig.sem, 1)
                for h in range(2):
                    a.wait_ge(cturned.sem, HB * (h + 1))
                    a.activation(cT[:, h * HALF:(h + 1) * HALF], ps[0:E3, 1 + h, :], ACT.Copy)\
                     .then_inc(cT_out.sem, 1)

            @block.vector
            def _(v):
                def then(m):
                    m.then_inc(own_step.sem, 1)
                    own_step.base += 1
                    v.wait_ge(own_step.sem, own_step.base)
                v.wait_ge(load.sem, 96)
                v.wait_ge(sig.sem, 1)
                route(v, own_step, sc[:, :, :], iota[:, :], top1[:, :], at[:, :, :], first[:, :], hot1[:, :, :])
                then(v.scalar_tensor_tensor(out=sc[:, :, :], in0=hot1[:, :, :], scalar=-4.0, in1=sc[:, :, :],
                                            op0=ALU.mult, op1=ALU.add))
                route(v, own_step, sc[:, :, :], iota[:, :], top2[:, :], at[:, :, :], first[:, :], hot2[:, :, :])
                then(v.tensor_tensor(tot[:, :], top1[:, :], top2[:, :], ALU.add))
                then(v.tensor_scalar(tot[:, :], tot[:, :], 1e-20, None, ALU.add))
                then(v.reciprocal(tot[:, :], tot[:, :]))
                then(v.tensor_tensor(hot1[:, :, :], hot1[:, :, :], spread(top1[:, :], E3), ALU.mult))
                then(v.tensor_tensor(hot2[:, :, :], hot2[:, :, :], spread(top2[:, :], E3), ALU.mult))
                then(v.tensor_tensor(mix[:, :, :], hot1[:, :, :], hot2[:, :, :], ALU.add))
                then(v.tensor_scalar(tot[:, :], tot[:, :], ROUTED_SCALE, None, ALU.mult))
                v.tensor_tensor(mix[:, :, :], mix[:, :, :], spread(tot[:, :], E3), ALU.mult)\
                 .then_inc(routed.sem, 1)

        with nc.Block() as block:
            @block.tensor
            def _(t):
                def ups(n):
                    h, c = units[n]
                    if n >= 2:
                        t.wait_ge(hid_made.sem, n - 1)
                    cols = slice(h * HALF, (h + 1) * HALF)
                    bank = 3 * (n % 2)
                    t.matmul(ps[:, bank, :], wg[:, c, :], k.xnT[:, cols], start=True, stop=True)\
                     .then_inc(up.sem, 1)
                    m = t.matmul(ps[:, bank + 1, :], wu[:, c, :], k.xnT[:, cols], start=True, stop=True)
                    if c < CH3 - 1:
                        m = t.matmul(ps[:, bank + 2, :], sel[:, c, :], cT[:, cols], start=True, stop=True)
                    m.then_inc(up.sem, 1)

                def downs(h):
                    t.wait_ge(hid_made.sem, CH3 * (h + 1))
                    for b in range(HB):
                        for c in range(CH3):
                            m = t.matmul(ps[:, 6 + h, b * P:(b + 1) * P], hid[:, h, c, b * P:(b + 1) * P],
                                         wd[:, c, :], start=(c == 0), stop=(c == CH3 - 1))
                    m.then_inc(out.sem, 1)
                for n in range(CH3 + 1):
                    ups(n)
                downs(0)
                for n in range(CH3 + 1, 2 * CH3):
                    ups(n)
                downs(1)

            @block.scalar
            def _(a):
                for n in range(2 * CH3):
                    a.wait_ge(up.sem, 2 * n + 1)
                    if n >= 2:
                        a.wait_ge(mixed.sem, n - 1)
                    a.activation(sg[:, n % 2, :], ps[:, 3 * (n % 2), :], ACT.Silu).then_inc(silud.sem, 1)

            @block.vector
            def _(v):
                for n, (h, c) in enumerate(units):
                    v.wait_ge(silud.sem, n + 1)
                    v.wait_ge(up.sem, 2 * n + 2)
                    bank = 3 * (n % 2)
                    if c < CH3 - 1:
                        v.tensor_tensor(uu[:, n % 2, :], sg[:, n % 2, :], ps[:, bank + 1, :], ALU.mult)\
                         .then_inc(mixed.sem, 1)
                        v.wait_ge(mixed.sem, n + 1)
                        v.tensor_tensor(hid[:, h, c, :], uu[:, n % 2, :], ps[:, bank + 2, :], ALU.mult)\
                         .then_inc(hid_made.sem, 1)
                    else:
                        v.tensor_tensor(hid[:, h, c, :], sg[:, n % 2, :], ps[:, bank + 1, :], ALU.mult)\
                         .then_inc(hid_made.sem, 1)
                        v.memset(k.prime2[:, :], 0.0).then_inc(mixed.sem, 1)
                for h in range(2):
                    v.wait_ge(out.sem, h + 1)
                    v.tensor_tensor(k.x[:, HB * h:HB * h + HB, :], k.x[:, HB * h:HB * h + HB, :],
                                    ps[:, 6 + h, :].rearrange("p (b c) -> p b c", b=HB), ALU.add)


def store(k, out):
    done = k.count("stored")
    with k.nc.Block() as block:
        @block.sync
        def _(sp):
            sp.dma_start(out.rearrange("b t d -> t b d"), k.x[:, :, :]).then_inc(done.sem, 16)
            sp.wait_ge(done.sem, 16)


def build(nc, d, out, stages=8):
    with ExitStack() as ctx:
        k = Core(nc, ctx)
        k.ps = ctx.enter_context(nc.psum_tensor("ps", [P, 8, 512], F32))
        setup(k, d)
        cross_attention(k, 0)
        if stages > 1:
            local_transformer(k, d)
        if stages > 2:
            cross_attention(k, 1)
        if stages > 3:
            top1_experts(k, d)
        if stages > 4:
            cross_attention(k, 2)
        if stages > 5:
            capacity_experts(k, d)
        if stages > 6:
            cross_attention(k, 3)
        if stages > 7:
            top2_experts(k, d)
        store(k, out)




def heads_apart(np, m):
    out = np.zeros(m.shape[:-1] + (4, 4, 32), m.dtype)
    out[..., 0:XD] = m.reshape(m.shape[:-1] + (4, 4, XD))
    return out.reshape(m.shape[:-1] + (4 * P,))


def per_head(np, w):
    out = np.zeros((P, P), w.dtype)
    for h in range(XH):
        out[h * XD:(h + 1) * XD, h * XD:(h + 1) * XD] = w
    return out


def layouts(np, i):
    f = np.float32
    c = np.ascontiguousarray
    zero = np.zeros(P, f)
    d = {}
    d["x"] = c(i["x"].transpose(1, 0, 2))
    d["ctxT"] = c(i["ctx_1024"].transpose(2, 0, 1).reshape(P, T))
    wq = [per_head(np, i["L0_xattn_Wq"].T), i["L1_xattn_Wq"].T, i["L2_xattn_Wq"], per_head(np, i["L3_xattn_Wq"])]
    wk = [per_head(np, i["L0_xattn_Wk"].T), i["L1_xattn_Wk"].T, i["L2_xattn_Wk"], per_head(np, i["L3_xattn_Wk"])]
    wv = [per_head(np, i["L0_xattn_Wv"].T), i["L1_xattn_Wv"].T, i["L2_xattn_Wv"], per_head(np, i["L3_xattn_Wv"])]
    d["wq"] = c(np.stack([heads_apart(np, w) for w in wq], 1))
    d["wk"] = c(np.stack([heads_apart(np, w) for w in wk], 1))
    d["wv"] = c(np.concatenate(wv, 1))
    d["bv"] = np.concatenate([zero, i["L1_xattn_bv"], i["L2_xattn_bv"], zero])[None]
    bq = [heads_apart(np, v) for v in (zero, i["L1_xattn_bq"], i["L2_xattn_bq"], zero)]
    bk = [heads_apart(np, v) for v in (zero, i["L1_xattn_bk"], i["L2_xattn_bk"], zero)]
    d["bqk"] = c(np.stack([np.stack(bq), np.stack(bk)], 1).reshape(NX, 2, 4, P).transpose(3, 0, 1, 2))
    d["wo"] = c(np.stack([i["L0_xattn_Wo"].T, i["L1_xattn_Wo"].T, i["L2_xattn_Wo"]], 1))
    d["bo"] = np.stack([i["L0_xattn_bo"], i["L1_xattn_bo"], i["L2_xattn_bo"]])[None]
    d["keys"] = i["mask_Bx1x1xS2_if1"].reshape(1, B, P)
    d["mask1"] = i["mask_1x1xSxS2_if1"].reshape(P, P)
    d["mask3"] = i["mask_1x1xSxS2_fk0"].reshape(P, P)
    d["wqkv"] = c(i["L0_ffn_wqkv"].reshape(LAYERS, P, 3, LH * LD).transpose(1, 0, 2, 3))
    d["lwo"] = c(i["L0_ffn_wo"].reshape(LAYERS, 4, P, P).transpose(2, 0, 1, 3))
    d["w1"] = c(i["L0_ffn_w1"].transpose(1, 0, 2))
    nch = len(HCH)
    w2 = np.zeros((LAYERS, nch * P, P), f)
    w2[:, 0:HID] = i["L0_ffn_w2"]
    d["w2"] = c(w2.reshape(LAYERS, nch, P, P).transpose(2, 0, 1, 3))
    b1 = np.zeros((LAYERS, 2, nch * P), f)
    b1[:, :, 0:HID] = i["L0_ffn_b1"].reshape(LAYERS, 2, HID)
    d["b1"] = c(b1.reshape(LAYERS, 2, nch, P).transpose(3, 0, 1, 2))
    d["b2"] = i["L0_ffn_b2"][None]
    d["gb"] = c(np.stack([i["L0_ffn_ln_g"], i["L0_ffn_ln_b"]], 1).transpose(2, 0, 1))
    d["qks"] = c(np.stack([i["L0_ffn_q_scale"], i["L0_ffn_k_scale"]], 1)[None])
    half = np.arange(0, LD, 2, dtype=f)
    t = np.arange(P, dtype=f)
    ang = t[:, None] * (f(1.0) / f(10000.0) ** (half / f(LD)))[None]
    ang = np.concatenate([ang, ang], 1)
    base = (half + f(0.4 * LD)) / f(1.4 * LD)
    sc = base[None] ** ((t - P // 2) / f(WINDOW // 2))[:, None]
    sc = np.concatenate([sc, sc], 1)
    cos, sin = np.cos(ang), np.sin(ang)
    sign = np.where(np.arange(LD) < LD // 2, f(-1), f(1))
    d["rotc"] = c(np.stack([cos * sc, cos / sc], 1).astype(f))
    d["rots"] = c(np.stack([sin * sc * sign, sin / sc * sign], 1).astype(f))
    d["cent"] = c(i["L1_ffn_centroids"].T)
    d["t1w1"] = c(i["L1_ffn_W1"].transpose(0, 2, 1))
    d["t1w2"] = c(i["L1_ffn_W2"].transpose(0, 2, 1).reshape(E1, FC1, P, P).transpose(0, 2, 1, 3))
    d["t1eb"] = c(np.concatenate([i["L1_ffn_gamma"][:, :, None], i["L1_ffn_beta"][:, :, None],
                                  i["L1_ffn_b1"].reshape(E1, FC1, P).transpose(0, 2, 1)], 2))
    d["t1b2"] = i["L1_ffn_b2"]
    d["iota"] = np.arange(E2, dtype=f)[None]
    d["rw"] = i["L2_ffn_w_router"]
    w = np.stack([i["L2_ffn_w_gate"], i["L2_ffn_w_up"], i["L2_ffn_w_down"]])
    d["w2x"] = c(w.reshape(3, E2 // SPAN2, SPAN2, P, P).transpose(1, 3, 0, 2, 4))
    d["gw"] = c(i["L3_ffn_gate_weight"].T)

    def chunks(routed, shared):
        return c(np.concatenate([routed.reshape(E3 * I3, P), shared]).reshape(CH3, P, P).transpose(2, 0, 1))
    d["wg3"] = chunks(i["L3_ffn_w_gate"], i["L3_ffn_ws_gate"])
    d["wu3"] = chunks(i["L3_ffn_w_up"], i["L3_ffn_ws_up"])
    down = np.concatenate([i["L3_ffn_w_down"].transpose(0, 2, 1).reshape(E3 * I3, P), i["L3_ffn_ws_down"].T])
    d["wd3"] = c(down.reshape(CH3, P, P).transpose(1, 0, 2))
    d["sel"] = c(np.repeat(np.eye(E3, dtype=f), I3, 1).reshape(E3, CH3 - 1, P))
    return d


STAGES = 8


def kernel(**inputs):
    import numpy as np
    import concourse.bacc as _bacc
    from concourse.bass_utils import run_bass_kernel_spmd as _run

    nc = _bacc.Bacc("TRN2", target_bir_lowering=False, num_devices=1)
    arrays = {"in_" + n: np.ascontiguousarray(a) for n, a in
              layouts(np, {n: np.asarray(a) for n, a in inputs.items()}).items()}
    d = {n[3:]: nc.dram_tensor(n, a.shape, mybir.dt.from_np(a.dtype), kind="ExternalInput").ap()
         for n, a in arrays.items()}
    out = nc.dram_tensor("out_0", (B, P, P), F32, kind="ExternalOutput").ap()
    build(nc, d, out, STAGES)
    return _run(nc, [arrays], core_ids=[0]).results[0]["out_0"]
```

```python
from contextlib import ExitStack

import concourse.bass as bass
from concourse import mybir

ALU = mybir.AluOpType
ACT = mybir.ActivationFunctionType
AX = mybir.AxisListType
F32 = mybir.dt.float32
I32 = mybir.dt.int32

B = 8
P = 128
T = B * P
HB = B // 2
HALF = T // 2
NX = 4
XH, XD = 16, 8
LH, LD = 8, 64
LAYERS = 2
WINDOW = 64
HID = 341
HCH = [(0, 128), (128, 128), (256, HID - 256)]
E1, F1 = 8, 512
FC1 = F1 // P
E2, C2 = 32, 40
SLOTS = E2 * C2
SCH = SLOTS // P
SPAN2 = 4
SPANS = E2 // SPAN2
SPANS_FIRST = 2
SPANS_AHEAD = SPANS_FIRST + (B - 2) // 2
E3, I3 = 8, 64
CH3 = E3 * I3 // P + 1
ROUTED_SCALE = 2.5
EPS = 1e-5
NEG = -float(2 ** 100)
LOWEST = -3.0e38


class Count:

    def __init__(self, sem):
        self.sem = sem
        self.base = 0


class Core:

    def __init__(self, nc, ctx):
        self.nc = nc
        self.ctx = ctx
        self.counts = {}
        self.made = {}

    def sb(self, name, shape, dt=F32):
        return self.ctx.enter_context(self.nc.sbuf_tensor(name, shape, dt))

    def fresh(self, ctx, name, shape, dt=F32):
        self.made[name] = self.made.get(name, 0) + 1
        return ctx.enter_context(self.nc.sbuf_tensor(f"{name}_{self.made[name]}", shape, dt))

    def count(self, name):
        if name not in self.counts:
            self.counts[name] = Count(self.ctx.enter_context(self.nc.semaphore(name)))
        return self.counts[name]


def spread(ap, n):
    return ap.unsqueeze(len(ap.shape)).to_broadcast(list(ap.shape) + [n])


def shared_memory(k):
    k.x, k.xn = k.sb("x", [P, B, P]), k.sb("xn", [P, B, P])
    k.xnT, k.ctxT = k.sb("xnT", [P, T]), k.sb("ctxT", [P, T])
    k.st, k.mv = k.sb("st", [P, B, 6]), k.sb("mv", [P, B, 2])
    k.std, k.rs = k.sb("std", [P, B]), k.sb("rs", [P, B])
    k.ident, k.ones, k.zeros = k.sb("ident", [P, P]), k.sb("ones", [P, HALF]), k.sb("zeros", [P, P])
    k.band, k.mask1, k.mask3 = k.sb("band", [P, P]), k.sb("mask1", [P, P]), k.sb("mask3", [P, P])
    k.negkeys = k.sb("negkeys", [P, B, P])
    k.wq, k.wk = k.sb("wq", [P, NX, 4 * P]), k.sb("wk", [P, NX, 4 * P])
    k.bqk, k.wo, k.bo = k.sb("bqk", [P, NX, 2, 4]), k.sb("wo", [P, 3, P]), k.sb("bo", [P, 3, P])
    k.v1 = k.sb("v1", [P, B, NX, XH, XD + 1])
    k.work = k.sb("work", [P, 12 * T])
    k.qkT = k.work[:, 0:8 * T].rearrange("p (b w c t) -> p b w c t", b=B, w=2, c=4)
    k.kslot_flat = k.work[:, 8 * T:12 * T]
    k.kslot = k.kslot_flat.rearrange("p (s c r t) -> p s c r t", s=2, c=4, r=4)
    k.qslot, k.mslot = k.sb("qslot", [P, 2, 4, P]), k.sb("mslot", [P, 2, P])
    k.cent, k.t1b2 = k.sb("cent", [P, E1]), k.sb("t1b2s", [E1, P])
    k.rw, k.gw, k.sel = k.sb("rw", [P, E2]), k.sb("gw", [P, E3]), k.sb("sel", [E3, CH3 - 1, P])
    k.iota = k.sb("iota", [P, E2])
    k.eps = k.sb("eps", [P, 1])
    k.prime = k.sb("prime", [P, 1])


def setup(k, d):
    nc = k.nc
    load_v, load, made = (k.count(n) for n in ("su_load_v", "su_load", "su_made"))
    with ExitStack() as own:
        def sb(name, shape, dt=F32):
            return k.fresh(own, name, shape, dt)
        wv, bv = sb("wv", [P, NX * P]), sb("bv", [P, NX * P])
        keys_i, mask1_i = sb("keys_i", [P, B, P], I32), sb("mask1_i", [P, P], I32)
        vready = k.count("su_v")
        LOADS = 15
        with nc.Block() as block:
            @block.sync
            def _(sp):
                sp.dma_start(k.ctxT[:, 0:HALF], d["ctxT"][:, 0:HALF]).then_inc(load_v.sem, 16)
                sp.dma_start(bv[:, :], d["bv"].to_broadcast([P, NX * P])).then_inc(load_v.sem, 16)
                sp.dma_start(k.x[:, :, :], d["x"]).then_inc(load.sem, 16)
                sp.dma_start(keys_i[:, :, :], d["keys"].to_broadcast([P, B, P])).then_inc(load.sem, 16)
                sp.dma_start(mask1_i[:, :], d["mask1"]).then_inc(load.sem, 16)
                sp.dma_start(k.mask3[:, :], d["mask3"]).then_inc(load.sem, 16)
                sp.dma_start(k.bqk[:, :, :, :], d["bqk"]).then_inc(load.sem, 16)
                sp.dma_start(k.bo[:, :, :], d["bo"].to_broadcast([P, 3, P])).then_inc(load.sem, 16)
                sp.dma_start(k.cent[:, :], d["cent"]).then_inc(load.sem, 16)
                sp.dma_start(k.t1b2[:, :], d["t1b2"]).then_inc(load.sem, 16)
                sp.dma_start(k.rw[:, :], d["rw"]).then_inc(load.sem, 16)
                sp.dma_start(k.gw[:, :], d["gw"]).then_inc(load.sem, 16)
                sp.dma_start(k.sel[:, :, :], d["sel"]).then_inc(load.sem, 16)
                sp.dma_start(k.iota[:, :], d["iota"].to_broadcast([P, E2])).then_inc(load.sem, 16)
                sp.wait_ge(load.sem, 16 * LOADS)

            @block.scalar
            def _(a):
                a.dma_start(wv[:, :], d["wv"]).then_inc(load_v.sem, 16)
                a.dma_start(k.ctxT[:, HALF:T], d["ctxT"][:, HALF:T]).then_inc(load_v.sem, 16)
                a.dma_start(k.wk[:, :, :], d["wk"]).then_inc(load.sem, 16)
                a.dma_start(k.wq[:, :, :], d["wq"]).then_inc(load.sem, 16)
                a.dma_start(k.wo[:, :, :], d["wo"]).then_inc(load.sem, 16)

            @block.gpsimd
            def _(g):
                g.memset(k.ident[:, :], 0.0).then_inc(made.sem, 1)
                g.memset(k.band[:, :], 0.0).then_inc(made.sem, 1)
                g.memset(k.ones[:, :], 1.0).then_inc(made.sem, 1)
                g.memset(k.zeros[:, :], 0.0).then_inc(made.sem, 1)
                g.memset(k.v1[:, :, :, :, XD:XD + 1], 1.0).then_inc(made.sem, 1)
                g.wait_ge(made.sem, 5)
                g.affine_select(out=k.ident[:, :], in_=k.ident[:, :], compare_op=ALU.not_equal, fill=1.0,
                                base=0, pattern=[[-1, P]], channel_multiplier=1).then_inc(made.sem, 1)
                g.affine_select(out=k.band[:, :], in_=k.band[:, :], compare_op=ALU.is_ge, fill=NEG,
                                base=0, pattern=[[-1, P]], channel_multiplier=1).then_inc(made.sem, 1)
                g.wait_ge(made.sem, 7)
                g.affine_select(out=k.band[:, :], in_=k.band[:, :], compare_op=ALU.is_ge, fill=NEG,
                                base=WINDOW, pattern=[[1, P]], channel_multiplier=-1).then_inc(made.sem, 1)

            @block.vector
            def _(v):
                v.memset(k.eps[:, :], EPS)
                v.memset(k.kslot_flat, 0.0)
                v.wait_ge(load_v.sem, 64)
                for b in range(B):
                    v.wait_ge(vready.sem, b + 1)
                    v.tensor_tensor(k.v1[:, b, :, :, 0:XD],
                                    k.ps[:, b, :].rearrange("p (a h e) -> p a h e", a=NX, e=XD),
                                    bv[:, :].rearrange("p (a h e) -> p a h e", a=NX, e=XD), ALU.add)
                v.wait_ge(load.sem, 16 * LOADS)
                v.tensor_scalar(k.negkeys[:, :, :], keys_i[:, :, :], 0.0, NEG, ALU.is_equal, ALU.mult)
                v.tensor_scalar(k.mask1[:, :], mask1_i[:, :], 0.0, NEG, ALU.is_equal, ALU.mult)

            @block.tensor
            def _(t):
                t.wait_ge(load_v.sem, 64)
                for b in range(B):
                    t.matmul(k.ps[:, b, :], k.ctxT[:, b * P:(b + 1) * P], wv[:, :], start=True, stop=True)\
                     .then_inc(vready.sem, 1)


def layer_norm(k, src, dst, dst_t, gain=None, shift=None, keys_of=None, sync=None,
               pool=None, counted=False, shifted=False, bring=None, first=None, last=None,
               slots=None):
    nc, ps = k.nc, k.ps
    stats, var, std, rstd, norm, turned, out, kready, kout, brought = (k.count("ln_" + n) for n in (
        "stats", "var", "std", "rstd", "norm", "turned", "out", "kready", "kout", "brought"))
    qready, qout_a, qout_v = k.count("ln_qready"), k.count("ln_qout_a"), k.count("ln_qout_v")
    units = [(g, h) for g in range(4) for h in range(2)] if keys_of is not None else []
    qunits = [(g, h) for h in range(2) for g in range(4)] if keys_of is not None else []
    banks = 6

    def query(n):
        g, h = qunits[n]
        return (k.qkT[:, HB * h:HB * h + HB, 0, g, :],
                ps[:, 2 + n % banks, :].rearrange("p (b t) -> p b t", b=HB), k.bqk[:, keys_of, 0, g:g + 1])
    with nc.Block() as block:
        if slots is not None:
            @block.sync
            def _(sp):
                if sync is not None:
                    sync(sp)
                for b in range(2):
                    if b == 0:
                        sp.wait_ge(kout.sem, kout.base + len(units))
                        cleared = k.count("ln_cleared")
                        if cleared.base > 0:
                            sp.wait_ge(cleared.sem, cleared.base)
                    slots.copy_k(sp, b, b)
                    sp.wait_ge(qout_a.sem, qout_a.base + 2)
                    sp.wait_ge(qout_v.sem, qout_v.base + 2)
                    slots.copy_q(sp, b, b)
        elif sync is not None:
            block.sync(sync)
        if pool is not None:
            block.gpsimd(pool)

        @block.vector
        def _(v):
            if not counted:
                for b in range(B):
                    if bring is not None and b % HB == 0:
                        v.wait_ge(brought.sem, brought.base + b // HB + 1)
                    v.bn_stats(k.st[:, b, :], src(b)).then_inc(stats.sem, 1)
            for b in range(B):
                if not counted:
                    v.wait_ge(stats.sem, stats.base + b + 1)
                v.bn_aggr(k.mv[:, b, :], k.st[:, b, :]).then_inc(var.sem, 1)
            v.wait_ge(std.sem, std.base + 1)
            v.reciprocal(k.rs[:, :], k.std[:, :]).then_inc(rstd.sem, 1)
            v.wait_ge(rstd.sem, rstd.base + 1)
            for b in range(B):
                v.tensor_scalar(dst[:, b, :], src(b), k.mv[:, b, 0:1], k.rs[:, b:b + 1],
                                ALU.subtract, ALU.mult).then_inc(norm.sem, 1)
            for n in range(1, len(qunits), 2):
                where, product, bias = query(n)
                v.wait_ge(qready.sem, qready.base + n + 1)
                v.tensor_scalar(where, product, bias, None, ALU.add).then_inc(qout_v.sem, 1)
            if last is not None:
                last(v)

        @block.tensor
        def _(t):
            if first is not None:
                first(t)
            if bring is not None:
                for h in range(2):
                    bring(t, h).then_inc(brought.sem, 1)
            for n, (g, h) in enumerate(units):
                if n >= banks:
                    t.wait_ge(kout.sem, kout.base + n - banks + 1)
                t.matmul(ps[:, 2 + n % banks, :], k.wk[:, keys_of, g * P:(g + 1) * P],
                         k.ctxT[:, h * HALF:(h + 1) * HALF], start=True, stop=True).then_inc(kready.sem, 1)
            for b in range(B):
                t.wait_ge(norm.sem, norm.base + b + 1)
                t.transpose(ps[:, b // HB, P * (b % HB):P * (b % HB) + P], dst[:, b, :],
                            k.ident[:, :]).then_inc(turned.sem, 1)
            for n, (g, h) in enumerate(qunits):
                t.wait_ge(out.sem, out.base + h + 1)
                if n < banks:
                    t.wait_ge(kout.sem, kout.base + (n + banks + 1 if n + banks < len(units) else n + 1))
                else:
                    q = qout_v if n % 2 else qout_a
                    t.wait_ge(q.sem, q.base + (n - banks) // 2 + 1)
                t.matmul(ps[:, 2 + n % banks, :], k.wq[:, keys_of, g * P:(g + 1) * P],
                         dst_t[:, h * HALF:(h + 1) * HALF], start=True, stop=True).then_inc(qready.sem, 1)

        @block.scalar
        def _(a):
            def keys(n):
                g, h = units[n]
                a.wait_ge(kready.sem, kready.base + n + 1)
                a.activation(k.qkT[:, HB * h:HB * h + HB, 1, g, :],
                             ps[:, 2 + n % banks, :].rearrange("p (b t) -> p b t", b=HB), ACT.Identity,
                             bias=k.bqk[:, keys_of, 1, g:g + 1]).then_inc(kout.sem, 1)
            a.activation(k.prime[:, :], k.ones[:, 0:1], ACT.Sqrt)
            for n in range(len(units) // 4):
                keys(n)
            a.wait_ge(var.sem, var.base + B)
            a.activation(k.std[:, :], k.mv[:, :, 1], ACT.Sqrt, bias=k.eps[:, :]).then_inc(std.sem, 1)
            for n in range(len(units) // 4, len(units)):
                keys(n)
            for h in range(2):
                a.wait_ge(turned.sem, turned.base + HB * (h + 1))
                cols = slice(h * HALF, (h + 1) * HALF)
                if shifted:
                    dst = dst_t[:, cols].rearrange("p (b t) -> p b t", b=HB)
                    tok = ps[:, h, :].rearrange("p (b t) -> p b t", b=HB)
                    a.activation(dst[0:P // 2], tok[0:P // 2], ACT.Copy).then_inc(out.sem, 1)
                    a.activation(dst[P // 2:P, :, 1:P], tok[P // 2:P, :, 0:P - 1], ACT.Copy)
                elif gain is None:
                    a.activation(dst_t[:, cols], ps[:, h, :], ACT.Copy).then_inc(out.sem, 1)
                else:
                    a.activation(dst_t[:, cols], ps[:, h, :], ACT.Identity, scale=gain, bias=shift)\
                     .then_inc(out.sem, 1)
            for n in range(0, len(qunits), 2):
                where, product, bias = query(n)
                a.wait_ge(qready.sem, qready.base + n + 1)
                a.activation(where, product, ACT.Identity, bias=bias).then_inc(qout_a.sem, 1)
    if not counted:
        stats.base += B
    brought.base += 2 * (bring is not None)
    qready.base += len(qunits)
    for s in (qout_a, qout_v):
        s.base += len(qunits) // 2
    for s, n in ((var, B), (std, 1), (rstd, 1), (norm, B), (turned, B), (out, 2),
                 (kready, len(units)), (kout, len(units))):
        s.base += n


class Slots:

    def __init__(self, k, kslot, R, masked):
        self.k, self.kslot, self.R, self.masked = k, kslot, R, masked
        self.copies = R + 1 + masked
        self.full = [k.count("at_slot0_in"), k.count("at_slot1_in")]

    def copy_q(self, sp, b, p):
        sp.dma_start(self.k.qslot[:, p], self.k.qkT[:, b, 0]).then_inc(self.full[p].sem, 16)

    def copy_k(self, sp, b, p):
        k, R, full = self.k, self.R, self.full[p]
        if self.masked:
            sp.dma_start(k.mslot[:, p], k.negkeys[:, b]).then_inc(full.sem, 16)
        for r in range(R):
            rows = slice(r * P // R, (r + 1) * P // R)
            sp.dma_start(self.kslot[rows, p, :, r, :], k.qkT[rows, b, 1]).then_inc(full.sem, 16)


def over_batches(eng, step):
    step(0, 0, 0)
    step(1, 1, 1)
    with eng.Fori(0, (B - 4) // 2) as i:
        step(2 * i + 2, 0, 2)
        step(2 * i + 3, 1, 2)
    step(B - 2, 0, B - 2)
    step(B - 1, 1, B - 1)


def attention(k, kind, x, slots, values, weights, during=None, after=None):
    nc, ps = k.nc, k.ps
    local, select = kind == "local", kind == 3
    project = not select
    soon = select or local
    G = 2 if local else 4
    W = LD if local else XD
    NH = 4 * G
    R = 2 if local else 4
    qslot, mslot, kslot = k.qslot, k.mslot, slots.kslot
    slot_in, copies = slots.full, slots.copies
    CH = NH * W // P
    scale = {"local": 8.0, 0: P ** -0.5, 1: XD ** -0.5, 2: XD ** -0.5, 3: 1.0}[kind]
    mask = {"local": k.band, 0: None, 1: k.mask1, 2: k.zeros, 3: k.mask3}[kind]
    (scored, times, zeroed, top, minus, expd, turned, evac_even, evac_odd, pv, recip, normed,
     oturned, oT_out, projected, res) = (k.count("at_" + n) for n in (
        "scored", "times", "zeroed", "top", "minus", "expd", "turned", "evac_even",
        "evac_odd", "pv", "recip", "normed", "oturned", "oT_out", "projected", "res"))
    with ExitStack() as own:
        def sb(name, shape):
            return k.fresh(own, name, shape)
        sm = sb("sm", [P, 2, G, 4, P])
        pace = sb("pace", [P, 2, G])
        mx, pt, zt = sb("mx", [P, 2, G, 4]), sb("pt", [P, 2, 4, P]), sb("zt", [P, 2, 4, P])
        ro, on, oT = sb("ro", [P, NH]), sb("on", [P, NH, W]), sb("oT", [P, CH * P])
        on_flat = on[:, :, :].rearrange("p h w -> p (h w)")

        def out(g, j):
            if local:
                return ps[:, 2 + g, j * (W + 1):(j + 1) * (W + 1)]
            return ps[:, 6, (4 * g + j) * (W + 1):(4 * g + j + 1) * (W + 1)]

        if local:
            o_all = ps[:, 2:4, 0:4 * (W + 1)].rearrange("p g (h w) -> p g h w", w=W + 1)
            on_all = on[:, :, :].rearrange("p (g h) w -> p g h w", g=2)
            ro_all = ro[:, :].rearrange("p (g h) -> p g h", g=2)
            o_sum, o_val = o_all[:, :, :, W], o_all[:, :, :, 0:W]
        else:
            o_all = ps[:, 6, 0:NH * (W + 1)].rearrange("p (h w) -> p h w", w=W + 1)
            on_all, ro_all = on[:, :, :], ro[:, :]
            o_sum, o_val = o_all[:, :, W], o_all[:, :, 0:W]
        oT_ps = ps[:, 6, :] if local else ps[:, 7, 0:P]
        proj_ps = ps[:, 7, 3 * P:4 * P]

        with nc.Block() as block:
            @block.sync
            def _(sp):
                with sp.Fori(0, (B - 2) // 2) as i:
                    for p in range(2):
                        if kind == 0:
                            sp.wait_ge(top.sem, top.base + NH * (2 * i + p + 1))
                        else:
                            sp.wait_ge(scored.sem, scored.base + G * (2 * i + p + 1))
                        slots.copy_q(sp, 2 * i + 2 + p, p)
                        slots.copy_k(sp, 2 * i + 2 + p, p)
                        if during is not None:
                            during(sp, i, p)
                if after is not None:
                    after(sp)

            @block.tensor
            def _(t):
                def score(b, p, g, first=False):
                    t.wait_ge(slot_in[p].sem, slot_in[p].base + copies * (8 * (b - p) + 16))
                    if not first and select:
                        t.wait_ge(times.sem, times.base + G * (b - 1) + g + 1)
                    elif not first:
                        t.wait_ge(top.sem, top.base + NH * (b - 1) + 4 * g + 4)
                    for c in range(g * 4 // R, (g + 1) * 4 // R):
                        at = c * R * P - g * 4 * P
                        m = t.matmul(ps[:, g, at:at + R * P], qslot[:, p, c, :], kslot[:, p, c],
                                     start=True, stop=True)
                    m.then_inc(scored.sem, 1)

                def turn(b, p, g, first):
                    t.wait_ge(expd.sem, expd.base + G * b + g + 1)
                    if not (first and g < 2):
                        e = evac_odd if g % 2 else evac_even
                        t.wait_ge(e.sem, e.base + G // 2 * b + g // 2)
                    for j in range(4):
                        m = t.transpose(ps[:, 4 + g % 2, j * P:(j + 1) * P], sm[:, p, g, j, :],
                                        k.ident[:, :])
                    m.then_inc(turned.sem, 1)

                def weigh(b, g, first):
                    e = evac_odd if g % 2 else evac_even
                    t.wait_ge(e.sem, e.base + G // 2 * b + g // 2 + 1)
                    if g == 0 and not first:
                        t.wait_ge(normed.sem, normed.base + b)
                    for j in range(4):
                        m = t.matmul(out(g, j), pt[:, g % 2, j, :], values(b, 4 * g + j),
                                     start=True, stop=True)
                    m.then_inc(pv.sem, 1)

                def turn_out(b, first):
                    t.wait_ge(normed.sem, normed.base + b + 1)
                    if not first:
                        t.wait_ge(res.sem, res.base + b)
                    for n in range(CH):
                        m = t.transpose(oT_ps[:, n * P:(n + 1) * P], on_flat[:, n * P:(n + 1) * P],
                                        k.ident[:, :])
                    m.then_inc(oturned.sem, 1)

                def project_out(b):
                    t.wait_ge(oT_out.sem, oT_out.base + b + 1)
                    for n in range(CH):
                        m = t.matmul(proj_ps, oT[:, n * P:(n + 1) * P], weights(n), start=(n == 0),
                                     stop=(n == CH - 1))
                    m.then_inc(projected.sem, 1)

                def step(b, p, place):
                    if place < B - 1:
                        score(b + 1, 1 - p, 0)
                    if place > 0 and project:
                        turn_out(b - 1, place == 1)
                    turn(b, p, 0, place == 0)
                    if soon and place < B - 1:
                        score(b + 1, 1 - p, 1)
                    turn(b, p, 1, place == 0)
                    if place > 0 and project:
                        project_out(b - 1)
                    for g in range(2, G):
                        if place < B - 1:
                            score(b + 1, 1 - p, g if soon else g - 1)
                        weigh(b, g - 2, place == 0)
                        turn(b, p, g, place == 0)
                    if place < B - 1 and not soon:
                        score(b + 1, 1 - p, G - 1)
                    weigh(b, G - 2, place == 0)
                    weigh(b, G - 1, place == 0)

                for g in range(G):
                    score(0, 0, g, True)
                over_batches(t, step)
                if project:
                    turn_out(B - 1, False)
                    project_out(B - 1)

            @block.vector
            def _(v):
                def masked_max(b, p, g, early):
                    if select:
                        v.wait_ge(zeroed.sem, zeroed.base + G * b + g + 1)
                    else:
                        v.wait_ge(scored.sem, scored.base + G * b + g + 1)
                        if not early:
                            v.wait_ge(turned.sem, turned.base + G * (b - 2) + g + 1)
                    v.memset(pace[:, p, g:g + 1], 0.0)
                    for j in range(4):
                        if select:
                            score, term = sm[:, p, g, j, :], zt[:, g % 2, j, :]
                        else:
                            score = ps[:, g, j * P:(j + 1) * P]
                            term = mslot[:, p, :] if kind == 0 else mask[:, :]
                        v.tensor_tensor_reduce(sm[:, p, g, j, :], score, term, 1.0, LOWEST, ALU.add,
                                               ALU.max, mx[:, p, g, j:j + 1]).then_inc(top.sem, 1)

                def multiply(b, p, g, early):
                    v.wait_ge(scored.sem, scored.base + G * b + g + 1)
                    if not early:
                        v.wait_ge(turned.sem, turned.base + G * (b - 2) + g + 1)
                    v.tensor_tensor(sm[:, p, g], ps[:, g, :].rearrange("p (j t) -> p j t", j=4),
                                    mask[:, :].unsqueeze(1).to_broadcast([P, 4, P]), ALU.mult)\
                     .then_inc(times.sem, 1)

                def zero_term(b, p, g, first):
                    v.wait_ge(times.sem, times.base + G * b + g + 1)
                    if not (first and g < 2):
                        v.wait_ge(top.sem, top.base + 4 * (G * b + g - 1))
                    v.tensor_scalar(zt[:, g % 2], sm[:, p, g], 0.0, NEG, ALU.is_equal, ALU.mult)\
                     .then_inc(zeroed.sem, 1)

                def evacuate(b, g, first):
                    v.wait_ge(turned.sem, turned.base + G * b + g + 1)
                    if not (first and g < 2):
                        v.wait_ge(pv.sem, pv.base + G * b + g - 1)
                    v.tensor_copy(pt[:, g % 2], ps[:, 4 + g % 2, :].rearrange("p (j t) -> p j t", j=4))\
                     .then_inc(evac_even.sem, 1)

                def normalise(b, first):
                    v.wait_ge(pv.sem, pv.base + G * b + G)
                    v.reciprocal(ro_all, o_sum).then_inc(recip.sem, 1)
                    v.wait_ge(recip.sem, recip.base + b + 1)
                    if project and not first:
                        v.wait_ge(oturned.sem, oturned.base + b)
                    v.tensor_tensor(on_all, o_val, spread(ro_all, W), ALU.mult).then_inc(normed.sem, 1)
                    if not project:
                        v.wait_ge(normed.sem, normed.base + b + 1)
                        v.tensor_tensor(x[:, b, :], x[:, b, :], on_flat, ALU.add).then_inc(res.sem, 1)
                        statistics(b)

                def residual(b):
                    v.wait_ge(projected.sem, projected.base + b + 1)
                    v.tensor_tensor(x[:, b, :], x[:, b, :], proj_ps, ALU.add).then_inc(res.sem, 1)
                    if not local:
                        statistics(b)

                def statistics(b):
                    v.wait_ge(res.sem, res.base + b + 1)
                    v.bn_stats(k.st[:, b, :], x[:, b, :])

                def select_scores(b, p, early, first=False):
                    multiply(b, p, 0, early)
                    zero_term(b, p, 0, first)
                    for g in range(1, G):
                        multiply(b, p, g, early)
                        masked_max(b, p, g - 1, early)
                        zero_term(b, p, g, first)
                    masked_max(b, p, G - 1, early)

                def step(b, p, place):
                    first, more = place == 0, place < B - 1
                    if select:
                        if more:
                            select_scores(b + 1, 1 - p, first)
                    else:
                        if more:
                            masked_max(b + 1, 1 - p, 0, first)
                        evacuate(b, 0, first)
                        if place > 0:
                            residual(b - 1)
                        if more:
                            masked_max(b + 1, 1 - p, 1, first)
                        if G > 2:
                            evacuate(b, 2, first)
                            for g in range(2, G):
                                if more:
                                    masked_max(b + 1, 1 - p, g, first)
                    normalise(b, first)

                if select:
                    select_scores(0, 0, True, True)
                else:
                    for g in range(G):
                        masked_max(0, 0, g, True)
                over_batches(v, step)
                if project:
                    residual(B - 1)

            @block.gpsimd
            def _(g_):
                def subtract(b, p, g):
                    g_.wait_ge(top.sem, top.base + NH * b + 4 * g + 4)
                    g_.tensor_tensor(sm[:, p, g], sm[:, p, g], spread(mx[:, p, g, :], P), ALU.subtract)\
                      .then_inc(minus.sem, 1)

                def shift(b, p):
                    for g in range(G):
                        subtract(b, p, g)

                def step(b, p, place):
                    if place < B - 1:
                        shift(b + 1, 1 - p)

                shift(0, 0)
                over_batches(g_, step)

            @block.scalar
            def _(a):
                def exponent(b, p, g):
                    a.wait_ge(minus.sem, minus.base + G * b + g + 1)
                    a.activation(sm[:, p, g], sm[:, p, g], ACT.Exp, scale=scale).then_inc(expd.sem, 1)

                def evacuate(b, g, first):
                    a.wait_ge(turned.sem, turned.base + G * b + g + 1)
                    if not (first and g < 2):
                        a.wait_ge(pv.sem, pv.base + G * b + g - 1)
                    a.activation(pt[:, g % 2], ps[:, 4 + g % 2, :].rearrange("p (j t) -> p j t", j=4),
                                 ACT.Copy).then_inc((evac_odd if g % 2 else evac_even).sem, 1)

                def take_oT(b, first):
                    a.wait_ge(oturned.sem, oturned.base + b + 1)
                    if not first:
                        a.wait_ge(projected.sem, projected.base + b)
                    a.activation(oT[:, :], oT_ps, ACT.Copy).then_inc(oT_out.sem, 1)

                def step(b, p, place):
                    if place > 0 and project:
                        take_oT(b - 1, place == 1)
                    if select:
                        for g in range(G):
                            evacuate(b, g, place == 0)
                        if place < B - 1:
                            for g in range(G):
                                exponent(b + 1, 1 - p, g)
                    else:
                        for g in range(0, G, 2):
                            evacuate(b, g + 1, place == 0)
                            if place < B - 1:
                                exponent(b + 1, 1 - p, g)
                                exponent(b + 1, 1 - p, g + 1)

                a.activation(k.prime[:, :], k.ones[:, 0:1], ACT.Exp)
                for g in range(G):
                    exponent(0, 0, g)
                over_batches(a, step)
                if project:
                    take_oT(B - 1, False)
    for s in slot_in:
        s.base += 16 * copies * B // 2
    scored.base += G * B
    top.base += NH * B
    for s in (minus, expd, turned, pv):
        s.base += G * B
    for s in (evac_even, evac_odd):
        s.base += G // 2 * B
    for s in (recip, normed, res):
        s.base += B
    if select:
        times.base += G * B
        zeroed.base += G * B
    if project:
        for s in (oturned, oT_out, projected):
            s.base += B


def cross_attention(k, a, sync=None, clear=False, during=None, after=None):
    slots = Slots(k, k.kslot, 4, a == 0)
    cleared = k.count("ln_cleared")
    cleared.base += clear

    def meanwhile(g):
        if clear:
            g.memset(k.kslot_flat, 0.0).then_inc(cleared.sem, 1)
        if a < 3:
            g.wait_ge(k.count("ln_norm").sem, k.count("ln_norm").base + B)
            g.tensor_tensor(k.x[:, :, :], k.x[:, :, :], k.bo[:, a, :].unsqueeze(1).to_broadcast([P, B, P]),
                            ALU.add)

    layer_norm(k, lambda b: k.x[:, b, :], k.xn, k.xnT, keys_of=a, sync=sync, pool=meanwhile, slots=slots)
    attention(k, a, k.x, slots, lambda b, h: k.v1[:, b, a, h, :], lambda n: k.wo[:, a, :],
              during, after)

def shift_tokens(k, y, hT, loaded=None):
    nc, ps = k.nc, k.ps
    turned, out = k.count("sh_turned"), k.count("sh_out")
    with nc.Block() as block:
        if loaded is not None:
            @block.sync
            def _(sp):
                sp.wait_ge(loaded[0].sem, loaded[1])

        @block.tensor
        def _(t):
            for b in range(B):
                t.transpose(ps[:, b // HB, P * (b % HB):P * (b % HB) + P], y[:, b, :],
                            k.ident[:, :]).then_inc(turned.sem, 1)

        @block.scalar
        def _(a):
            for h in range(2):
                a.wait_ge(turned.sem, turned.base + HB * (h + 1))
                dst = hT[:, h * HALF:(h + 1) * HALF].rearrange("p (b t) -> p b t", b=HB)
                src = ps[:, h, :].rearrange("p (b t) -> p b t", b=HB)
                a.activation(dst[0:P // 2], src[0:P // 2], ACT.Copy).then_inc(out.sem, 1)
                a.activation(dst[P // 2:P, :, 1:P], src[P // 2:P, :, 0:P - 1], ACT.Copy).then_inc(out.sem, 1)
    turned.base += B
    out.base += 4


def local_qkv(k, hT, wqkv, v2, tab_a, tab_b, slots):
    nc, ps = k.nc, k.ps
    slot_in = [k.count("lq_slot0_in"), k.count("lq_slot1_in")]
    made, raw_out, v_out, squared, rotated, swapped, summed, norms, rstd, added, scaled, turned, out = (
        k.count("lq_" + n) for n in ("made", "raw_out", "v_out", "squared", "rotated", "swapped", "summed",
                                     "norms", "rstd", "added", "scaled", "turned", "out"))
    with ExitStack() as own:
        def sb(name, shape):
            return k.fresh(own, name, shape)
        hs = sb("hs", [P, 2, P])
        raw, sq = (k.kslot_flat[:, n * 2 * T:(n + 1) * 2 * T]
                   .rearrange("p (s w h e) -> p s w h e", s=2, w=2, h=LH) for n in range(2))
        t1, t2 = sb("t1", [P, 2, 2, LH, LD]), sb("t2", [P, 2, 2, LH, LD])
        ss, ssm, nrm, rn = (sb(n, [P, 2, 2 * LH]) for n in ("ss", "ssm", "nrm", "rn"))
        half = LD // 2
        with nc.Block() as block:
            @block.sync
            def _(sp):
                hb = hT[:, :].rearrange("p (b t) -> p b t", b=B)
                sp.dma_start(hs[:, 0], hb[:, 2]).then_inc(slot_in[0].sem, 16)
                sp.dma_start(hs[:, 1], hb[:, 3]).then_inc(slot_in[1].sem, 16)
                with sp.Fori(0, (B - 4) // 2) as i:
                    for p in range(2):
                        sp.wait_ge(made.sem, made.base + 3 * (2 * i + p + 3))
                        sp.dma_start(hs[:, p], hb[:, 2 * i + 4 + p]).then_inc(slot_in[p].sem, 16)
                sp.wait_ge(out.sem, out.base + 2 * 2)
                for b in range(2):
                    slots.copy_q(sp, b, b)
                    slots.copy_k(sp, b, b)

            @block.tensor
            def _(t):
                def qkv(b, p, early):
                    h = hT[:, b * P:(b + 1) * P] if early else hs[:, p, :]
                    if not early:
                        t.wait_ge(slot_in[p].sem, slot_in[p].base + 8 * (b - p))
                        t.wait_ge(v_out.sem, v_out.base + b - 1)
                    for n in range(3):
                        t.matmul(ps[:, 3 * p + n, :], h, wqkv[:, n, :],
                                 start=True, stop=True).then_inc(made.sem, 1)

                def turn(b, p, first):
                    t.wait_ge(scaled.sem, scaled.base + b + 1)
                    if not first:
                        t.wait_ge(out.sem, out.base + 2 * b)
                    for w in range(2):
                        for c in range(4):
                            m = t.transpose(ps[:, 6 + w, c * P:(c + 1) * P], t1[:, p, w, 2 * c:2 * c + 2, :]
                                            .rearrange("p h e -> p (h e)"), k.ident[:, :])
                        m.then_inc(turned.sem, 1)

                def step(b, p, place):
                    if place < B - 2:
                        qkv(b + 2, p, False)
                    turn(b, p, place == 0)

                qkv(0, 0, True)
                qkv(1, 1, True)
                over_batches(t, step)

            @block.scalar
            def _(a):
                def take(b, p, early):
                    if not early:
                        a.wait_ge(rotated.sem, rotated.base + b - 1)
                        a.wait_ge(swapped.sem, swapped.base + 2 * (b - 1))
                    for w in range(2):
                        a.wait_ge(made.sem, made.base + 3 * b + w + 1)
                        a.activation(raw[:, p, w], ps[:, 3 * p + w, :].rearrange("p (h e) -> p h e", e=LD),
                                     ACT.Copy).then_inc(raw_out.sem, 1)
                    a.wait_ge(made.sem, made.base + 3 * b + 3)
                    a.activation(v2[:, b, :, 0:LD], ps[:, 3 * p + 2, :].rearrange("p (h e) -> p h e", e=LD),
                                 ACT.Copy).then_inc(v_out.sem, 1)
                    a.wait_ge(raw_out.sem, raw_out.base + 2 * b + 2)
                    if not early:
                        a.wait_ge(summed.sem, summed.base + 2 * (b - 1))
                    a.activation(sq[:, p], raw[:, p], ACT.Square).then_inc(squared.sem, 1)

                def norm(b, p):
                    a.wait_ge(summed.sem, summed.base + 2 * b + 2)
                    a.activation(nrm[:, p, :], ssm[:, p, :], ACT.Sqrt).then_inc(norms.sem, 1)

                def give(b):
                    for w in range(2):
                        a.wait_ge(turned.sem, turned.base + 2 * b + w + 1)
                        a.activation(k.qkT[:, b, w], ps[:, 6 + w, :].rearrange("p (c t) -> p c t", c=4),
                                     ACT.Copy).then_inc(out.sem, 1)

                def step(b, p, place):
                    give(b)
                    if place < B - 1:
                        norm(b + 1, 1 - p)
                    if place < B - 2:
                        take(b + 2, p, False)

                a.activation(k.prime[:, :], k.ones[:, 0:1], ACT.Sqrt)
                take(0, 0, True)
                norm(0, 0)
                take(1, 1, True)
                over_batches(a, step)

            @block.vector
            def _(v):
                def rotate(b, p, early):
                    v.wait_ge(raw_out.sem, raw_out.base + 2 * b + 2)
                    if not early:
                        v.wait_ge(turned.sem, turned.base + 2 * (b - 1))
                    v.tensor_tensor(t1[:, p], raw[:, p], tab_a[:, :, :].unsqueeze(2)
                                    .to_broadcast([P, 2, LH, LD]), ALU.mult).then_inc(rotated.sem, 1)
                    v.wait_ge(squared.sem, squared.base + b + 1)
                    v.tensor_reduce(ss[:, p, :], sq[:, p].rearrange("p w h e -> p (w h) e"), AX.X, ALU.add)\
                     .then_inc(summed.sem, 1)
                    v.wait_ge(summed.sem, summed.base + 2 * b + 1)
                    v.tensor_scalar(ssm[:, p, :], ss[:, p, :], 1e-24, None, ALU.max).then_inc(summed.sem, 1)
                    v.wait_ge(swapped.sem, swapped.base + 2 * b + 2)
                    v.wait_ge(rotated.sem, rotated.base + b + 1)
                    v.tensor_tensor(t1[:, p], t1[:, p], t2[:, p], ALU.add).then_inc(added.sem, 1)

                def scale(b, p):
                    v.wait_ge(norms.sem, norms.base + b + 1)
                    v.reciprocal(rn[:, p, :], nrm[:, p, :]).then_inc(rstd.sem, 1)
                    v.wait_ge(added.sem, added.base + b + 1)
                    v.wait_ge(rstd.sem, rstd.base + b + 1)
                    both = t1[:, p].rearrange("p w h e -> p (w h) e")
                    v.tensor_tensor(both, both, spread(rn[:, p, :], LD), ALU.mult).then_inc(scaled.sem, 1)

                def step(b, p, place):
                    if place < B - 1:
                        rotate(b + 1, 1 - p, place == 0)
                        scale(b + 1, 1 - p)

                rotate(0, 0, True)
                scale(0, 0)
                over_batches(v, step)

            @block.gpsimd
            def _(g):
                def swap(b, p, early):
                    g.wait_ge(raw_out.sem, raw_out.base + 2 * b + 2)
                    if not early:
                        g.wait_ge(added.sem, added.base + b - 1)
                    for lo, other in ((0, half), (half, 0)):
                        g.tensor_tensor(
                            t2[:, p, :, :, lo:lo + half], raw[:, p, :, :, other:other + half],
                            tab_b[:, :, lo:lo + half].unsqueeze(2).to_broadcast([P, 2, LH, half]),
                            ALU.mult).then_inc(swapped.sem, 1)

                def step(b, p, place):
                    if place < B - 1:
                        swap(b + 1, 1 - p, place == 0)

                swap(0, 0, True)
                over_batches(g, step)
    for s in slot_in:
        s.base += 16 * (B - 2) // 2
    for s, n in ((made, 3), (raw_out, 2), (v_out, 1), (squared, 1), (rotated, 1), (swapped, 2),
                 (summed, 2), (norms, 1), (rstd, 1), (added, 1), (scaled, 1), (turned, 2), (out, 2)):
        s.base += n * B


def gated_ffn(k, y, dst, hT, w1, b1, w2, b2):
    nc, ps = k.nc, k.ps
    made, gelud, gated, out, biased, res = (k.count("gf_" + n) for n in (
        "made", "gelud", "gated", "out", "biased", "res"))
    NC = len(HCH)
    adds = 1 if dst is y else 2
    units = [(h, c) for h in range(2) for c in range(NC)]
    with ExitStack() as own:
        gl = k.fresh(own, "gl", [P, 2, HALF])
        uT = k.fresh(own, "uT", [P, 2, NC, HALF])
        with nc.Block() as block:
            @block.tensor
            def _(t):
                def up(n):
                    h, c = units[n]
                    o, m = HCH[c]
                    if n >= 2:
                        t.wait_ge(gated.sem, gated.base + n - 1)
                    for w in range(2):
                        t.matmul(ps[0:m, 2 * (n % 2) + w, :], w1[:, w * HID + o:w * HID + o + m],
                                 hT[:, h * HALF:(h + 1) * HALF], start=True, stop=True)\
                         .then_inc(made.sem, 1)

                def down(h):
                    t.wait_ge(gated.sem, gated.base + NC * (h + 1))
                    for b in range(HB):
                        o = ps[:, 4 + h, b * P:(b + 1) * P]
                        for c, (_, m) in enumerate(HCH):
                            x = t.matmul(o, uT[0:m, h, c, b * P:(b + 1) * P], w2[0:m, c, :],
                                         start=(c == 0), stop=(c == NC - 1))
                    x.then_inc(out.sem, 1)

                for n in range(NC + 1):
                    up(n)
                down(0)
                for n in range(NC + 1, 2 * NC):
                    up(n)
                down(1)

            @block.scalar
            def _(a):
                for n, (h, c) in enumerate(units):
                    m = HCH[c][1]
                    a.wait_ge(made.sem, made.base + 2 * n + 2)
                    if n >= 2:
                        a.wait_ge(gated.sem, gated.base + n - 1)
                    a.activation(gl[0:m, n % 2, :], ps[0:m, 2 * (n % 2) + 1, :], ACT.Gelu,
                                 bias=b1[0:m, 1, c:c + 1]).then_inc(gelud.sem, 1)

            @block.vector
            def _(v):
                def residual(h):
                    v.wait_ge(biased.sem, biased.base + adds)
                    v.wait_ge(out.sem, out.base + h + 1)
                    v.tensor_tensor(dst[:, HB * h:HB * h + HB, :], dst[:, HB * h:HB * h + HB, :],
                                    ps[:, 4 + h, :].rearrange("p (b c) -> p b c", b=HB), ALU.add)\
                     .then_inc(res.sem, 1)
                for n, (h, c) in enumerate(units):
                    m = HCH[c][1]
                    v.wait_ge(gelud.sem, gelud.base + n + 1)
                    v.scalar_tensor_tensor(out=uT[0:m, h, c, :], in0=ps[0:m, 2 * (n % 2), :],
                                           scalar=b1[0:m, 0, c:c + 1], in1=gl[0:m, n % 2, :],
                                           op0=ALU.add, op1=ALU.mult).then_inc(gated.sem, 1)
                residual(0)
                residual(1)

            @block.gpsimd
            def _(g):
                g.tensor_tensor(y[:, :, :], y[:, :, :], b2.unsqueeze(1).to_broadcast([P, B, P]), ALU.add)\
                 .then_inc(biased.sem, 1)
                if dst is not y:
                    g.wait_ge(biased.sem, biased.base + 1)
                    g.tensor_tensor(dst[:, :, :], dst[:, :, :], y[:, :, :], ALU.add).then_inc(biased.sem, 1)
    made.base += 4 * NC
    gelud.base += 2 * NC
    gated.base += 2 * NC
    out.base += 2
    biased.base += adds
    res.base += 2


def local_memory(k, ctx):
    k.lt_load = k.count("lt_load")
    k.lt = {name: k.fresh(ctx, "lt_" + name, shape) for name, shape in (
        ("wqkv", [P, LAYERS, 3, LH * LD]), ("lwo", [P, LAYERS, 4, P]), ("w1", [P, LAYERS, 2 * HID]),
        ("w2", [P, LAYERS, len(HCH), P]), ("b1", [P, LAYERS, 2, len(HCH)]), ("b2", [P, LAYERS, P]),
        ("gb", [P, LAYERS, 2]), ("qks", [P, LAYERS, 2, LD]), ("rotc", [P, 2, LD]), ("rots", [P, 2, LD]))}


def local_loads(k, d):
    def first(sp):
        sp.dma_start(k.lt["wqkv"][:, 0], d["wqkv"][:, 0]).then_inc(k.lt_load.sem, 16)
        for name in ("rotc", "rots", "b1", "gb"):
            sp.dma_start(k.lt[name][:], d[name]).then_inc(k.lt_load.sem, 16)
        sp.dma_start(k.lt["b2"][:, :, :], d["b2"].to_broadcast([P, LAYERS, P])).then_inc(k.lt_load.sem, 16)
        sp.dma_start(k.lt["qks"][:, :, :, :], d["qks"].to_broadcast([P, LAYERS, 2, LD]))\
          .then_inc(k.lt_load.sem, 16)

    def after(sp):
        for name in ("lwo", "w1", "w2"):
            sp.dma_start(k.lt[name][:], d[name]).then_inc(k.lt_load.sem, 16)
    return first, after


def local_transformer(k, d):
    ps, lt = k.ps, k.lt
    last_load, cleared = k.count("lt_last_load"), k.count("lt_cleared")
    with ExitStack() as own:
        def sb(name, shape):
            return k.fresh(own, name, shape)
        y = k.xn
        hT, v2, hnT = sb("hT", [P, T]), sb("v2", [P, B, LH, LD + 1]), k.xnT
        htok = k.work[:, 0:T].rearrange("p (b c) -> p b c", b=B)
        tab_a, tab_b = sb("tab_a", [P, LAYERS, 2, LD]), sb("tab_b", [P, LAYERS, 2, LD])
        half = LD // 2
        kslot, later = sb("lkslot", [P, 2, 4, 2, P]), sb("later", [P, P])
        slots = Slots(k, kslot, 2, False)

        def loads(sp):
            sp.dma_start(lt["wqkv"][:, 1], d["wqkv"][:, 1]).then_inc(last_load.sem, 16)
            sp.wait_ge(k.lt_load.sem, 16 * 10)

        def tables(g):
            g.memset(v2[:, :, :, LD:LD + 1], 1.0).then_inc(cleared.sem, 1)
            g.memset(kslot[:, :], 0.0).then_inc(cleared.sem, 1)
            g.wait_ge(cleared.sem, 2)
            g.memset(hT[P // 2:P, :].rearrange("p (b t) -> p b t", b=B)[:, :, 0:1], 0.0)\
             .then_inc(cleared.sem, 1)
            g.wait_ge(cleared.sem, 3)
            g.memset(later[:, :], 0.0).then_inc(cleared.sem, 1)
            g.wait_ge(cleared.sem, 4)
            g.affine_select(out=later[:, :], in_=later[:, :], compare_op=ALU.not_equal, fill=1.0,
                            base=1, pattern=[[-1, P]], channel_multiplier=1).then_inc(cleared.sem, 1)
            g.wait_ge(cleared.sem, 5)
            g.wait_ge(k.lt_load.sem, 16 * 10)
            rotc, rots, qks = lt["rotc"], lt["rots"], lt["qks"]
            for l in range(LAYERS):
                g.tensor_tensor(tab_a[:, l], rotc[:, :, :], qks[:, l], ALU.mult)
                g.tensor_tensor(tab_b[:, l, :, 0:half], rots[:, :, 0:half], qks[:, l, :, half:LD], ALU.mult)
                g.tensor_tensor(tab_b[:, l, :, half:LD], rots[:, :, half:LD], qks[:, l, :, 0:half], ALU.mult)

        layer_norm(k, lambda b: k.x[:, b, :], y, hT, sync=loads, pool=tables, counted=True, shifted=True)

        def shift(t, h):
            tok = ps[:, 2 + h, :].rearrange("p (b c) -> p b c", b=HB)
            for mat, cols in ((k.ident, slice(0, P // 2)), (later, slice(P // 2, P))):
                m = t.matmul(tok[:, :, cols], mat[:, :], y[:, h * HB:(h + 1) * HB, cols],
                             start=True, stop=True)
            return m

        for l in range(LAYERS):
            if l > 0:
                shift_tokens(k, y, hT, (last_load, 16))
            local_qkv(k, hT, lt["wqkv"][:, l], v2, tab_a[:, l], tab_b[:, l], slots)
            attention(k, "local", y, slots, lambda b, h: v2[:, b, h, :], lambda n: lt["lwo"][:, l, n, :])
            layer_norm(k, lambda b: ps[:, 2 + b // HB, P * (b % HB):P * (b % HB) + P], htok, hnT,
                       lt["gb"][:, l, 0:1], lt["gb"][:, l, 1:2], bring=shift)
            gated_ffn(k, y, k.x if l == LAYERS - 1 else y, hnT, lt["w1"][:, l], lt["b1"][:, l],
                      lt["w2"][:, l], lt["b2"][:, l, :])


def route(v, done, vals, iota, top, at, first, hot):
    n, e = vals.shape[1], vals.shape[2]
    places = iota.unsqueeze(1).to_broadcast([P, n, e])

    def then(m):
        m.then_inc(done.sem, 1)
        done.base += 1
        v.wait_ge(done.sem, done.base)

    then(v.tensor_reduce(top, vals, AX.X, ALU.max))
    then(v.tensor_tensor(at, vals, spread(top, e), ALU.is_equal))
    then(v.scalar_tensor_tensor(out=at, in0=at, scalar=-64.0, in1=places, op0=ALU.mult, op1=ALU.add))
    then(v.tensor_reduce(first, at, AX.X, ALU.min))
    then(v.tensor_tensor(hot, at, spread(first, e), ALU.is_equal))


def top1_experts(k, d):
    nc, ps = k.nc, k.ps
    own_step, scored, turned, hot_out, b2_made, acc_made, alpha_out, features_in = (
        k.count("t1_" + n) for n in ("own_step", "scored", "turned", "hot_out", "b2_made", "acc",
                                     "alpha", "features"))
    w_in = [k.count("t1_w0_in"), k.count("t1_w1_in")]
    hx, up, relu_a, relu_v, down, summed = (k.count("t1_" + n) for n in (
        "hx", "up", "relu_a", "relu_v", "down", "summed"))
    layer_norm(k, lambda b: k.x[:, b, :], k.xn, k.xnT, counted=True)
    with ExitStack() as own:
        def sb(name, shape):
            return k.fresh(own, name, shape)
        zn, zT, acc = sb("zn", [P, B, P]), sb("zT", [P, T]), sb("acc", [P, B, P])
        cent, iota, b2 = k.cent, k.iota[:, 0:E1], k.t1b2
        sc, at, hot = sb("sc", [P, B, E1]), sb("at", [P, B, E1]), sb("hot", [P, B, E1])
        top, chosen, alpha = sb("top", [P, B]), sb("chosen", [P, B]), sb("alpha", [P, B])
        hotT = sb("hotT", [E1, T])
        w1, w2, eb = sb("w1s", [P, 2, F1]), sb("w2s", [P, 2, FC1, P]), sb("ebs", [P, 2, 2 + FC1])
        hT, r1 = sb("h1T", [P, 2, T]), sb("r1", [P, 2, FC1, HALF])

        def first_weights(sp):
            for e in range(2):
                sp.dma_start(w1[:, e, :], d["t1w1"][e]).then_inc(w_in[e].sem, 16)
                sp.dma_start(w2[:, e], d["t1w2"][e]).then_inc(w_in[e].sem, 16)
                sp.dma_start(eb[:, e, :], d["t1eb"][e]).then_inc(w_in[e].sem, 16)

        def scores(t):
            for b in range(B):
                m = t.matmul(ps[:, 2, b * E1:(b + 1) * E1], k.xnT[:, b * P:(b + 1) * P], cent[:, :],
                             start=True, stop=True)
            m.then_inc(scored.sem, 1)

        def choose(v):
            v.wait_ge(scored.sem, 1)
            v.tensor_copy(sc[:, :, :], ps[:, 2, 0:B * E1].rearrange("p (b e) -> p b e", b=B))\
             .then_inc(own_step.sem, 1)
            own_step.base += 1
            v.wait_ge(own_step.sem, own_step.base)
            route(v, own_step, sc[:, :, :], iota, top[:, :], at[:, :, :], chosen[:, :], hot[:, :, :])

        layer_norm(k, lambda b: k.xn[:, b, :], zn, zT, sync=first_weights, first=scores, last=choose)
        with nc.Block() as block:
            @block.sync
            def _(sp):
                def fetch(e, p):
                    sp.wait_ge(down.sem, 2 * (e - 1))
                    sp.dma_start(w1[:, p, :], d["t1w1"][e]).then_inc(w_in[p].sem, 16)
                    sp.dma_start(w2[:, p], d["t1w2"][e]).then_inc(w_in[p].sem, 16)
                    sp.dma_start(eb[:, p, :], d["t1eb"][e]).then_inc(w_in[p].sem, 16)
                with sp.Fori(0, (E1 - 2) // 2) as i:
                    fetch(2 * i + 2, 0)
                    fetch(2 * i + 3, 1)

            @block.tensor
            def _(t):
                for b in range(B):
                    t.transpose(ps[0:E1, 1 + b // HB, P * (b % HB):P * (b % HB) + P], hot[:, b, :],
                                k.ident[:, :]).then_inc(turned.sem, 1)
                t.wait_ge(hot_out.sem, 2)
                for b in range(B):
                    t.matmul(ps[:, 4 + b // HB, P * (b % HB):P * (b % HB) + P], hotT[:, b * P:(b + 1) * P],
                             b2[:, :], start=True, stop=True).then_inc(b2_made.sem, 1)

                def step(e, p, place):
                    t.wait_ge(w_in[p].sem, 24 * (e - p) + 48)
                    t.wait_ge(hx.sem, e + 1)
                    for h in range(2):
                        for c in range(FC1):
                            if place > 0 or h > 0:
                                r = relu_v if c % 2 else relu_a
                                t.wait_ge(r.sem, 4 * e + 2 * h + c // 2 - 1)
                            t.matmul(ps[:, c, :], w1[:, p, c * P:(c + 1) * P],
                                     hT[:, p, h * HALF:(h + 1) * HALF], start=True, stop=True)\
                             .then_inc(up.sem, 1)
                    for h in range(2):
                        t.wait_ge(relu_a.sem, 4 * e + 2 * h + 2)
                        t.wait_ge(relu_v.sem, 4 * e + 2 * h + 2)
                        if place == 0:
                            t.wait_ge(acc_made.sem, h + 1)
                        if place > 1:
                            t.wait_ge(summed.sem, 8 * (e - 2) + 4 * h + 4)
                        for b in range(HB):
                            for c in range(FC1):
                                m = t.matmul(ps[:, 4 + 2 * p + h, b * P:(b + 1) * P],
                                             r1[:, h, c, b * P:(b + 1) * P], w2[:, p, c, :],
                                             start=(c == 0), stop=(c == FC1 - 1))
                        m.then_inc(down.sem, 1)
                over_batches(t, step)

            @block.scalar
            def _(a):
                def step(e, p, place):
                    for h in range(2):
                        for c in range(0, FC1, 2):
                            a.wait_ge(up.sem, 8 * e + 4 * h + c + 1)
                            if place > 0 and c == 0:
                                a.wait_ge(down.sem, 2 * (e - 1) + h + 1)
                            a.activation(r1[:, h, c, :], ps[:, c, :], ACT.Relu,
                                         bias=eb[:, p, 2 + c:3 + c]).then_inc(relu_a.sem, 1)
                a.activation(alpha[:, :], top[:, :], ACT.Sigmoid).then_inc(alpha_out.sem, 1)
                for h in range(2):
                    a.wait_ge(turned.sem, HB * (h + 1))
                    a.activation(hotT[:, h * HALF:(h + 1) * HALF], ps[0:E1, 1 + h, :], ACT.Copy)\
                     .then_inc(hot_out.sem, 1)
                over_batches(a, step)

            @block.vector
            def _(v):
                def inputs(e, p, early):
                    v.wait_ge(w_in[p].sem, 24 * (e - p) + 48)
                    if not early:
                        v.wait_ge(down.sem, 2 * (e - 1))
                    v.tensor_scalar(hT[:, p, :], zT[:, :], eb[:, p, 0:1], eb[:, p, 1:2], ALU.mult, ALU.add)\
                     .then_inc(hx.sem, 1)

                def step(e, p, place):
                    for h in range(2):
                        for c in range(1, FC1, 2):
                            v.wait_ge(up.sem, 8 * e + 4 * h + c + 1)
                            if place > 0 and c == 1:
                                v.wait_ge(down.sem, 2 * (e - 1) + h + 1)
                            v.tensor_scalar(r1[:, h, c, :], ps[:, c, :], eb[:, p, 2 + c:3 + c], 0.0,
                                            ALU.add, ALU.max).then_inc(relu_v.sem, 1)
                    if place < E1 - 1:
                        inputs(e + 1, 1 - p, place == 0)
                    for h in range(2):
                        v.wait_ge(down.sem, 2 * e + h + 1)
                        for b in range(HB * h, HB * h + HB):
                            if place > 0 and b == 0:
                                v.wait_ge(summed.sem, 8 * e)
                            v.scalar_tensor_tensor(
                                out=acc[:, b, :], in0=ps[:, 4 + 2 * p + h, P * (b % HB):P * (b % HB) + P],
                                scalar=hot[:, b, bass.ds(e, 1)], in1=acc[:, b, :], op0=ALU.mult,
                                op1=ALU.add).then_inc(summed.sem, 1)
                inputs(0, 0, True)
                for h in range(2):
                    v.wait_ge(b2_made.sem, HB * (h + 1))
                    v.tensor_copy(acc[:, HB * h:HB * h + HB, :],
                                  ps[:, 4 + h, :].rearrange("p (b c) -> p b c", b=HB)).then_inc(acc_made.sem, 1)
                over_batches(v, step)
                v.wait_ge(summed.sem, 8 * E1)
                v.wait_ge(alpha_out.sem, 1)
                v.wait_ge(features_in.sem, 1)
                for b in range(B):
                    v.scalar_tensor_tensor(out=k.x[:, b, :], in0=acc[:, b, :], scalar=alpha[:, b:b + 1],
                                           in1=k.x[:, b, :], op0=ALU.mult, op1=ALU.add)

            @block.gpsimd
            def _(g):
                g.tensor_tensor(k.x[:, :, :], k.x[:, :, :], k.xn[:, :, :], ALU.add).then_inc(features_in.sem, 1)


def capacity_experts(k, d):
    nc, ps = k.nc, k.ps
    own_step, scored, lessed, expd, routed, counted, diag, rows, rows_out = (k.count("ce_" + n) for n in (
        "own_step", "scored", "lessed", "expd", "routed", "counted", "diag", "rows", "rows_out"))
    iota_made, hot_made, sent, buf_out = (k.count("ce_" + n) for n in ("iota", "hot", "sent", "buf_out"))
    w_in, w = k.count("ce_w_in"), k.w2x
    up, silud, hid_made, down, y_out = (k.count("ce_" + n) for n in ("up", "silud", "hid", "down", "y_out"))
    yturned, y_sb_out, back_made = (k.count("ce_" + n) for n in ("yturned", "y_sb", "back"))

    def loads(sp):
        for s in range(SPANS_AHEAD, SPANS):
            sp.dma_start(w[:, s], d["w2x"][s]).then_inc(w_in.sem, 16)

    layer_norm(k, lambda b: k.x[:, b, :], k.xn, k.xnT, sync=loads, counted=True)
    GB = SPAN2 * C2
    w_in_all = 16 * (SPANS_FIRST + (B - 2) + SPANS - SPANS_AHEAD)
    with ExitStack() as own:
        def sb(name, shape, dt=F32, ctx=own):
            return k.fresh(ctx, name, shape, dt)
        gate, slot, slot_row = sb("gate", [P, B]), sb("slot_of", [P, B]), sb("slot_row", [P, T])
        bufT, yT = sb("bufT", [P, SLOTS]), sb("yT", [P, SLOTS])
        mine = sb("mine", [P, SCH])
        back = k.work[:, 0:SCH * T].rearrange("p (c t) -> p c t", c=SCH)
        ysl = k.work[:, SCH * T:SCH * T + SLOTS].rearrange("p (c h) -> p c h", c=SCH)
        with ExitStack() as early:
            rw, iota, tri = k.rw, k.iota, sb("tri", [P, P], ctx=early)
            slots_i, slots_f = sb("slots_i", [P, SLOTS], I32, early), sb("slots_f", [P, SLOTS], ctx=early)
            mine_i = sb("mine_i", [P, SCH], I32, early)
            pr, at, hot = (sb(n, [P, B, E2], ctx=early) for n in ("pr", "at2", "hot2"))
            base, done = sb("base", [P, B, E2], ctx=early), sb("done", [P, 1], ctx=early)
            dg = k.work[:, B * SLOTS:B * SLOTS + T].rearrange("p (b t) -> p b t", b=B)
            top, rsum, first, pos, eid, over = (sb(n, [P, B], ctx=early) for n in (
                "top2", "rsum", "first2", "pos", "eid", "over"))
            send = k.work[:, 0:B * SLOTS].rearrange("p (b s) -> p b s", b=B)
            sg, hid = sb("sg", [P, 2, GB], ctx=early), sb("hid", [P, 2, GB], ctx=early)
            chunks = ((0, 512), (512, 1024), (1024, SLOTS))
            with nc.Block() as block:
                @block.gpsimd
                def _(g):
                    g.memset(tri[:, :], 1.0).then_inc(iota_made.sem, 1)
                    g.iota(slots_i[:, :], pattern=[[1, SLOTS]], base=0, channel_multiplier=0)\
                     .then_inc(iota_made.sem, 1)
                    g.iota(mine_i[:, :], pattern=[[P, SCH]], base=0, channel_multiplier=1)\
                     .then_inc(iota_made.sem, 1)
                    g.memset(base[:, 0, :], 0.0).then_inc(iota_made.sem, 1)
                    g.wait_ge(iota_made.sem, 4)
                    g.affine_select(out=tri[:, :], in_=tri[:, :], compare_op=ALU.is_gt, fill=0.0, base=0,
                                    pattern=[[1, P]], channel_multiplier=-1).then_inc(iota_made.sem, 1)
                    g.wait_ge(iota_made.sem, 5)
                    g.tensor_tensor(k.x[:, :, :], k.x[:, :, :], k.xn[:, :, :], ALU.add)

                @block.tensor
                def _(t):
                    for b in range(B):
                        m = t.matmul(ps[:, 0, b * E2:(b + 1) * E2], k.xnT[:, b * P:(b + 1) * P], rw[:, :],
                                     start=True, stop=True)
                    m.then_inc(scored.sem, 1)
                    t.wait_ge(iota_made.sem, 5)
                    t.wait_ge(routed.sem, 1)
                    flat = hot[:, :, :].rearrange("p b e -> p (b e)")
                    t.matmul(ps[:, 1, 0:B * E2], tri[:, :], flat, start=True, stop=True).then_inc(counted.sem, 1)
                    t.matmul(ps[:, 2, 0:B * E2], k.ones[:, 0:P], flat, start=True, stop=True)\
                     .then_inc(counted.sem, 1)
                    for b in range(B):
                        t.wait_ge(diag.sem, b + 1)
                        t.matmul(ps[:, 3 + b // HB, P * (b % HB):P * (b % HB) + P], k.ones[:, 0:P],
                                 dg[:, b, :], start=True, stop=True).then_inc(rows.sem, 1)

                    def send_slots(n, batches):
                        lo, hi = chunks[n]
                        for b in batches:
                            if n == 0:
                                t.wait_ge(hot_made.sem, b + 1)
                            m = t.matmul(ps[:, 5 + n, 0:hi - lo], k.xn[:, b, :], send[:, b, lo:hi],
                                         start=(b == 0), stop=(b == B - 1))
                        if b == B - 1:
                            m.then_inc(sent.sem, 1)

                    def ups(s):
                        t.wait_ge(buf_out.sem, (s + 1) * GB // 512 + ((s + 1) * GB % 512 > 0))
                        if s == 1:
                            t.wait_ge(rows_out.sem, 2)
                        if s > 1:
                            t.wait_ge(hid_made.sem, s - 1)
                        for n in range(2):
                            for q in range(SPAN2):
                                m = t.matmul(ps[:, 2 * (s % 2) + n, q * C2:(q + 1) * C2], w[:, s, n, q, :],
                                             bufT[:, s * GB + q * C2:s * GB + (q + 1) * C2],
                                             start=True, stop=True)
                            m.then_inc(up.sem, 1)

                    def downs(s):
                        t.wait_ge(hid_made.sem, s + 1)
                        if s > 0:
                            t.wait_ge(y_out.sem, s)
                        for q in range(SPAN2):
                            m = t.matmul(ps[:, 4, q * C2:(q + 1) * C2], w[:, s, 2, q, :],
                                         hid[:, s % 2, q * C2:(q + 1) * C2], start=True, stop=True)
                        m.then_inc(down.sem, 1)

                    send_slots(0, range(B))
                    t.wait_ge(w_in.sem, w_in_all)
                    send_slots(1, range(0, 2))
                    ups(0)
                    send_slots(1, range(2, 4))
                    ups(1)
                    send_slots(1, range(4, 6))
                    downs(0)
                    ups(2)
                    send_slots(1, range(6, B))
                    downs(1)
                    send_slots(2, range(0, 2))
                    downs(2)
                    ups(3)
                    send_slots(2, range(2, 4))
                    ups(4)
                    send_slots(2, range(4, 6))
                    downs(3)
                    ups(5)
                    send_slots(2, range(6, B))
                    downs(4)
                    ups(6)
                    downs(5)
                    ups(7)
                    downs(6)
                    downs(7)

                @block.scalar
                def _(a):
                    a.wait_ge(lessed.sem, 1)
                    a.activation(pr[:, :, :], pr[:, :, :], ACT.Exp).then_inc(expd.sem, 1)
                    for h in range(2):
                        a.wait_ge(rows.sem, HB * (h + 1))
                        a.activation(slot_row[:, h * HALF:(h + 1) * HALF], ps[:, 3 + h, :], ACT.Copy)\
                         .then_inc(rows_out.sem, 1)
                    a.activation(k.prime[:, :], k.ones[:, 0:1], ACT.Silu)

                    def slots_out(n):
                        lo, hi = chunks[n]
                        a.wait_ge(sent.sem, n + 1)
                        a.activation(bufT[:, lo:hi], ps[:, 5 + n, 0:hi - lo], ACT.Copy).then_inc(buf_out.sem, 1)

                    def silu(s):
                        a.wait_ge(up.sem, 2 * (s + 1))
                        a.activation(sg[:, s % 2, :], ps[:, 2 * (s % 2), 0:GB], ACT.Silu).then_inc(silud.sem, 1)

                    def give(s):
                        a.wait_ge(down.sem, s + 1)
                        a.activation(yT[:, s * GB:(s + 1) * GB], ps[:, 4, 0:GB], ACT.Copy).then_inc(y_out.sem, 1)

                    slots_out(0)
                    silu(0)
                    silu(1)
                    give(0)
                    silu(2)
                    slots_out(1)
                    give(1)
                    give(2)
                    silu(3)
                    silu(4)
                    give(3)
                    silu(5)
                    slots_out(2)
                    give(4)
                    silu(6)
                    give(5)
                    silu(7)
                    give(6)
                    give(7)

                @block.vector
                def _(v):
                    def then(m):
                        m.then_inc(own_step.sem, 1)
                        own_step.base += 1
                        v.wait_ge(own_step.sem, own_step.base)
                    v.wait_ge(iota_made.sem, 4)
                    v.tensor_copy(slots_f[:, :], slots_i[:, :])
                    v.tensor_copy(mine[:, :], mine_i[:, :])
                    v.wait_ge(scored.sem, 1)
                    then(v.tensor_reduce(top[:, :], ps[:, 0, 0:B * E2].rearrange("p (b e) -> p b e", b=B),
                                         AX.X, ALU.max))
                    v.tensor_tensor(pr[:, :, :], ps[:, 0, 0:B * E2].rearrange("p (b e) -> p b e", b=B),
                                    spread(top[:, :], E2), ALU.subtract).then_inc(lessed.sem, 1)
                    v.wait_ge(expd.sem, 1)
                    then(v.tensor_reduce(rsum[:, :], pr[:, :, :], AX.X, ALU.add))
                    then(v.reciprocal(rsum[:, :], rsum[:, :]))
                    then(v.tensor_tensor(pr[:, :, :], pr[:, :, :], spread(rsum[:, :], E2), ALU.mult))
                    route(v, own_step, pr[:, :, :], iota[:, :], gate[:, :], at[:, :, :], first[:, :],
                          hot[:, :, :])
                    v.memset(done[:, :], 0.0).then_inc(routed.sem, 1)
                    v.wait_ge(counted.sem, 2)
                    for b in range(1, B):
                        then(v.tensor_tensor(base[:, b, :], base[:, b - 1, :],
                                             ps[:, 2, (b - 1) * E2:b * E2], ALU.add))
                    then(v.tensor_tensor(base[:, :, :], base[:, :, :],
                                         ps[:, 1, 0:B * E2].rearrange("p (b e) -> p b e", b=B), ALU.add))
                    then(v.tensor_tensor(base[:, :, :], base[:, :, :], hot[:, :, :], ALU.mult))
                    then(v.tensor_reduce(pos[:, :], base[:, :, :], AX.X, ALU.add))
                    then(v.tensor_scalar(eid[:, :], first[:, :], 64.0, float(C2), ALU.add, ALU.mult))
                    then(v.tensor_scalar(over[:, :], pos[:, :], float(C2), 4.0 * SLOTS, ALU.is_ge, ALU.mult))
                    then(v.tensor_tensor(slot[:, :], pos[:, :], eid[:, :], ALU.add))
                    then(v.tensor_tensor(slot[:, :], slot[:, :], over[:, :], ALU.add))
                    for b in range(B):
                        v.tensor_scalar(dg[:, b, :], k.ident[:, :], slot[:, b:b + 1], None, ALU.mult)\
                         .then_inc(diag.sem, 1)
                    for b in range(B):
                        v.tensor_scalar(send[:, b, :], slots_f[:, :], slot[:, b:b + 1], None, ALU.is_equal)\
                         .then_inc(hot_made.sem, 1)

                    def gate_up(s):
                        v.wait_ge(silud.sem, s + 1)
                        if s > 1:
                            v.wait_ge(down.sem, s - 1)
                        v.tensor_tensor(hid[:, s % 2, :], sg[:, s % 2, :], ps[:, 2 * (s % 2) + 1, 0:GB],
                                        ALU.mult).then_inc(hid_made.sem, 1)

                    def places(chunks_of_slots):
                        for c in chunks_of_slots:
                            v.tensor_scalar(back[:, c, :], slot_row[:, :], mine[:, c:c + 1], None, ALU.is_equal)

                    for s in range(6):
                        gate_up(s)
                    v.wait_ge(sent.sem, len(chunks))
                    v.wait_ge(rows_out.sem, 2)
                    places(range(0, 2))
                    gate_up(6)
                    places(range(2, 4))
                    gate_up(7)
                    places(range(4, SCH))

        with nc.Block() as block:
            @block.tensor
            def _(t):
                for c in range(SCH):
                    t.transpose(ps[:, c // 4, P * (c % 4):P * (c % 4) + P], yT[:, c * P:(c + 1) * P],
                                k.ident[:, :]).then_inc(yturned.sem, 1)
                t.wait_ge(y_sb_out.sem, 3)
                for b in range(B):
                    for c in range(SCH):
                        m = t.matmul(ps[:, 4 + b // 2, P * (b % 2):P * (b % 2) + P],
                                     back[:, c, b * P:(b + 1) * P], ysl[:, c, :],
                                     start=(c == 0), stop=(c == SCH - 1))
                    m.then_inc(back_made.sem, 1)

            @block.scalar
            def _(a):
                for n, (lo, hi) in enumerate(((0, 4), (4, 8), (8, SCH))):
                    a.wait_ge(yturned.sem, hi)
                    a.activation(ysl[:, lo:hi, :], ps[:, n, 0:(hi - lo) * P].rearrange("p (c h) -> p c h", h=P),
                                 ACT.Copy).then_inc(y_sb_out.sem, 1)

            @block.vector
            def _(v):
                for b in range(B):
                    v.wait_ge(back_made.sem, 2 * (b // 2) + 2)
                    v.scalar_tensor_tensor(out=k.x[:, b, :], in0=ps[:, 4 + b // 2, P * (b % 2):P * (b % 2) + P],
                                           scalar=gate[:, b:b + 1], in1=k.x[:, b, :], op0=ALU.mult,
                                           op1=ALU.add)


def capacity_loads(k, d, ctx):
    k.w2x = k.fresh(ctx, "w2x", [P, SPANS, 3, SPAN2, P])
    w_in = k.count("ce_w_in")
    flat = k.w2x[:, :, :, :, :].rearrange("p s w q f -> p s (w q f)")
    source = d["w2x"].rearrange("s p w q f -> s p (w q f)")
    half = 3 * SPAN2 * P // 2

    def first(sp):
        for s in range(SPANS_FIRST):
            sp.dma_start(flat[:, s, :], source[s]).then_inc(w_in.sem, 16)

    def during(sp, i, p):
        cols = slice(p * half, (p + 1) * half)
        sp.dma_start(flat[:, bass.ds(SPANS_FIRST + i, 1), cols],
                     source[bass.ds(SPANS_FIRST + i, 1), :, cols].rearrange("s p f -> p s f"))\
          .then_inc(w_in.sem, 16)
    return first, during


def top2_experts(k, d):
    nc, ps = k.nc, k.ps
    load, own_step, scored, sig, routed, cturned, cT_out, mixed, up, silud, hid_made, out = (
        k.count("t2_" + n) for n in ("load", "own_step", "scored", "sig", "routed", "cturned", "cT_out",
                                     "mixed", "up", "silud", "hid", "out"))
    shared = CH3 - 1
    units = [(h, shared) for h in range(2)] + [(h, c) for h in range(2) for c in range(CH3 - 1)]
    gw, iota, sel = k.gw, k.iota[:, 0:E3], k.sel
    with ExitStack() as own:
        def sb(name, shape):
            return k.fresh(own, name, shape)
        wg, wu, wd = (sb(n, [P, CH3, P]) for n in ("wg3", "wu3", "wd3"))

        def loads(sp):
            for dst, src in ((wg, "wg3"), (wu, "wu3"), (wd, "wd3")):
                sp.dma_start(dst[:], d[src]).then_inc(load.sem, 16)

        layer_norm(k, lambda b: k.x[:, b, :], k.xn, k.xnT, sync=loads, counted=True)
        sc, at, hot1, hot2, mix = (sb(n, [P, B, E3]) for n in ("sc3", "at3", "hot31", "hot32", "mix"))
        top1, top2, first, tot = (sb(n, [P, B]) for n in ("top31", "top32", "first3", "tot"))
        cT, sg, uu, hid = sb("cT", [E3, T]), sb("sg3", [P, 2, HALF]), sb("uu", [P, 2, HALF]), \
            sb("hid3", [P, 2, CH3, HALF])
        with nc.Block() as block:
            @block.tensor
            def _(t):
                for b in range(B):
                    m = t.matmul(ps[:, 7, b * E3:(b + 1) * E3], k.xnT[:, b * P:(b + 1) * P], gw[:, :],
                                 start=True, stop=True)
                m.then_inc(scored.sem, 1)
                t.wait_ge(load.sem, 16 * 3)

                def ups(n):
                    h, c = units[n]
                    if n >= 2:
                        t.wait_ge(hid_made.sem, n - 1)
                    cols = slice(h * HALF, (h + 1) * HALF)
                    bank = 3 * (n % 2)
                    t.matmul(ps[:, bank, :], wg[:, c, :], k.xnT[:, cols], start=True, stop=True)\
                     .then_inc(up.sem, 1)
                    m = t.matmul(ps[:, bank + 1, :], wu[:, c, :], k.xnT[:, cols], start=True, stop=True)
                    if c < CH3 - 1:
                        m = t.matmul(ps[:, bank + 2, :], sel[:, c, :], cT[:, cols], start=True, stop=True)
                    m.then_inc(up.sem, 1)

                def downs(h):
                    t.wait_ge(hid_made.sem, 2 + shared * (h + 1))
                    for b in range(HB):
                        for c in range(CH3):
                            m = t.matmul(ps[:, 6 + h, b * P:(b + 1) * P], hid[:, h, c, b * P:(b + 1) * P],
                                         wd[:, c, :], start=(c == 0), stop=(c == CH3 - 1))
                    m.then_inc(out.sem, 1)
                ups(0)
                ups(1)
                t.wait_ge(routed.sem, 1)
                for b in range(B):
                    t.transpose(ps[0:E3, 6 + b // HB, P * (b % HB):P * (b % HB) + P], mix[:, b, :],
                                k.ident[:, :]).then_inc(cturned.sem, 1)
                t.wait_ge(cT_out.sem, 2)
                for n in range(2, shared + 3):
                    ups(n)
                downs(0)
                for n in range(shared + 3, len(units)):
                    ups(n)
                downs(1)

            @block.scalar
            def _(a):
                a.wait_ge(scored.sem, 1)
                a.activation(sc[:, :, :], ps[:, 7, 0:B * E3].rearrange("p (b e) -> p b e", b=B), ACT.Sigmoid)\
                 .then_inc(sig.sem, 1)

                def silu(n):
                    a.wait_ge(up.sem, 2 * n + 1)
                    if n in (2, 3):
                        a.wait_ge(hid_made.sem, n - 1)
                    if n > 3:
                        a.wait_ge(mixed.sem, n - 3)
                    a.activation(sg[:, n % 2, :], ps[:, 3 * (n % 2), :], ACT.Silu).then_inc(silud.sem, 1)

                silu(0)
                silu(1)
                for h in range(2):
                    a.wait_ge(cturned.sem, HB * (h + 1))
                    a.activation(cT[:, h * HALF:(h + 1) * HALF], ps[0:E3, 6 + h, :], ACT.Copy)\
                     .then_inc(cT_out.sem, 1)
                for n in range(2, len(units)):
                    silu(n)

            @block.vector
            def _(v):
                def then(m):
                    m.then_inc(own_step.sem, 1)
                    own_step.base += 1
                    v.wait_ge(own_step.sem, own_step.base)
                v.wait_ge(sig.sem, 1)
                route(v, own_step, sc[:, :, :], iota, top1[:, :], at[:, :, :], first[:, :], hot1[:, :, :])
                then(v.scalar_tensor_tensor(out=sc[:, :, :], in0=hot1[:, :, :], scalar=-4.0, in1=sc[:, :, :],
                                            op0=ALU.mult, op1=ALU.add))
                route(v, own_step, sc[:, :, :], iota, top2[:, :], at[:, :, :], first[:, :], hot2[:, :, :])
                then(v.tensor_tensor(tot[:, :], top1[:, :], top2[:, :], ALU.add))
                then(v.tensor_scalar(tot[:, :], tot[:, :], 1e-20, None, ALU.add))
                then(v.reciprocal(tot[:, :], tot[:, :]))
                then(v.tensor_tensor(hot1[:, :, :], hot1[:, :, :], spread(top1[:, :], E3), ALU.mult))
                then(v.tensor_tensor(hot2[:, :, :], hot2[:, :, :], spread(top2[:, :], E3), ALU.mult))
                then(v.tensor_tensor(mix[:, :, :], hot1[:, :, :], hot2[:, :, :], ALU.add))
                then(v.tensor_scalar(tot[:, :], tot[:, :], ROUTED_SCALE, None, ALU.mult))
                v.tensor_tensor(mix[:, :, :], mix[:, :, :], spread(tot[:, :], E3), ALU.mult)\
                 .then_inc(routed.sem, 1)
                for n, (h, c) in enumerate(units):
                    v.wait_ge(silud.sem, n + 1)
                    v.wait_ge(up.sem, 2 * n + 2)
                    bank = 3 * (n % 2)
                    if c < CH3 - 1:
                        v.tensor_tensor(uu[:, n % 2, :], sg[:, n % 2, :], ps[:, bank + 1, :], ALU.mult)\
                         .then_inc(mixed.sem, 1)
                        v.wait_ge(mixed.sem, n - 1)
                        v.tensor_tensor(hid[:, h, c, :], uu[:, n % 2, :], ps[:, bank + 2, :], ALU.mult)\
                         .then_inc(hid_made.sem, 1)
                    else:
                        v.tensor_tensor(hid[:, h, c, :], sg[:, n % 2, :], ps[:, bank + 1, :], ALU.mult)\
                         .then_inc(hid_made.sem, 1)
                for h in range(2):
                    v.wait_ge(out.sem, h + 1)
                    v.tensor_tensor(k.x[:, HB * h:HB * h + HB, :], k.x[:, HB * h:HB * h + HB, :],
                                    ps[:, 6 + h, :].rearrange("p (b c) -> p b c", b=HB), ALU.add)


def store(k, out):
    done = k.count("stored")
    with k.nc.Block() as block:
        @block.sync
        def _(sp):
            sp.dma_start(out.rearrange("b t d -> t b d"), k.x[:, :, :]).then_inc(done.sem, 16)
            sp.wait_ge(done.sem, 16)


def build(nc, d, out):
    with ExitStack() as ctx:
        k = Core(nc, ctx)
        k.ps = ctx.enter_context(nc.psum_tensor("ps", [P, 8, 512], F32))
        shared_memory(k)
        with ExitStack() as local:
            local_memory(k, local)
            setup(k, d)
            first, after = local_loads(k, d)
            cross_attention(k, 0, sync=first, after=after)
            local_transformer(k, d)
        cross_attention(k, 1, clear=True)
        top1_experts(k, d)
        with ExitStack() as capacity:
            first, during = capacity_loads(k, d, capacity)
            cross_attention(k, 2, sync=first, during=during)
            capacity_experts(k, d)
        cross_attention(k, 3, clear=True)
        top2_experts(k, d)
        store(k, out)




def heads_apart(np, m):
    out = np.zeros(m.shape[:-1] + (4, 4, 32), m.dtype)
    out[..., 0:XD] = m.reshape(m.shape[:-1] + (4, 4, XD))
    return out.reshape(m.shape[:-1] + (4 * P,))


def per_head(np, w):
    out = np.zeros((P, P), w.dtype)
    for h in range(XH):
        out[h * XD:(h + 1) * XD, h * XD:(h + 1) * XD] = w
    return out


def layouts(np, i):
    f = np.float32
    c = np.ascontiguousarray
    zero = np.zeros(P, f)
    d = {}
    d["x"] = c(i["x"].transpose(1, 0, 2))
    d["ctxT"] = c(i["ctx_1024"].transpose(2, 0, 1).reshape(P, T))
    wq = [per_head(np, i["L0_xattn_Wq"].T), i["L1_xattn_Wq"].T, i["L2_xattn_Wq"], per_head(np, i["L3_xattn_Wq"])]
    wk = [per_head(np, i["L0_xattn_Wk"].T), i["L1_xattn_Wk"].T, i["L2_xattn_Wk"], per_head(np, i["L3_xattn_Wk"])]
    wv = [per_head(np, i["L0_xattn_Wv"].T), i["L1_xattn_Wv"].T, i["L2_xattn_Wv"], per_head(np, i["L3_xattn_Wv"])]
    d["wq"] = c(np.stack([heads_apart(np, w) for w in wq], 1))
    d["wk"] = c(np.stack([heads_apart(np, w) for w in wk], 1))
    d["wv"] = c(np.concatenate(wv, 1))
    d["bv"] = np.concatenate([zero, i["L1_xattn_bv"], i["L2_xattn_bv"], zero])[None]
    bq = [heads_apart(np, v) for v in (zero, i["L1_xattn_bq"], i["L2_xattn_bq"], zero)]
    bk = [heads_apart(np, v) for v in (zero, i["L1_xattn_bk"], i["L2_xattn_bk"], zero)]
    d["bqk"] = c(np.stack([np.stack(bq), np.stack(bk)], 1).reshape(NX, 2, 4, P).transpose(3, 0, 1, 2))
    d["wo"] = c(np.stack([i["L0_xattn_Wo"].T, i["L1_xattn_Wo"].T, i["L2_xattn_Wo"]], 1))
    d["bo"] = np.stack([i["L0_xattn_bo"], i["L1_xattn_bo"], i["L2_xattn_bo"]])[None]
    d["keys"] = i["mask_Bx1x1xS2_if1"].reshape(1, B, P)
    d["mask1"] = i["mask_1x1xSxS2_if1"].reshape(P, P)
    d["mask3"] = i["mask_1x1xSxS2_fk0"].reshape(P, P)
    d["wqkv"] = c(i["L0_ffn_wqkv"].reshape(LAYERS, P, 3, LH * LD).transpose(1, 0, 2, 3))
    d["lwo"] = c(i["L0_ffn_wo"].reshape(LAYERS, 4, P, P).transpose(2, 0, 1, 3))
    d["w1"] = c(i["L0_ffn_w1"].transpose(1, 0, 2))
    nch = len(HCH)
    w2 = np.zeros((LAYERS, nch * P, P), f)
    w2[:, 0:HID] = i["L0_ffn_w2"]
    d["w2"] = c(w2.reshape(LAYERS, nch, P, P).transpose(2, 0, 1, 3))
    b1 = np.zeros((LAYERS, 2, nch * P), f)
    b1[:, :, 0:HID] = i["L0_ffn_b1"].reshape(LAYERS, 2, HID)
    d["b1"] = c(b1.reshape(LAYERS, 2, nch, P).transpose(3, 0, 1, 2))
    d["b2"] = i["L0_ffn_b2"][None]
    d["gb"] = c(np.stack([i["L0_ffn_ln_g"], i["L0_ffn_ln_b"]], 1).transpose(2, 0, 1))
    d["qks"] = c(np.stack([i["L0_ffn_q_scale"], i["L0_ffn_k_scale"]], 1)[None])
    half = np.arange(0, LD, 2, dtype=f)
    t = np.arange(P, dtype=f)
    ang = t[:, None] * (f(1.0) / f(10000.0) ** (half / f(LD)))[None]
    ang = np.concatenate([ang, ang], 1)
    base = (half + f(0.4 * LD)) / f(1.4 * LD)
    sc = base[None] ** ((t - P // 2) / f(WINDOW // 2))[:, None]
    sc = np.concatenate([sc, sc], 1)
    cos, sin = np.cos(ang), np.sin(ang)
    sign = np.where(np.arange(LD) < LD // 2, f(-1), f(1))
    d["rotc"] = c(np.stack([cos * sc, cos / sc], 1).astype(f))
    d["rots"] = c(np.stack([sin * sc * sign, sin / sc * sign], 1).astype(f))
    d["cent"] = c(i["L1_ffn_centroids"].T)
    d["t1w1"] = c(i["L1_ffn_W1"].transpose(0, 2, 1))
    d["t1w2"] = c(i["L1_ffn_W2"].transpose(0, 2, 1).reshape(E1, FC1, P, P).transpose(0, 2, 1, 3))
    d["t1eb"] = c(np.concatenate([i["L1_ffn_gamma"][:, :, None], i["L1_ffn_beta"][:, :, None],
                                  i["L1_ffn_b1"].reshape(E1, FC1, P).transpose(0, 2, 1)], 2))
    d["t1b2"] = i["L1_ffn_b2"]
    d["iota"] = np.arange(E2, dtype=f)[None]
    d["rw"] = i["L2_ffn_w_router"]
    w = np.stack([i["L2_ffn_w_gate"], i["L2_ffn_w_up"], i["L2_ffn_w_down"]])
    d["w2x"] = c(w.reshape(3, E2 // SPAN2, SPAN2, P, P).transpose(1, 3, 0, 2, 4))
    d["gw"] = c(i["L3_ffn_gate_weight"].T)

    def chunks(routed, shared):
        return c(np.concatenate([routed.reshape(E3 * I3, P), shared]).reshape(CH3, P, P).transpose(2, 0, 1))
    d["wg3"] = chunks(i["L3_ffn_w_gate"], i["L3_ffn_ws_gate"])
    d["wu3"] = chunks(i["L3_ffn_w_up"], i["L3_ffn_ws_up"])
    down = np.concatenate([i["L3_ffn_w_down"].transpose(0, 2, 1).reshape(E3 * I3, P), i["L3_ffn_ws_down"].T])
    d["wd3"] = c(down.reshape(CH3, P, P).transpose(1, 0, 2))
    d["sel"] = c(np.repeat(np.eye(E3, dtype=f), I3, 1).reshape(E3, CH3 - 1, P))
    return d


def kernel(**inputs):
    import numpy as np
    import concourse.bacc as _bacc
    from concourse.bass_utils import run_bass_kernel_spmd as _run

    nc = _bacc.Bacc("TRN2", target_bir_lowering=False, num_devices=1)
    arrays = {"in_" + n: np.ascontiguousarray(a) for n, a in
              layouts(np, {n: np.asarray(a) for n, a in inputs.items()}).items()}
    d = {n[3:]: nc.dram_tensor(n, a.shape, mybir.dt.from_np(a.dtype), kind="ExternalInput").ap()
         for n, a in arrays.items()}
    out = nc.dram_tensor("out_0", (B, P, P), F32, kind="ExternalOutput").ap()
    build(nc, d, out)
    return _run(nc, [arrays], core_ids=[0]).results[0]["out_0"]
```
